# Optimizing a Trainium2 kernel written in Bass

```python
import numpy as np
import jax
import jax.numpy as jnp

def _softmax(x, axis=-1):
    return jax.nn.softmax(x, axis=axis)

def _gelu(x):
    return jax.nn.gelu(x, approximate=True)

def _silu(x):
    return jax.nn.silu(x)

def _sigmoid(x):
    return jax.nn.sigmoid(x)

def _layernorm(x, axis=-1, eps=1e-05):
    m = jnp.mean(x, axis=axis, keepdims=True)
    v = jnp.var(x, axis=axis, keepdims=True)
    return (x - m) / jnp.sqrt(v + eps)

def _scatter_add(tgt, idx, src, axis=0):
    return tgt.at[idx].add(src)

def _segment_sum(src, seg, n):
    return jax.ops.segment_sum(src, seg, n)
kernel_name = 'mk_conv_attn_hybrid_d4_conv_nhwc768_r4_341aa6'

def setup_inputs(seed: int=0):
    np.random.seed(seed)
    _w = jnp.asarray

    def _rec_inputs():
        import jax
        import jax.numpy as jnp
        _gk = jax.random.key(seed)
        x = -0.0002221 + 1 * jax.random.normal(jax.random.fold_in(_gk, 1), (8, 16, 16, 192), jnp.float32)
        return x
    x = _rec_inputs()

    def _L0_conv_setup():
        import jax, jax.numpy as jnp
        import numpy as np
        WS = 14
        NUM_HEADS = 12
        EPS = 1e-06

        def _ln(x, w, b):
            mu = jnp.mean(x, axis=-1, keepdims=True)
            var = jnp.mean(jnp.square(x - mu), axis=-1, keepdims=True)
            return (x - mu) * jax.lax.rsqrt(var + EPS) * w + b
        key = jax.random.key(seed)
        ks = jax.random.split(key, 12)
        C, FF = (192, 768)
        hd = C // NUM_HEADS
        return {'x': jax.random.normal(ks[0], (8, 16, 16, C), jnp.float32), 'norm1_w': jnp.ones((C,), jnp.float32), 'norm1_b': jnp.zeros((C,), jnp.float32), 'qkv_w': jax.random.normal(ks[1], (C, 3 * C), jnp.float32) * 0.02, 'qkv_b': jax.random.normal(ks[2], (3 * C,), jnp.float32) * 0.02, 'proj_w': jax.random.normal(ks[3], (C, C), jnp.float32) * 0.02, 'proj_b': jax.random.normal(ks[4], (C,), jnp.float32) * 0.02, 'rel_pos_h': jax.random.normal(ks[5], (2 * WS - 1, hd), jnp.float32) * 0.02, 'rel_pos_w': jax.random.normal(ks[6], (2 * WS - 1, hd), jnp.float32) * 0.02, 'norm2_w': jnp.ones((C,), jnp.float32), 'norm2_b': jnp.zeros((C,), jnp.float32), 'fc1_w': jax.random.normal(ks[7], (C, FF), jnp.float32) * 0.02, 'fc1_b': jax.random.normal(ks[8], (FF,), jnp.float32) * 0.02, 'fc2_w': jax.random.normal(ks[9], (FF, C), jnp.float32) * 0.02, 'fc2_b': jax.random.normal(ks[10], (C,), jnp.float32) * 0.02}
    _L0_conv_all = _L0_conv_setup()
    _L0_conv_in = {k: v for k, v in _L0_conv_all.items() if k in ('norm1_w', 'norm1_b', 'qkv_w', 'qkv_b', 'proj_w', 'proj_b', 'rel_pos_h', 'rel_pos_w', 'norm2_w', 'norm2_b', 'fc1_w', 'fc1_b', 'fc2_w', 'fc2_b')}
    del _L0_conv_all

    def _L1_conv_setup():
        import jax, jax.numpy as jnp
        import numpy as np
        NUM_BLOCKS = 8
        BLOCK_SIZE = 24
        LAMBDA = 0.01

        def softshrink(x, lam=LAMBDA):
            return jnp.sign(x) * jnp.maximum(jnp.abs(x) - lam, 0.0)
        key = jax.random.key(seed)
        k1, k2, k3 = jax.random.split(key, 3)
        B, H, W, C = (4, 32, 32, 192)
        bound = float(np.sqrt(6.0 / (BLOCK_SIZE + BLOCK_SIZE)))
        x = jax.random.normal(k1, (B, H, W, C), dtype=jnp.float32)
        w1 = jax.random.uniform(k2, (2, NUM_BLOCKS, BLOCK_SIZE, BLOCK_SIZE), minval=-bound, maxval=bound, dtype=jnp.float32)
        w2 = jax.random.uniform(k3, (2, NUM_BLOCKS, BLOCK_SIZE, BLOCK_SIZE), minval=-bound, maxval=bound, dtype=jnp.float32)
        b1 = jnp.zeros((2, NUM_BLOCKS, BLOCK_SIZE), dtype=jnp.float32)
        b2 = jnp.zeros((2, NUM_BLOCKS, BLOCK_SIZE), dtype=jnp.float32)
        return {'x': x, 'w1': w1, 'w2': w2, 'b1': b1, 'b2': b2}
    _L1_conv_all = _L1_conv_setup()
    _L1_conv_in = {k: v for k, v in _L1_conv_all.items() if k in ('w1', 'w2', 'b1', 'b2')}
    del _L1_conv_all

    def _L2_attn_setup():
        import jax, jax.numpy as jnp
        import numpy as np
        from jax import lax
        B, S, D = (4, 1024, 192)
        H, LM, KS = (12, 16, 33)
        HD = D // H

        def _iterative_pinv(k_mat, n_iter=6):
            m = k_mat.shape[-1]
            I = jnp.eye(m, dtype=k_mat.dtype)
            v = (1.0 / jnp.max(jnp.sum(k_mat, axis=-2), axis=-1))[:, None, None] * jnp.swapaxes(k_mat, -1, -2)
            for _ in range(n_iter):
                kv = k_mat @ v
                v = 0.25 * v @ (13.0 * I - kv @ (15.0 * I - kv @ (7.0 * I - kv)))
            return v
        key = jax.random.key(seed)
        ks = jax.random.split(key, 4)
        return {'x': jax.random.normal(ks[0], (B, S, D), dtype=jnp.float32), 'Wqkv': jax.random.normal(ks[1], (D, 3 * D), dtype=jnp.float32) * 0.02, 'bqkv': jnp.zeros((3 * D,), dtype=jnp.float32), 'Wo': jax.random.normal(ks[2], (D, D), dtype=jnp.float32) * 0.02, 'bo': jnp.zeros((D,), dtype=jnp.float32), 'Wconv': jax.random.normal(ks[3], (H, 1, KS, 1), dtype=jnp.float32) * 0.1}
    _L2_attn_all = _L2_attn_setup()
    _L2_attn_in = {k: v for k, v in _L2_attn_all.items() if k in ('Wqkv', 'bqkv', 'Wo', 'bo', 'Wconv')}
    del _L2_attn_all

    def _L2_ffn_setup():
        import jax, jax.numpy as jnp
        import numpy as np
        DECAY = 0.9
        EPS = 0.01
        TOP_K = 2
        key = jax.random.key(seed)
        k1, k2, k3, k4 = jax.random.split(key, 4)
        B, S, H, I, E = (4, 512, 192, 512, 8)
        return {'hidden_states': jax.random.normal(k1, (B, S, H), jnp.float32), 'router_w': jax.random.normal(k2, (E, H), jnp.float32) * 0.02, 'w1': jax.random.normal(k3, (E, I, H), jnp.float32) * 0.02, 'w2': jax.random.normal(k4, (E, H, I), jnp.float32) * 0.02}
    _L2_ffn_all = _L2_ffn_setup()
    _L2_ffn_in = {k: v for k, v in _L2_ffn_all.items() if k in ('router_w', 'w1', 'w2')}
    del _L2_ffn_all

    def _L3_attn_setup():
        import jax, jax.numpy as jnp
        import numpy as np
        N_HEAD = 12
        key = jax.random.key(seed)
        k1, k2, k3 = jax.random.split(key, 3)
        C = 192
        x = jax.random.normal(k1, (2, 1024, C), dtype=jnp.float32)
        w_qkv = jax.random.normal(k2, (C, 3 * C), dtype=jnp.float32) * C ** (-0.5)
        w_proj = jax.random.normal(k3, (C, C), dtype=jnp.float32) * C ** (-0.5)
        return {'x': x, 'w_qkv': w_qkv, 'w_proj': w_proj}
    _L3_attn_all = _L3_attn_setup()
    _L3_attn_in = {k: v for k, v in _L3_attn_all.items() if k in ('w_qkv', 'w_proj')}
    del _L3_attn_all

    def _L3_ffn_setup():
        import jax, jax.numpy as jnp
        import numpy as np
        import math
        SQRT_2_OVER_PI = math.sqrt(2.0 / math.pi)

        def gelu(x):
            return x * 0.5 * (1.0 + jnp.tanh(SQRT_2_OVER_PI * (x + 0.044715 * x * x * x)))
        key = jax.random.key(seed)
        ks = jax.random.split(key, 6)
        B, S, D, M, E = (8, 128, 192, 768, 8)
        return {'x': jax.random.normal(ks[0], (B, S, D), dtype=jnp.float32), 'router_w': jax.random.normal(ks[1], (D, E), dtype=jnp.float32) * (1.0 / np.sqrt(D)), 'w1': jax.random.normal(ks[2], (E, D, M), dtype=jnp.float32) * (1.0 / np.sqrt(D)), 'b1': jax.random.normal(ks[3], (E, M), dtype=jnp.float32) * 1e-06, 'w2': jax.random.normal(ks[4], (E, M, D), dtype=jnp.float32) * (1.0 / np.sqrt(M)), 'b2': jax.random.normal(ks[5], (E, D), dtype=jnp.float32) * 1e-06}
    _L3_ffn_all = _L3_ffn_setup()
    _L3_ffn_in = {k: v for k, v in _L3_ffn_all.items() if k in ('router_w', 'w1', 'b1', 'w2', 'b2')}
    del _L3_ffn_all
    return {'x': x, 'L0_conv_norm1_w': _L0_conv_in['norm1_w'], 'L0_conv_norm1_b': _L0_conv_in['norm1_b'], 'L0_conv_qkv_w': _L0_conv_in['qkv_w'], 'L0_conv_qkv_b': _L0_conv_in['qkv_b'], 'L0_conv_proj_w': _L0_conv_in['proj_w'], 'L0_conv_proj_b': _L0_conv_in['proj_b'], 'L0_conv_rel_pos_h': _L0_conv_in['rel_pos_h'], 'L0_conv_rel_pos_w': _L0_conv_in['rel_pos_w'], 'L0_conv_norm2_w': _L0_conv_in['norm2_w'], 'L0_conv_norm2_b': _L0_conv_in['norm2_b'], 'L0_conv_fc1_w': _L0_conv_in['fc1_w'], 'L0_conv_fc1_b': _L0_conv_in['fc1_b'], 'L0_conv_fc2_w': _L0_conv_in['fc2_w'], 'L0_conv_fc2_b': _L0_conv_in['fc2_b'], 'L1_conv_w1': _L1_conv_in['w1'], 'L1_conv_w2': _L1_conv_in['w2'], 'L1_conv_b1': _L1_conv_in['b1'], 'L1_conv_b2': _L1_conv_in['b2'], 'L2_attn_Wqkv': _L2_attn_in['Wqkv'], 'L2_attn_bqkv': _L2_attn_in['bqkv'], 'L2_attn_Wo': _L2_attn_in['Wo'], 'L2_attn_bo': _L2_attn_in['bo'], 'L2_attn_Wconv': _L2_attn_in['Wconv'], 'L2_ffn_router_w': _L2_ffn_in['router_w'], 'L2_ffn_w1': _L2_ffn_in['w1'], 'L2_ffn_w2': _L2_ffn_in['w2'], 'L3_attn_w_qkv': _L3_attn_in['w_qkv'], 'L3_attn_w_proj': _L3_attn_in['w_proj'], 'L3_ffn_router_w': _L3_ffn_in['router_w'], 'L3_ffn_w1': _L3_ffn_in['w1'], 'L3_ffn_b1': _L3_ffn_in['b1'], 'L3_ffn_w2': _L3_ffn_in['w2'], 'L3_ffn_b2': _L3_ffn_in['b2']}

def reference(x, L0_conv_norm1_w, L0_conv_norm1_b, L0_conv_qkv_w, L0_conv_qkv_b, L0_conv_proj_w, L0_conv_proj_b, L0_conv_rel_pos_h, L0_conv_rel_pos_w, L0_conv_norm2_w, L0_conv_norm2_b, L0_conv_fc1_w, L0_conv_fc1_b, L0_conv_fc2_w, L0_conv_fc2_b, L1_conv_w1, L1_conv_w2, L1_conv_b1, L1_conv_b2, L2_attn_Wqkv, L2_attn_bqkv, L2_attn_Wo, L2_attn_bo, L2_attn_Wconv, L2_ffn_router_w, L2_ffn_w1, L2_ffn_w2, L3_attn_w_qkv, L3_attn_w_proj, L3_ffn_router_w, L3_ffn_w1, L3_ffn_b1, L3_ffn_w2, L3_ffn_b2):
    import jax
    import jax.numpy as jnp

    def _L0_conv_ref(x, norm1_w, norm1_b, qkv_w, qkv_b, proj_w, proj_b, rel_pos_h, rel_pos_w, norm2_w, norm2_b, fc1_w, fc1_b, fc2_w, fc2_b):
        import jax, jax.numpy as jnp
        import numpy as np
        WS = 14
        NUM_HEADS = 12
        EPS = 1e-06

        def _ln(x, w, b):
            mu = jnp.mean(x, axis=-1, keepdims=True)
            var = jnp.mean(jnp.square(x - mu), axis=-1, keepdims=True)
            return (x - mu) * jax.lax.rsqrt(var + EPS) * w + b
        B, H, W, C = x.shape
        hd = C // NUM_HEADS
        scale = hd ** (-0.5)
        shortcut = x
        h = _ln(x, norm1_w, norm1_b)
        pad_h = -H % WS
        pad_w = -W % WS
        Hp, Wp = (H + pad_h, W + pad_w)
        hp = jnp.pad(h, ((0, 0), (0, pad_h), (0, pad_w), (0, 0)))
        win = hp.reshape(B, Hp // WS, WS, Wp // WS, WS, C)
        win = win.transpose(0, 1, 3, 2, 4, 5).reshape(-1, WS, WS, C)
        Bw = win.shape[0]
        N = WS * WS
        qkv = win.reshape(Bw, N, C) @ qkv_w + qkv_b
        qkv = qkv.reshape(Bw, N, 3, NUM_HEADS, hd).transpose(2, 0, 3, 1, 4)
        qkv = qkv.reshape(3, Bw * NUM_HEADS, N, hd)
        q, k, v = (qkv[0], qkv[1], qkv[2])
        attn = jnp.einsum('bqc,bkc->bqk', q * scale, k)
        idx = jnp.arange(WS)[:, None] - jnp.arange(WS)[None, :] + (WS - 1)
        Rh = rel_pos_h[idx]
        Rw = rel_pos_w[idx]
        r_q = q.reshape(-1, WS, WS, hd)
        rel_h = jnp.einsum('bhwc,hkc->bhwk', r_q, Rh)
        rel_w = jnp.einsum('bhwc,wkc->bhwk', r_q, Rw)
        attn = (attn.reshape(-1, WS, WS, WS, WS) + rel_h[:, :, :, :, None] + rel_w[:, :, :, None, :]).reshape(-1, N, N)
        attn = jax.nn.softmax(attn, axis=-1)
        out = attn @ v
        out = out.reshape(Bw, NUM_HEADS, WS, WS, hd).transpose(0, 2, 3, 1, 4)
        out = out.reshape(Bw, WS, WS, C) @ proj_w + proj_b
        xw = out.reshape(B, Hp // WS, Wp // WS, WS, WS, C)
        xw = xw.transpose(0, 1, 3, 2, 4, 5).reshape(B, Hp, Wp, C)[:, :H, :W, :]
        x = shortcut + xw
        h2 = _ln(x, norm2_w, norm2_b)
        h2 = jax.nn.gelu(h2 @ fc1_w + fc1_b, approximate=False)
        h2 = h2 @ fc2_w + fc2_b
        return x + h2

    def _L1_conv_ref(x, w1, w2, b1, b2):
        import jax, jax.numpy as jnp
        import numpy as np
        NUM_BLOCKS = 8
        BLOCK_SIZE = 24
        LAMBDA = 0.01

        def softshrink(x, lam=LAMBDA):
            return jnp.sign(x) * jnp.maximum(jnp.abs(x) - lam, 0.0)
        bias = x
        B, H, W, C = x.shape
        xf = jnp.fft.rfft2(x.astype(jnp.float32), axes=(1, 2), norm='ortho')
        Wf = xf.shape[2]
        xf = xf.reshape(B, H, Wf, NUM_BLOCKS, BLOCK_SIZE)
        xr, xi = (jnp.real(xf), jnp.imag(xf))
        o1r = jnp.einsum('bhwki,kio->bhwko', xr, w1[0]) - jnp.einsum('bhwki,kio->bhwko', xi, w1[1]) + b1[0]
        o1i = jnp.einsum('bhwki,kio->bhwko', xi, w1[0]) + jnp.einsum('bhwki,kio->bhwko', xr, w1[1]) + b1[1]
        o1r = softshrink(o1r)
        o1i = softshrink(o1i)
        o2r = jnp.einsum('bhwki,kio->bhwko', o1r, w2[0]) - jnp.einsum('bhwki,kio->bhwko', o1i, w2[1]) + b2[0]
        o2i = jnp.einsum('bhwki,kio->bhwko', o1i, w2[0]) + jnp.einsum('bhwki,kio->bhwko', o1r, w2[1]) + b2[1]
        o2r = softshrink(o2r)
        o2i = softshrink(o2i)
        yf = (o2r + 1j * o2i).reshape(B, H, Wf, C)
        y = jnp.fft.irfft2(yf, s=(H, W), axes=(1, 2), norm='ortho')
        return y.astype(x.dtype) + bias

    def _L2_attn_ref(x, Wqkv, bqkv, Wo, bo, Wconv):
        import jax, jax.numpy as jnp
        import numpy as np
        from jax import lax
        B, S, D = (4, 1024, 192)
        H, LM, KS = (12, 16, 33)
        HD = D // H

        def _iterative_pinv(k_mat, n_iter=6):
            m = k_mat.shape[-1]
            I = jnp.eye(m, dtype=k_mat.dtype)
            v = (1.0 / jnp.max(jnp.sum(k_mat, axis=-2), axis=-1))[:, None, None] * jnp.swapaxes(k_mat, -1, -2)
            for _ in range(n_iter):
                kv = k_mat @ v
                v = 0.25 * v @ (13.0 * I - kv @ (15.0 * I - kv @ (7.0 * I - kv)))
            return v
        b, s, dim = x.shape
        qkv = x @ Wqkv + bqkv
        q, k, v = jnp.split(qkv, 3, axis=-1)

        def to_heads(t):
            return t.reshape(b, s, H, HD).transpose(0, 2, 1, 3).reshape(b * H, s, HD)
        q, k, v = (to_heads(q), to_heads(k), to_heads(v))
        scale = 1.0 / np.sqrt(HD).astype(np.float32)
        seg = s // LM

        def pool(t):
            return t.reshape(b * H, LM, seg, HD).mean(axis=2)
        q_l, k_l = (pool(q), pool(k))
        kernel_1 = jax.nn.softmax(jnp.einsum('bsd,bmd->bsm', q, k_l) * scale, axis=-1)
        kernel_2 = jax.nn.softmax(jnp.einsum('bmd,bnd->bmn', q_l, k_l) * scale, axis=-1)
        attn_3 = jax.nn.softmax(jnp.einsum('bmd,bsd->bms', q_l, k) * scale, axis=-1)
        kernel_3 = attn_3 @ v
        kernel_2_inv = _iterative_pinv(kernel_2, n_iter=6)
        x_out = kernel_1 @ kernel_2_inv @ kernel_3
        v4 = v.reshape(b, H, s, HD)
        pad = KS // 2
        v_conv = lax.conv_general_dilated(v4, Wconv, window_strides=(1, 1), padding=((pad, pad), (0, 0)), dimension_numbers=('NCHW', 'OIHW', 'NCHW'), feature_group_count=H)
        x_out = x_out + v_conv.reshape(b * H, s, HD)
        x_out = x_out.reshape(b, H, s, HD).transpose(0, 2, 1, 3).reshape(b, s, dim)
        return x_out @ Wo + bo

    def _L2_ffn_ref(hidden_states, router_w, w1, w2):
        import jax, jax.numpy as jnp
        import numpy as np
        DECAY = 0.9
        EPS = 0.01
        TOP_K = 2
        B, S, H = hidden_states.shape
        E = router_w.shape[0]
        flat = hidden_states.reshape(B * S, H)
        logits = flat @ router_w.T
        probs = jax.nn.softmax(logits, axis=-1)
        topk_probs, topk_idx = jax.lax.top_k(probs, TOP_K)
        importance = jax.lax.stop_gradient(probs).sum(axis=0)
        running = jnp.ones((E,), dtype=flat.dtype)
        blended = running + (1.0 - DECAY) * (importance - running)
        running = blended + EPS
        balance = running[topk_idx]
        balanced = topk_probs / balance
        balanced = balanced / balanced.sum(axis=-1, keepdims=True)
        h = jnp.einsum('th,eih->tei', flat, w1)
        h = jax.nn.silu(h)
        outs = jnp.einsum('tei,ehi->teh', h, w2)
        sel = jnp.take_along_axis(outs, topk_idx[:, :, None], axis=1)
        combined = (sel * balanced[..., None]).sum(axis=1)
        return combined.reshape(B, S, H)

    def _L3_attn_ref(x, w_qkv, w_proj):
        import jax, jax.numpy as jnp
        import numpy as np
        N_HEAD = 12
        B, T, C = x.shape
        H = N_HEAD
        D = C // H
        qkv = x @ w_qkv
        q, k, v = jnp.split(qkv, 3, axis=-1)
        q = q.reshape(B, T, H, D).transpose(0, 2, 1, 3)
        k = k.reshape(B, T, H, D).transpose(0, 2, 1, 3)
        v = v.reshape(B, T, H, D).transpose(0, 2, 1, 3)
        scale = 1.0 / D ** 0.5
        att = jnp.einsum('bhqd,bhkd->bhqk', q, k) * scale
        att = jax.nn.softmax(att, axis=-1)
        y = jnp.einsum('bhqk,bhkd->bhqd', att, v)
        y = y.transpose(0, 2, 1, 3).reshape(B, T, C)
        return y @ w_proj

    def _L3_ffn_ref(x, router_w, w1, b1, w2, b2):
        import jax, jax.numpy as jnp
        import numpy as np
        import math
        SQRT_2_OVER_PI = math.sqrt(2.0 / math.pi)

        def gelu(x):
            return x * 0.5 * (1.0 + jnp.tanh(SQRT_2_OVER_PI * (x + 0.044715 * x * x * x)))
        B, S, D = x.shape
        E = router_w.shape[1]
        T = B * S
        C = T // E
        xf = x.reshape(T, D)
        router_logits = xf @ router_w
        router_probs = jax.nn.softmax(router_logits, axis=-1)
        expert_gate = jnp.max(router_probs, axis=-1)
        expert_index = jnp.argmax(router_probs, axis=-1)
        expert_mask = jax.nn.one_hot(expert_index, E, dtype=xf.dtype)
        position_in_expert = (jnp.cumsum(expert_mask, axis=0) * expert_mask).astype(jnp.int32)
        expert_mask = expert_mask * (position_in_expert < C).astype(xf.dtype)
        expert_mask_flat = jnp.sum(expert_mask, axis=-1)
        expert_gate = expert_gate * expert_mask_flat
        combine = (expert_gate * expert_mask_flat)[:, None, None] * jax.nn.one_hot(expert_index, E, dtype=xf.dtype)[:, :, None] * jax.nn.one_hot(position_in_expert, C, dtype=xf.dtype)
        dispatch = (combine != 0).astype(xf.dtype)
        expert_inputs = jnp.einsum('td,tec->ecd', xf, dispatch)
        h = gelu(jnp.einsum('ecd,edm->ecm', expert_inputs, w1) + b1[:, None, :])
        expert_outputs = gelu(jnp.einsum('ecm,emd->ecd', h, w2) + b2[:, None, :])
        out = jnp.einsum('ecd,tec->td', expert_outputs, combine)
        return out.reshape(B, S, D)

    def _gn(v, G=32, eps=1e-05):
        B_, H_, W_, C_ = v.shape
        g = v.reshape(B_, H_, W_, G, C_ // G)
        m = jnp.mean(g, axis=(1, 2, 4), keepdims=True)
        s = jnp.var(g, axis=(1, 2, 4), keepdims=True)
        return ((g - m) / jnp.sqrt(s + eps)).reshape(v.shape)

    def _ln_c(v, eps=1e-06):
        m = jnp.mean(v, axis=-1, keepdims=True)
        s = jnp.var(v, axis=-1, keepdims=True)
        return (v - m) / jnp.sqrt(s + eps)

    def _ln_t(v, eps=1e-05):
        m = jnp.mean(v, axis=-1, keepdims=True)
        s = jnp.var(v, axis=-1, keepdims=True)
        return (v - m) / jnp.sqrt(s + eps)

    def _to_tokens(v):
        B_, H_, W_, C_ = v.shape
        return v.reshape(B_, H_ * W_, C_)

    def _from_tokens(t, like):
        return t.reshape(like.shape)
    x = _L0_conv_ref(x, L0_conv_norm1_w, L0_conv_norm1_b, L0_conv_qkv_w, L0_conv_qkv_b, L0_conv_proj_w, L0_conv_proj_b, L0_conv_rel_pos_h, L0_conv_rel_pos_w, L0_conv_norm2_w, L0_conv_norm2_b, L0_conv_fc1_w, L0_conv_fc1_b, L0_conv_fc2_w, L0_conv_fc2_b)
    x = x + _L1_conv_ref(_gn(x), L1_conv_w1, L1_conv_w2, L1_conv_b1, L1_conv_b2)
    t = _to_tokens(x)
    t = t + _L2_attn_ref(_ln_t(t), L2_attn_Wqkv, L2_attn_bqkv, L2_attn_Wo, L2_attn_bo, L2_attn_Wconv)
    t = t + _L2_ffn_ref(_ln_t(t), L2_ffn_router_w, L2_ffn_w1, L2_ffn_w2)
    t = t + _L3_attn_ref(_ln_t(t), L3_attn_w_qkv, L3_attn_w_proj)
    t = t + _L3_ffn_ref(_ln_t(t), L3_ffn_router_w, L3_ffn_w1, L3_ffn_b1, L3_ffn_w2, L3_ffn_b2)
    x = _from_tokens(t, x)
    return x

_drawn_inputs = setup_inputs


def setup_inputs(seed=0):
    import zlib

    import numpy as np

    out = dict(_drawn_inputs(seed))
    spreads = {'L0_conv_norm1_w': (1.0, 0.6),
     'L0_conv_norm1_b': (0.0, 0.73),
     'L0_conv_norm2_w': (1.0, 0.6),
     'L0_conv_norm2_b': (0.0, 0.8),
     'L1_conv_b1': (0.0, 0.1),
     'L1_conv_b2': (0.0, 0.1),
     'L2_attn_bqkv': (0.0, 0.536),
     'L2_attn_bo': (0.0, 0.1)}
    factors = {'L0_conv_qkv_w': 5.388,
     'L0_conv_qkv_b': 8.0,
     'L0_conv_proj_w': 4.468,
     'L0_conv_proj_b': 3.29,
     'L0_conv_rel_pos_h': 8.0,
     'L0_conv_rel_pos_w': 8.0,
     'L0_conv_fc1_b': 8.0,
     'L0_conv_fc2_b': 2.865,
     'L2_attn_Wqkv': 3.525,
     'L2_attn_Wo': 2.844,
     'L2_attn_Wconv': 3.353,
     'L2_ffn_router_w': 3.587,
     'L2_ffn_w1': 3.168,
     'L2_ffn_w2': 3.204,
     'L3_ffn_b1': 8.0,
     'L3_ffn_b2': 8.0}
    for name, (base, spread) in spreads.items():
        noise = np.random.default_rng([zlib.crc32(name.encode()), seed]).standard_normal(out[name].shape)
        drawn = base * np.exp(spread * noise) if base else spread * noise
        out[name] = jnp.asarray(drawn.astype(out[name].dtype))
    for name, factor in factors.items():
        out[name] = (out[name] * factor).astype(out[name].dtype)
    return out
```

```python
from contextlib import ExitStack, contextmanager

import concourse.bass as bass
from concourse import mybir

F32 = mybir.dt.float32
BF16 = mybir.dt.bfloat16
I32 = mybir.dt.int32
U32 = mybir.dt.uint32
ALU = mybir.AluOpType
ACT = mybir.ActivationFunctionType
AX = mybir.AxisListType

B, HH, WW, C = 8, 16, 16, 192
T = HH * WW
P = 128
NT = B * T // P
TI = T // P
NH, HD = 12, 16
CH = C // 2
HB = CH // HD
WS = 14
W0 = WS * WS
WQ = W0 // 2
EXT = T - W0
PADS = W0 - 4
EK = EXT + PADS
EKT = EK // 2
REL = 2 * WS
SR = 96
FF = 768
MF = FF // P
Q_TERM = (0, 0, 1, 1, 0, 2)
K_TERM = (0, 1, 0, 1, 2, 0)


def free(ap, *dims):
    return bass.AP(tensor=ap.tensor, offset=ap.offset, ap=[list(ap.ap[0])] + [list(d) for d in dims])


def rows(ap, offset, *dims):
    return bass.AP(tensor=ap.tensor, offset=offset, ap=[list(d) for d in dims])


def wait_all(eng, steady, *waits):
    values = [value if isinstance(value, int) else eng.to_reg(value) for _, value in waits]
    eng.wait_ge(waits[0][0], 1)
    eng.wait_ge(steady, 1)
    for (sem, _), value in zip(waits, values):
        eng.wait_ge(sem, value)


class Stage:

    def __init__(self, nc, name):
        self.nc, self.name, self.ctx, self.used = nc, name, ExitStack(), []

    def __enter__(self):
        self.ctx.__enter__()
        return self

    def __exit__(self, *e):
        left = self.ctx.__exit__(*e)
        numbers = sorted(self.used)
        first = 0
        for k in range(1, len(numbers) + 1):
            if k == len(numbers) or numbers[k] != numbers[k - 1] + 1:
                self.nc.gpsimd.sem_clear(range(numbers[first], numbers[k - 1] + 1))
                first = k
        return left

    def sb(self, name, shape, dt=F32):
        return self.ctx.enter_context(self.nc.sbuf_tensor(f"{self.name}_{name}", shape, dt))

    def ps(self, name, shape=(P, 512), dt=F32):
        return self.ctx.enter_context(self.nc.psum_tensor(f"{self.name}_{name}", list(shape), dt))

    def sem(self, name):
        sem = self.ctx.enter_context(self.nc.semaphore(f"{self.name}_{name}"))
        self.used.append(sem.num)
        return sem

    def sems(self, names):
        return [self.sem(n) for n in names.split()]

    def block(self):
        return self.ctx.enter_context(self.nc.Block())


class LnStats:

    def __init__(self, st, G, eps):
        self.nc, self.G, self.eps = st.nc, G, eps
        self.part = st.sb("stat_part", [P, 2, TI, 6])
        self.mv = st.sb("stat_mv", [P, 2, TI, 2])
        self.ve = st.sb("stat_ve", [P, 2, TI])
        self.rstd = st.sb("stat_rstd", [P, 2, TI])
        self.exponent = st.sb("stat_exponent", [P, TI])
        self.parts_done, self.mv_done, self.pow_done, self.kept = st.sems("stat_parts stat_mv stat_pow stat_kept")

    def init(self, pool):
        pool.sem_inc(self.kept, 2)
        self.nc.gpsimd.memset(self.exponent[:, :], -0.5).then_inc(self.pow_done, 1)

    def vector(self, nc, dve, i, u, *ready):
        wait_all(dve, self.G["steady"], *ready, (self.kept, i + 1))
        for t in range(TI):
            nc.vector.bn_stats(self.part[:, u, t, :], self.G["X"][:, bass.ds(TI * i + t, 1), :].rearrange("p a c -> p (a c)")).then_inc(self.parts_done, 1)
        wait_all(dve, self.G["steady"], (self.parts_done, TI * (i + 1)))
        for t in range(TI):
            nc.vector.bn_aggr(self.mv[:, u, t, :], self.part[:, u, t, :]).then_inc(self.mv_done, 1)

    def gpsimd(self, nc, pool, i, u):
        wait_all(pool, self.G["steady"], (self.mv_done, TI * (i + 1)))
        nc.gpsimd.tensor_scalar(self.ve[:, u, :], self.mv[:, u, :, 1], self.eps, None, ALU.add).then_inc(self.pow_done, 1)
        pool.wait_ge(self.pow_done, 2 * i + 2)
        nc.gpsimd.tensor_tensor(self.rstd[:, u, :], self.ve[:, u, :], self.exponent[:, :], ALU.pow).then_inc(self.pow_done, 1)
        wait_all(pool, self.G["steady"], (self.pow_done, 2 * i + 3))
        nc.gpsimd.tensor_copy(self.G["MEAN"][:, bass.ds(TI * i, TI)], self.mv[:, u, :, 0])
        nc.gpsimd.tensor_copy(self.G["RSTD"][:, bass.ds(TI * i, TI)], self.rstd[:, u, :]).then_inc(self.kept, 1)


class Normed:

    def __init__(self, st, G, weights=None):
        self.st, self.G, self.weights = st, G, weights
        self.xn = st.sb("xn", [P, 2, TI, C])
        self.xT = [st.sb(f"xT{u}", [CH, 2, T]) for u in range(2)]
        self.psT = [st.ps(f"psT{u}") for u in range(2)]
        self.normed, self.turned, self.xT_done, self.xT_free = st.sems("xn_done xn_turned xT_done xT_free")

    def vector(self, nc, dve, i, u):
        dve.wait_ge(self.turned, i + 1)
        for t in range(TI):
            k = TI * i + t
            nc.vector.tensor_scalar(self.xn[:, u, t, :], self.G["X"][:, bass.ds(k, 1), :].rearrange("p a c -> p (a c)"),
                                    self.G["MEAN"][:, bass.ds(k, 1)], self.G["RSTD"][:, bass.ds(k, 1)],
                                    ALU.subtract, ALU.mult).then_inc(self.normed, 1)

    def tensor(self, nc, pe, i, u):
        pe.wait_ge(self.normed, TI * (i + 1))
        pe.wait_ge(self.xT_done, i + 1)
        ps = self.psT[u][0:CH, :].rearrange("p (k n) -> p k n", k=2)
        for t in range(TI):
            for k in range(2):
                mm = nc.tensor.transpose(ps[:, k, t * P:(t + 1) * P], self.xn[:, u, t, k * CH:(k + 1) * CH], self.G["ident"][:, :])
        mm.then_inc(self.turned, 1)

    def scalar(self, nc, act, i, u):
        act.wait_ge(self.turned, i + 3)
        act.wait_ge(self.xT_free, i + 1)
        ps = self.psT[u][0:CH, :].rearrange("p (k n) -> p k n", k=2)
        if self.weights is None:
            nc.scalar.activation(self.xT[u][:, :, :], ps, ACT.Copy).then_inc(self.xT_done, 1)
        else:
            w, b = self.weights
            nc.scalar.activation(self.xT[u][:, 0, :], ps[:, 0, :], ACT.Identity, bias=b[:, 0:1], scale=w[:, 0:1])
            nc.scalar.activation(self.xT[u][:, 1, :], ps[:, 1, :], ACT.Identity, bias=b[:, 1:2], scale=w[:, 1:2]).then_inc(self.xT_done, 1)

    def init_credit(self, eng):
        eng.sem_inc(self.turned, 2)
        eng.sem_inc(self.xT_done, 2)
        eng.sem_inc(self.xT_free, 2)


@contextmanager
def images(eng):
    with eng.Fori(0, B // 2) as pair:
        yield pair * 2


KS = 33
TW = P + KS - 1


def load_x(nc, G, x, w_conv, consts):
    with Stage(nc, "load") as st:
        taps, rev, backwards = st.sb("taps", [KS, NH]), st.sb("rev", [KS, KS]), st.sb("backwards", [NH, KS])
        psR = st.ps("psR")
        taps_in, rev_mm, rev_done, band_out = st.sems("taps_in rev_mm rev_done band_out")
        stats = LnStats(st, G, 1e-6)
        ordered, loaded, const_in = st.sems("ordered loaded const_in")
        xw = G["xw"]
        block = st.block()

        @block.sync
        def _(sp):
            for r0, c0, h, w, n0 in WINDOWS:
                sp.dma_start(rows(xw, n0 * C, [T * C, B], [w * C, h], [1, w * C]),
                             rows(x, (r0 * WW + c0) * C, [T * C, B], [WW * C, h], [1, w * C])).then_inc(ordered, 16)
            sp.wait_ge(ordered, 16 * len(WINDOWS))
            for i in range(0, B, 2):
                sp.dma_start(G["X"][:, TI * i:TI * (i + 2), :], rows(xw, i * T * C, [C, P], [P * C, 2 * TI], [1, C])).then_inc(loaded, 16)

        @block.scalar
        def _(act):
            act.sem_inc(G["steady"], 1)
            act.dma_start(taps[:, :], rows(w_conv, 0, [1, KS], [KS, NH]), allow_slow_non_contiguous=True).then_inc(taps_in, 16)
            act.dma_start(rev[:, :], consts["reverse"]).then_inc(taps_in, 16)
            act.dma_start(G["ident"][:, :], consts["ident"]).then_inc(const_in, 16)
            act.dma_start(rows(G["band"], 0, [P * TW, NH], [8 * TW, P // 8], [1, 8 * TW]), rows(consts["zeros"], 0, [0, NH], [0, P // 8], [1, 8 * TW])).then_inc(band_out, 16)
            act.wait_ge(rev_mm, 1)
            nc.scalar.activation(backwards[:, :], psR[0:NH, 0:KS], ACT.Copy).then_inc(rev_done, 1)
            act.wait_ge(band_out, 16)
            act.wait_ge(rev_done, 1)
            act.dma_start(rows(G["band"], 0, [P * TW, NH], [TW + 1, P], [1, KS]), free(backwards[:, 0:1], [0, P], [1, KS])).then_inc(band_out, 16)
            act.wait_ge(band_out, 32)
            act.wait_ge(const_in, 16)

        @block.tensor
        def _(pe):
            pe.wait_ge(taps_in, 32)
            nc.tensor.matmul(psR[0:NH, 0:KS], taps[:, :], rev[:, :], start=True, stop=True).then_inc(rev_mm, 1)

        @block.vector
        def _(dve):
            dve.wait_ge(loaded, 8 * B)
            with images(dve) as i:
                for u in range(2):
                    stats.vector(nc, dve, i + u, u)

        @block.gpsimd
        def _(pool):
            stats.init(pool)
            with images(pool) as i:
                for u in range(2):
                    stats.gpsimd(nc, pool, i + u, u)


WINDOWS = ((0, 0, WS, WS, 0), (0, WS, WS, WW - WS, W0), (WS, 0, HH - WS, WS, W0 + WS * (WW - WS)),
           (WS, WS, HH - WS, WW - WS, T - (HH - WS) * (WW - WS)))


class Pieces:

    def __init__(self, st, G, name, prt, dims):
        self.G = G
        self.p = [st.sb(f"{name}_p{u}", [prt, 3, *dims], BF16) for u in range(2)]
        self.r = [st.sb(f"{name}_r{u}", [prt, *dims]) for u in range(2)]
        self.p0, self.rest, self.p1, self.p2, *self.out = st.sems(f"{name}_p0 {name}_rest {name}_p1 {name}_p2 {name}_out0 {name}_out1")

    def scalar(self, nc, act, src, i, u, *ready):
        wait_all(act, self.G["steady"], *ready, (self.out[u], 8 * (i - u) + 16))
        nc.scalar.activation(self.p[u][:, 0], src, ACT.Copy).then_inc(self.p0, 1)

    def init(self, act):
        for u in range(2):
            act.sem_inc(self.out[u], 16)

    def finish(self, sp):
        for u in range(2):
            sp.wait_ge(self.out[u], 8 * B + 16)

    def vector(self, nc, dve, src, i, u):
        dve.wait_ge(self.p0, i + 1)
        nc.vector.tensor_tensor(self.r[u][:], src, self.p[u][:, 0], ALU.subtract).then_inc(self.rest, 1)

    def second(self, nc, act, i, u):
        act.wait_ge(self.rest, i + 1)
        nc.scalar.activation(self.p[u][:, 1], self.r[u][:], ACT.Copy).then_inc(self.p1, 1)

    def gpsimd(self, nc, pool, i, u):
        pool.wait_ge(self.p1, i + 1)
        nc.gpsimd.tensor_tensor(self.p[u][:, 2], self.r[u][:], self.p[u][:, 1], ALU.subtract).then_inc(self.p2, 1)

    def sync(self, sp, dst, i, u):
        sp.wait_ge(self.p2, i + 1)
        sp.dma_start(dst, self.p[u][:]).then_inc(self.out[u], 16)


def image_of(ap, i, size, *dims):
    base = ap[bass.ds(i, 1), :]
    return bass.AP(tensor=base.tensor, offset=base.offset, ap=[list(d) for d in dims])


def attention_inputs(nc, G, name, w_qkv, affine, v_tiles):
    with Stage(nc, name) as st:
        wn, bn = st.sb("wn", [CH, 2]), st.sb("bn", [CH, 2])
        W = st.sb("W", [CH, 2, 3 * C])
        qkb = st.sb("qkb", [CH, 6])
        kb4 = st.sb("kb4", [CH, 2])
        KF = [st.sb(f"KF{u}", [CH, 2, T]) for u in range(2)]
        kbp = st.sb("kbp", [CH, 3, 2], BF16)
        kbr = st.sb("kbr", [CH, 2])
        nm = Normed(st, G, (wn, bn) if affine else None)
        QFu = None if affine else [st.sb(f"QF{u}", [CH, 2, T]) for u in range(2)]
        qp, kp = Pieces(st, G, "q", CH, (2, T)), Pieces(st, G, "k", CH, (2, T))
        psQ, psK = st.ps("psQ"), st.ps("psK")
        psV, psE = [st.ps(f"psV{u}") for u in range(2)], [st.ps(f"psE{u}") for u in range(2)]
        vn, nv = v_tiles[0][1], len(v_tiles)
        w_in, b_in, q_mm, q_free, k_mm, k_free, v_free = st.sems("w_in b_in q_mm q_free k_mm k_free v_free")
        kb_step, kb_out, kf_free, qf_free = st.sems("kb_step kb_out kf_free qf_free")
        Vall = G["Vall"]
        q_of = lambda i, u: G["QF"][:, :, bass.ds(i * T, T)] if affine else QFu[u][:, :, :]
        block = st.block()

        @block.sync
        def _(sp):
            sp.dma_start(W[:, :, :], w_qkv.rearrange("(k p) n -> p k n", p=CH)).then_inc(w_in, 16)
            if affine:
                norm_w, norm_b, b_qkv, b_out = affine
                sp.dma_start(wn[:, :], norm_w.rearrange("(k p) -> p k", p=CH), allow_slow_non_contiguous=True).then_inc(b_in, 16)
                sp.dma_start(bn[:, :], norm_b.rearrange("(k p) -> p k", p=CH), allow_slow_non_contiguous=True).then_inc(b_in, 16)
                sp.dma_start(qkb[:, :], b_qkv.rearrange("(m p) -> p m", p=CH), allow_slow_non_contiguous=True).then_inc(b_in, 16)
                sp.dma_start(G["vb"][:, :], rows(b_qkv, 2 * C, [0, P], [1, C])).then_inc(b_in, 16)
                sp.dma_start(G["pb"][:, :], rows(b_out, 0, [0, P], [1, C])).then_inc(b_in, 16)
                sp.wait_ge(kb_step, 5)
                sp.dma_start(rows(G["kbd"], 0, [1, CH], [2 * CH, 3], [CH, 2]), kbp[:, :, :],
                             allow_slow_non_contiguous=True).then_inc(kb_out, 16)
            with images(sp) as i:
                for u in range(2):
                    qp.sync(sp, image_of(G["qd"], i + u, 0, [T, CH], [C * T, 3], [CH * T, 2], [1, T]), i + u, u)
                    kp.sync(sp, image_of(G["kd"], i + u, 0, [T, CH], [C * T, 3], [CH * T, 2], [1, T]), i + u, u)
            if affine:
                sp.wait_ge(kb_out, 16)
            qp.finish(sp)
            kp.finish(sp)

        @block.gpsimd
        def _(pool):
            with images(pool) as i:
                for u in range(2):
                    qp.gpsimd(nc, pool, i + u, u)
                    kp.gpsimd(nc, pool, i + u, u)

        @block.tensor
        def _(pe):
            nm.init_credit(pe)
            for s in (q_free, k_free):
                pe.sem_inc(s, 1)
            pe.sem_inc(v_free, 2)
            pe.wait_ge(w_in, 16)
            with images(pe) as i:
                for u in range(2):
                    nm.tensor(nc, pe, i + u, u)
                for u in range(2):
                    pe.wait_ge(nm.xT_done, i + u + 3)
                    for ps, m0, is_free, done in ((psQ, 0, q_free, q_mm), (psK, 2, k_free, k_mm)):
                        pe.wait_ge(is_free, i + u + 1)
                        for a in range(2):
                            for k in range(2):
                                mm = nc.tensor.matmul(ps[0:CH, a * T:(a + 1) * T], W[:, k, (m0 + a) * CH:(m0 + a + 1) * CH],
                                                      nm.xT[u][:, k, :], start=(k == 0), stop=(k == 1))
                        mm.then_inc(done, 1)
                    pe.wait_ge(v_free, i + u + 1)
                    for t, (n0, n) in enumerate(v_tiles):
                        ps = psE[u][0:n, 0:C] if t == 2 else psV[u][0:n, t * C:(t + 1) * C]
                        for k in range(2):
                            mm = nc.tensor.matmul(ps, nm.xT[u][:, k, n0:n0 + n], W[:, k, 2 * C:], start=(k == 0), stop=(k == 1))
                    mm.then_inc(nm.xT_free, 1)

        @block.scalar
        def _(act):
            qp.init(act)
            kp.init(act)
            act.sem_inc(kf_free, 2)
            act.sem_inc(qf_free, 2)
            if affine:
                act.wait_ge(b_in, 80)
                nc.scalar.activation(kb4[:, :], qkb[:, 2:4], ACT.Copy, scale=HD ** -0.5).then_inc(kb_step, 1)
                act.wait_ge(kb_step, 1)

            def evacuate(dst, ps, bias, scale):
                if affine:
                    for a in range(2):
                        ev = nc.scalar.activation(dst[:, a, :], ps[0:CH, a * T:(a + 1) * T], ACT.Identity, bias=bias[:, a:a + 1], scale=scale)
                    return ev
                return nc.scalar.activation(dst, ps[0:CH, :].rearrange("p (a n) -> p a n", a=2), ACT.Copy, scale=scale)

            with images(act) as i:
                for u in range(2):
                    nm.scalar(nc, act, i + u, u)
                for u in range(2):
                    act.wait_ge(q_mm, i + u + 1)
                    if not affine:
                        act.wait_ge(qf_free, i + u + 1)
                    evacuate(q_of(i + u, u), psQ, qkb[:, 0:2], 1.0).then_inc(q_free, 1)
                    act.wait_ge(k_mm, i + u + 1)
                    act.wait_ge(kf_free, i + u + 1)
                    evacuate(KF[u][:, :, :], psK, kb4, HD ** -0.5).then_inc(k_free, 1)
                    qp.scalar(nc, act, q_of(i + u, u), i + u, u, (q_free, i + u + 2))
                    kp.scalar(nc, act, KF[u][:, :, :], i + u, u, (k_free, i + u + 2))
                for u in range(2):
                    qp.second(nc, act, i + u, u)
                    kp.second(nc, act, i + u, u)

        @block.vector
        def _(dve):
            if affine:
                dve.wait_ge(kb_step, 1)
                nc.vector.tensor_copy(kbp[:, 0, :], kb4[:, :]).then_inc(kb_step, 1)
                dve.wait_ge(kb_step, 2)
                nc.vector.tensor_tensor(kbr[:, :], kb4[:, :], kbp[:, 0, :], ALU.subtract).then_inc(kb_step, 1)
                dve.wait_ge(kb_step, 3)
                nc.vector.tensor_copy(kbp[:, 1, :], kbr[:, :]).then_inc(kb_step, 1)
                dve.wait_ge(kb_step, 4)
                nc.vector.tensor_tensor(kbp[:, 2, :], kbr[:, :], kbp[:, 1, :], ALU.subtract).then_inc(kb_step, 1)
                dve.wait_ge(b_in, 80)
            with images(dve) as i:
                for u in range(2):
                    nm.vector(nc, dve, i + u, u)
                for u in range(2):
                    qp.vector(nc, dve, q_of(i + u, u), i + u, u)
                    kp.vector(nc, dve, KF[u][:, :, :], i + u, u)
                    dve.wait_ge(kp.rest, i + u + 1)
                    dve.sem_inc(kf_free, 1)
                    dve.sem_inc(qf_free, 1)
                    dve.wait_ge(nm.xT_free, i + u + 3)
                    V = Vall[0:vn, bass.ds((i + u) * nv, 2), :]
                    ps = psV[u][0:vn, 0:2 * C].rearrange("p (t c) -> p t c", t=2)
                    if not affine:
                        nc.vector.tensor_copy(V, ps).then_inc(v_free, 1)
                    else:
                        nc.vector.tensor_tensor(V, ps, free(G["vb"][0:vn, :], [0, 2], [1, C]), ALU.add)
                        nc.vector.tensor_tensor(Vall[0:EXT, bass.ds((i + u) * nv + 2, 1), :], psE[u][0:EXT, 0:C].rearrange("p (t c) -> p t c", t=1),
                                                free(G["vb"][0:EXT, :], [C, 1], [1, C]), ALU.add).then_inc(v_free, 1)


def runs(axis):
    for r0, c0, h, w, n0 in WINDOWS:
        yield (h, n0, w, w, 1) if axis == 0 else (w, n0, 1, h, w)


def l0_rel(nc, G, w, consts):
    with Stage(nc, "l0r") as st:
        NJ = 2 * WS - 1
        RT = st.sb("RT", [CH, 2, NJ])
        Rbd = st.sb("Rbd", [CH, 2, WS, HB * WS])
        hm = st.sb("hm", [CH, HB])
        RHW = st.sb("RHW", [HB * WS, 4, B * T])
        rp = Pieces(st, G, "r", HB * WS, (4, T))
        ps = [st.ps(f"ps{c}") for c in range(5)]
        full, emptied = [st.sem(f"full{c}") for c in range(5)], [st.sem(f"emptied{c}") for c in range(5)]
        t_in, rbd_done = st.sems("t_in rbd_done")
        QF = G["QF"]

        def fills(axis):
            first, *rest = runs(axis)
            out = [[(0, first, i0, min(4, WS - i0))] for i0 in range(0, WS, 4)]
            col, last = 0, []
            for run in rest:
                last.append((col, run, 0, run[0]))
                col += run[0] * B * run[3]
            return out + [last]

        def evacuate(copy, bank, axis, a):
            for col, (n, base, si, cnt, step), i0, ni in fills(axis)[bank]:
                dst = RHW[:, bass.ds(a + 2 * axis, 1), base + si * i0:base + si * i0 + 1]
                ins = copy(free(dst, [si, ni], [T, B], [step, cnt]),
                           ps[bank][0:HB * WS, col:col + ni * B * cnt].rearrange("p (i b c) -> p i b c", i=ni, b=B))
            return ins

        block = st.block()

        @block.sync
        def _(sp):
            for k, table in enumerate((w["rel_pos_h"], w["rel_pos_w"])):
                for hh in range(HB):
                    sp.dma_start(RT[hh * HD:(hh + 1) * HD, k, :], rows(table, 0, [1, HD], [HD, NJ]), allow_slow_non_contiguous=True).then_inc(t_in, 16)
            sp.dma_start(hm[:, :], consts["headmask"]).then_inc(t_in, 16)
            with images(sp) as i:
                for u in range(2):
                    rp.sync(sp, image_of(G["rd"], i + u, 0, [T, HB * WS], [4 * HB * WS * T, 3], [HB * WS * T, 4], [1, T]), i + u, u)
            rp.finish(sp)

        @block.gpsimd
        def _(pool):
            with images(pool) as i:
                for u in range(2):
                    rp.gpsimd(nc, pool, i + u, u)

        @block.tensor
        def _(pe):
            for c in range(5):
                pe.sem_inc(emptied[c], 1)
            pe.wait_ge(rbd_done, 2)
            with pe.Fori(0, 2) as a:
                for axis in range(2):
                    for bank, fill in enumerate(fills(axis)):
                        pe.wait_ge(emptied[bank], 2 * a + axis + 1)
                        for col, (n, base, si, cnt, step), i0, ni in fill:
                            for k in range(ni):
                                src = QF[:, bass.ds(a, 1), base + si * (i0 + k):base + si * (i0 + k) + 1]
                                mm = nc.tensor.matmul(ps[bank][0:HB * WS, col + k * B * cnt:col + (k + 1) * B * cnt], Rbd[:, axis, i0 + k, :],
                                                      free(src, [T, B], [step, cnt]), start=True, stop=True)
                        mm.then_inc(full[bank], 1)

        @block.scalar
        def _(act):
            rp.init(act)
            with act.Fori(0, 2) as a:
                for axis in range(2):
                    for bank in (0, 2):
                        act.wait_ge(full[bank], 2 * a + axis + 1)
                        evacuate(lambda o, i: nc.scalar.activation(o, i, ACT.Copy), bank, axis, a).then_inc(emptied[bank], 1)
            for bank in range(5):
                act.wait_ge(emptied[bank], 5)
            with images(act) as i:
                for u in range(2):
                    rp.scalar(nc, act, RHW[:, :, bass.ds((i + u) * T, T)], i + u, u)
                for u in range(2):
                    rp.second(nc, act, i + u, u)

        @block.vector
        def _(dve):
            dve.wait_ge(t_in, 16 * (2 * HB + 1))
            for axis in range(2):
                nc.vector.tensor_tensor(Rbd[:, axis].rearrange("p i (h k) -> p i h k", h=HB), free(RT[:, axis, WS - 1:WS], [1, WS], [0, HB], [-1, WS]),
                                        free(hm[:, 0:1], [0, WS], [1, HB], [0, WS]), ALU.mult).then_inc(rbd_done, 1)
            with dve.Fori(0, 2) as a:
                for axis in range(2):
                    for bank in (1, 3, 4):
                        dve.wait_ge(full[bank], 2 * a + axis + 1)
                        evacuate(nc.vector.tensor_copy, bank, axis, a).then_inc(emptied[bank], 1)
            with images(dve) as i:
                for u in range(2):
                    rp.vector(nc, dve, RHW[:, :, bass.ds((i + u) * T, T)], i + u, u)


class Region:

    def __init__(self, q0, qn, qt, k0, kn, pcol):
        self.q0, self.qn, self.qt, self.k0, self.kn, self.pcol = q0, qn, qt, k0, kn, pcol
        self.kt, self.nq = kn // 2, qn * qt


def stack_rows(sp, dst, src, i, blocks, size, sem):
    for t, block in enumerate(blocks):
        o = block * size * NH * T
        base = src[bass.ds(i, 1), o:o + 1]
        sp.dma_start(dst[t * size:(t + 1) * size, :, 0:T],
                     bass.AP(tensor=base.tensor, offset=base.offset, ap=[[T, size], [size * T, NH], [1, T]])).then_inc(sem, 16)


LEAD = 9


def slots_of_pairs(eng, slot):
    for s in range(-LEAD, 0):
        slot(0, s)
    with eng.Fori(0, B // 2 - 1) as pair:
        for s in range(2 * NH):
            if s >= 2 * NH - LEAD:
                slot(pair * 2 + 2, s - 2 * NH)
            slot(pair * 2, s)
    for s in range(2 * NH):
        slot(B - 2, s)


def head_at(s, ahead):
    n = s + ahead
    return divmod(n, NH) if 0 <= n < 2 * NH else None


def group_at(s, ahead):
    n = s + ahead
    return divmod(n // 4, NH // 4) if n % 4 == 0 and 0 <= n < 2 * NH else None


def attention(nc, G, name, w_out, b_out, regions, v_copies, vt, stats_eps, rel=None, setup=None):
    with Stage(nc, name) as st:
        setup = setup and setup(st, G)
        kw = max(r.k0 + r.kn for r in regions)
        QS = [st.sb(f"QS{u}", [SR, NH, T], BF16) for u in range(2)]
        KS = [st.sb(f"KS{u}", [SR, NH, kw], BF16) for u in range(2)]
        RS = [st.sb(f"RS{u}", [SR, NH, T], BF16) for u in range(2)] if rel else None
        KOH = st.sb("KOH", [SR, kw], BF16) if rel else None
        V = [[st.sb(f"V{u}{r}", [R.kt, 2, NH, 32]) for r, R in enumerate(regions)] for u in range(2)]
        Pr = [[st.sb(f"P{b}{r}", [R.qn, R.qt, R.kn]) for r, R in enumerate(regions)] for b in range(2)]
        PT = [[st.sb(f"PT{b}{r}", [R.kt, 2, R.nq]) for r, R in enumerate(regions)] for b in range(2)]
        ncol = sum(R.qt for R in regions)
        nmax = [st.sb(f"nmax{b}", [P, ncol]) for b in range(2)]
        G3 = NH // 4
        sums = st.sb("sums", [P, T])
        inv = st.sb("inv", [P, TI * 4])
        O = st.sb("O", [P, TI, C])
        OT = st.sb("OT", [CH, 2, T])
        Wo = st.sb("Wo", [CH, 2, C])
        stats = LnStats(st, G, stats_eps)
        psS = [[st.ps(f"psS{r}{b}") for b in range(2)] for r in range(len(regions))]
        psT = [st.ps(f"psT{b}") for b in range(2)]
        psO, psG = st.ps("psO"), st.ps("psG")
        s_full, m_done, e_done, t_full, av_done = st.sems("s_full max_done exp_done t_full av_done")
        pt_done = st.sems("ptv_done pta_done")
        o_copied, grouped, inverted, norm_done = st.sems("o_copied grouped inverted norm_done")
        o_turned, o_done, y_full, x_added = st.sems("o_turned o_done y_full x_added")
        stack_in = [st.sem(f"stack_in{u}") for u in range(2)]
        c_in, w_in, v_done, v_init, x_biased, own = st.sems("c_in w_in v_done v_init x_biased own")
        n_stack = (len(Q_TERM) + len(K_TERM) + (6 if rel else 0)) * 16
        block = st.block()

        def scores(b, r, R, t=None):
            if t is None:
                return psS[r][b][0:R.qn, 0:R.qt * R.kn].rearrange("p (t k) -> p t k", t=R.qt)
            return psS[r][b][0:R.qn, t * R.kn:(t + 1) * R.kn]

        def evacuate(eng, copy, i, h):
            n, b = NH * i + h, h % 2
            eng.wait_ge(t_full, n + 3)
            eng.wait_ge(av_done, n + 1)
            for r, R in enumerate(regions):
                cp = copy(PT[b][r][:, :, :], psT[b][0:R.kt, R.pcol:R.pcol + 2 * R.nq].rearrange("p (k q) -> p k q", k=2))
            cp.then_inc(pt_done[b], 1)

        @block.sync
        def _(sp):
            if setup:
                setup.sync(sp)
            if rel:
                for u in range(2):
                    sp.dma_start(RS[u][SR - 12:SR, :, :], rows(G["consts"]["winrows"], 0, [T, 12], [0, NH], [1, T])).then_inc(c_in, 16)
                sp.dma_start(KOH[:, :], G["consts"]["koh"]).then_inc(c_in, 16)
            with images(sp) as i:
                for u in range(2):
                    sp.wait_ge(s_full, NH * (i + u + 1))
                    stack_rows(sp, QS[u], G["qd"], i + u, Q_TERM, HD, stack_in[u])
                    stack_rows(sp, KS[u], G["kd"], i + u, K_TERM, HD, stack_in[u])
                    if rel:
                        stack_rows(sp, RS[u], G["rd"], i + u, range(6), WS, stack_in[u])

        @block.gpsimd
        def _(pool):
            stats.init(pool)
            for u in range(2):
                for r, R in enumerate(regions):
                    nc.gpsimd.memset(V[u][r][:, :, :, HD:], 0.0).then_inc(own, 1)
            n = 2 * len(regions)
            pool.wait_ge(own, n)
            for u in range(2):
                for r, R in enumerate(regions):
                    nc.gpsimd.memset(V[u][r][:, :, :, HD:HD + 1], 1.0).then_inc(v_init, 1)
                    if r:
                        for k in range(2):
                            nc.gpsimd.tensor_copy(V[u][r][:, k, :, 0:HD], G["vb"][0:R.kt, :].rearrange("p (h d) -> p h d", h=NH)).then_inc(own, 1)
                            n += 1
            pool.wait_ge(own, n)

            def values(i, u):
                wait_all(pool, G["steady"], (norm_done, G3 * i + 1))
                for r, k0, nk, prt, t0 in v_copies:
                    for k in range(nk):
                        cp = nc.gpsimd.tensor_copy(V[u][r][0:prt, k0 + k, :, 0:HD],
                                                   G["Vall"][0:prt, bass.ds(i * vt + t0 + k, 1), :].rearrange("p a (h d) -> p (a h) d", h=NH))
                cp.then_inc(v_done, 1)

            def finish(i, last):
                for u in range(2):
                    if not last:
                        values(i + u + 2, u)
                    stats.gpsimd(nc, pool, i + u, u)

            for u in range(2):
                values(u, u)
            if b_out is not None:
                nc.gpsimd.tensor_tensor(G["X"][:, :, :], G["X"][:, :, :], free(b_out[:, 0:1], [0, NT], [1, C]), ALU.add).then_inc(x_biased, 1)
            with pool.Fori(0, B // 2 - 1) as pair:
                finish(pair * 2, False)
            finish(B - 2, True)

        @block.tensor
        def _(pe):
            for s, k in ((e_done, 2), (pt_done[0], 1), (pt_done[1], 1), (t_full, 2), (av_done, 2), (s_full, 2 * NH),
                         (o_copied, 1), (grouped, 1), (norm_done, 4), (o_turned, 1), (o_done, 1), (y_full, 1), (x_added, 1)):
                pe.sem_inc(s, k)
            if rel:
                pe.wait_ge(c_in, 16 * 3)
            pe.wait_ge(v_init, 2 * len(regions) + (2 if rel else 0))

            def score(i, u, h):
                n, b = NH * i + h, h % 2
                pe.wait_ge(e_done, n + 1)
                for r, R in enumerate(regions):
                    for t in range(R.qt):
                        q = slice(R.q0 + t * R.qn, R.q0 + (t + 1) * R.qn)
                        mm = nc.tensor.matmul(scores(b, r, R, t), QS[u][:, h, q], KS[u][:, h, R.k0:R.k0 + R.kn], start=True, stop=not rel)
                        if rel:
                            mm = nc.tensor.matmul(scores(b, r, R, t), RS[u][:, h, q], KOH[:, R.k0:R.k0 + R.kn], start=False, stop=True)
                mm.then_inc(s_full, 1)

            def turn(i, h):
                n, b = NH * i + h, h % 2
                pe.wait_ge(e_done, n + 3)
                pe.wait_ge(pt_done[b], NH // 2 * i + h // 2 + 1)
                if h == 6:
                    pe.wait_ge(o_done, i + 1)
                if h == 7:
                    pe.wait_ge(x_added, i + 1)
                for r, R in enumerate(regions):
                    for k in range(2):
                        for t in range(R.qt):
                            col = R.pcol + k * R.nq + t * R.qn
                            mm = nc.tensor.transpose(psT[b][0:R.kt, col:col + R.qn], Pr[b][r][:, t, k * R.kt:(k + 1) * R.kt], G["ident"][0:R.qn, 0:R.qn])
                mm.then_inc(t_full, 1)

            def av(i, u, h):
                n, b, g, s = NH * i + h, h % 2, h // 4, h % 4
                if h == 0:
                    pe.wait_ge(v_done, i + 1)
                pe.wait_ge(pt_done[b], NH // 2 * i + h // 2 + 2)
                if s == 0:
                    pe.wait_ge(o_copied, G3 * i + g + 1)
                for r, R in enumerate(regions):
                    o = psO[32 * s:32 * s + 32, R.q0:R.q0 + R.nq]
                    for k in range(2):
                        mm = nc.tensor.matmul(o, V[u][r][:, k, h, :], PT[b][r][:, k, :], start=(k == 0), stop=(k == 1), skip_group_check=True)
                mm.then_inc(av_done, 1)

            def turn_group(i, g):
                pe.wait_ge(o_copied, G3 * i + g + 2)
                pe.wait_ge(norm_done, G3 * i + g + 4)
                for t in range(TI):
                    mm = nc.tensor.transpose(psG[:, t * P:(t + 1) * P], sums[:, t * P:(t + 1) * P], G["ident"][:, :])
                mm.then_inc(grouped, 1)

            def turn_out(i, last):
                pe.wait_ge(norm_done, G3 * i + G3 + 4)
                pe.wait_ge(pt_done[0], NH // 2 * (i + 1) + (1 if last else 4))
                for t in range(TI):
                    for a in range(2):
                        mm = nc.tensor.transpose(psT[0][0:CH, a * T + t * P:a * T + (t + 1) * P], O[:, t, a * CH:(a + 1) * CH], G["ident"][:, :])
                mm.then_inc(o_turned, 1)

            def project(i, last):
                pe.wait_ge(w_in, 16)
                pe.wait_ge(o_done, i + 2)
                pe.wait_ge(pt_done[1], NH // 2 * (i + 1) + (1 if last else 4))
                for t in range(TI):
                    for a in range(2):
                        mm = nc.tensor.matmul(psT[1][:, t * C:(t + 1) * C], OT[:, a, t * P:(t + 1) * P], Wo[:, a, :], start=(a == 0), stop=(a == 1))
                mm.then_inc(y_full, 1)

            def slot(i, s):
                if at := head_at(s, LEAD):
                    u, h = at
                    if h == 0:
                        pe.wait_ge(stack_in[u], (n_stack // 2) * i + n_stack)
                    score(i + u, u, h)
                if at := head_at(s, LEAD - 2):
                    turn(i + at[0], at[1])
                if at := head_at(s, LEAD - 3):
                    u, h = at
                    av(i + u, u, h)
                if at := group_at(s, 1):
                    turn_group(i + at[0], at[1])
                last = isinstance(i, int) and i == B - 2 and s >= NH
                if s in (10, NH + 10):
                    turn_out(i + s // NH, last)
                if s in (11, NH + 11):
                    project(i + s // NH, last)

            slots_of_pairs(pe, slot)

        @block.scalar
        def _(act):
            act.dma_start(Wo[:, :, :], w_out.rearrange("(a p) n -> p a n", p=CH)).then_inc(w_in, 16)

            def exps(i, h):
                n, b, c = NH * i + h, h % 2, 0
                act.wait_ge(m_done, n + 1)
                act.wait_ge(t_full, n + 1)
                for r, R in enumerate(regions):
                    for t in range(R.qt):
                        ex = nc.scalar.activation(Pr[b][r][:, t, :], scores(b, r, R, t), ACT.Exp, bias=nmax[b][0:R.qn, c:c + 1])
                        c += 1
                ex.then_inc(e_done, 1)

            def copy_out(i, g):
                act.wait_ge(av_done, NH * i + 4 * g + 6)
                act.wait_ge(grouped, G3 * i + g + 1)
                nc.scalar.activation(sums[:, :], psO[:, 0:T], ACT.Copy).then_inc(o_copied, 1)

            def evacuate_out(i):
                act.wait_ge(o_turned, i + 2)
                act.wait_ge(y_full, i + 1)
                nc.scalar.activation(OT[:, :, :], psT[0][0:CH, :].rearrange("p (a n) -> p a n", a=2), ACT.Copy).then_inc(o_done, 1)

            def slot(i, s):
                if at := group_at(s, 2):
                    copy_out(i + at[0], at[1])
                if at := head_at(s, LEAD):
                    exps(i + at[0], at[1])
                if (at := head_at(s, LEAD - 2)) and at[1] % 2:
                    evacuate(act, lambda o, x: nc.scalar.activation(o, x, ACT.Copy), i + at[0], at[1])
                if s in (10, NH + 10):
                    evacuate_out(i + s // NH)

            slots_of_pairs(act, slot)

        @block.vector
        def _(dve):
            if setup:
                setup.vector(nc, dve, KS, v_init)

            def maxima(i, h):
                n, b, c = NH * i + h, h % 2, 0
                dve.wait_ge(s_full, n + 1 + 2 * NH)
                for r, R in enumerate(regions):
                    mx = nc.vector.tensor_reduce(nmax[b][0:R.qn, c:c + R.qt], scores(b, r, R), AX.X, ALU.max, negate=True)
                    c += R.qt
                mx.then_inc(m_done, 1)

            def normalise(i, g):
                dve.wait_ge(grouped, G3 * i + g + 2)
                if g == 0:
                    dve.wait_ge(o_turned, i + 1)
                of_heads = psG[:, 0:T].rearrange("p (h d) -> p h d", d=32)
                nc.vector.reciprocal(inv[:, :], of_heads[:, :, HD]).then_inc(inverted, 1)
                dve.wait_ge(inverted, G3 * i + g + 1)
                nc.vector.tensor_tensor(O[:, :, 4 * g * HD:4 * (g + 1) * HD].rearrange("p t (h d) -> p t h d", h=4),
                                        of_heads[:, :, 0:HD].rearrange("p (t h) d -> p t h d", t=TI),
                                        free(inv[:, 0:1], [4, TI], [1, 4], [0, HD]), ALU.mult).then_inc(norm_done, 1)

            def residual(i, u):
                dve.wait_ge(y_full, i + 2)
                X = G["X"][:, bass.ds(TI * i, TI), :]
                nc.vector.tensor_tensor(X, psT[1][:, 0:TI * C].rearrange("p (t c) -> p t c", t=TI), X, ALU.add).then_inc(x_added, 1)
                stats.vector(nc, dve, i, u, (x_added, i + 2))

            def slot(i, s):
                if at := head_at(s, LEAD):
                    maxima(i + at[0], at[1])
                if (at := head_at(s, LEAD - 2)) and at[1] % 2 == 0:
                    evacuate(dve, nc.vector.tensor_copy, i + at[0], at[1])
                if at := group_at(s, 0):
                    normalise(i + at[0], at[1])
                if s in (11, NH + 11):
                    residual(i + s // NH, s // NH)

            if b_out is not None:
                dve.wait_ge(x_biased, 1)
            slots_of_pairs(dve, slot)


L0_REGIONS = (Region(0, WQ, 2, 0, W0, 0), Region(W0, EXT, 1, W0, EK, 2 * W0))
L3_REGIONS = (Region(0, P, 2, 0, T, 0),)


def l0_attention(nc, G, w):
    attention(nc, G, "l0a", w["proj_w"], G["pb"], L0_REGIONS, ((0, 0, 2, WQ, 0), (1, 0, 1, EXT, 2)), 3, 1e-6, rel=True,
              setup=PaddingKeys)


class PaddingKeys:

    def __init__(self, st, G):
        self.G = G
        self.kb = st.sb("kb", [SR, NH], BF16)
        self.kb_in = st.sem("kb_in")

    def sync(self, sp):
        for t, piece in enumerate(K_TERM):
            sp.dma_start(self.kb[t * HD:(t + 1) * HD, :], rows(self.G["kbd"], piece * C, [1, HD], [HD, NH]),
                         allow_slow_non_contiguous=True).then_inc(self.kb_in, 16)

    def vector(self, nc, dve, KS, done):
        dve.wait_ge(self.kb_in, 16 * len(K_TERM))
        for u in range(2):
            nc.vector.tensor_copy(KS[u][:, :, T:], free(self.kb[:, 0:1], [1, NH], [0, PADS])).then_inc(done, 1)



def l0_mlp(nc, G, w):
    with Stage(nc, "l0m") as st:
        wn, bn = st.sb("wn", [CH, 2]), st.sb("bn", [CH, 2])
        W1, b1 = st.sb("W1", [CH, 2, FF]), st.sb("b1", [P, MF])
        W2, b2 = st.sb("W2", [P, MF, C]), st.sb("b2", [P, C])
        hT = [st.sb(f"hT{u}", [P, MF, T]) for u in range(2)]
        nm = Normed(st, G, (wn, bn))
        psH = [st.ps(f"psH{k}") for k in range(MF // 2)]
        psY = [st.ps(f"psY{u}") for u in range(2)]
        c_in, h_mm, h_done, y_full, x_added, x_biased = st.sems("c_in h_mm h_done y_full x_added x_biased")
        xw_out, permuted, x_in = st.sems("xw_out permuted x_in")
        xw, xr = G["xw"], G["xr"]
        block = st.block()

        @block.sync
        def _(sp):
            sp.dma_start(wn[:, :], w["norm2_w"].rearrange("(k p) -> p k", p=CH), allow_slow_non_contiguous=True).then_inc(c_in, 16)
            sp.dma_start(bn[:, :], w["norm2_b"].rearrange("(k p) -> p k", p=CH), allow_slow_non_contiguous=True).then_inc(c_in, 16)
            sp.dma_start(W1[:, :, :], w["fc1_w"].rearrange("(k p) n -> p k n", p=CH)).then_inc(c_in, 16)
            sp.dma_start(b1[:, :], w["fc1_b"].rearrange("(m p) -> p m", p=P), allow_slow_non_contiguous=True).then_inc(c_in, 16)
            sp.dma_start(W2[:, :, :], w["fc2_w"].rearrange("(m p) n -> p m n", p=P)).then_inc(c_in, 16)
            sp.dma_start(b2[:, :], rows(w["fc2_b"], 0, [0, P], [1, C])).then_inc(c_in, 16)
            with images(sp) as pair:
                for u in range(2):
                    i = pair + u
                    X = G["X"][:, bass.ds(TI * i, TI), :]
                    sp.wait_ge(x_added, i + 2 + 1)
                    sp.dma_start(image_of(xw.rearrange("(b n) c -> b (n c)", b=B), i, 0, [C, P], [P * C, TI], [1, C]), X).then_inc(xw_out, 16)
                    sp.wait_ge(xw_out, 16 * i + 16)
                    for r0, c0, h, wd, n0 in WINDOWS:
                        o = (r0 * WW + c0) * C
                        dst = xr.rearrange("(b n) c -> b (n c)", b=B)[bass.ds(i, 1), o:o + 1]
                        src = xw.rearrange("(b n) c -> b (n c)", b=B)[bass.ds(i, 1), n0 * C:n0 * C + 1]
                        sp.dma_start(bass.AP(tensor=dst.tensor, offset=dst.offset, ap=[[WW * C, h], [1, wd * C]]),
                                     bass.AP(tensor=src.tensor, offset=src.offset, ap=[[wd * C, h], [1, wd * C]])).then_inc(permuted, 16)
                    sp.wait_ge(permuted, 16 * len(WINDOWS) * (i + 1))
                    sp.dma_start(X, image_of(xr.rearrange("(b n) c -> b (n c)", b=B), i, 0, [C, P], [P * C, TI], [1, C])).then_inc(x_in, 16)
                    wait_all(sp, G["steady"], (x_in, 16 * i + 16))

        @block.gpsimd
        def _(pool):
            pool.wait_ge(c_in, 16 * 6)
            with images(pool) as pair:
                for u in range(2):
                    i = pair + u
                    pool.wait_ge(nm.normed, TI * (i + 1))
                    X = G["X"][:, bass.ds(TI * i, TI), :]
                    nc.gpsimd.tensor_tensor(X, X, free(b2[:, 0:1], [0, TI], [1, C]), ALU.add).then_inc(x_biased, 1)

        @block.tensor
        def _(pe):
            nm.init_credit(pe)
            for s, k in ((h_done, MF // 2), (x_added, 2)):
                pe.sem_inc(s, k)
            pe.wait_ge(c_in, 16 * 6)
            with images(pe) as pair:
                for u in range(2):
                    nm.tensor(nc, pe, pair + u, u)
                for u in range(2):
                    i = pair + u
                    pe.wait_ge(nm.xT_done, i + 3)
                    for k2 in range(MF // 2):
                        pe.wait_ge(h_done, MF // 2 * i + k2 + 1)
                        for m in (2 * k2, 2 * k2 + 1):
                            for k in range(2):
                                mm = nc.tensor.matmul(psH[k2][:, m % 2 * T:(m % 2 + 1) * T], W1[:, k, m * P:(m + 1) * P], nm.xT[u][:, k, :],
                                                      start=(k == 0), stop=(k == 1))
                        mm.then_inc(h_mm if k2 < MF // 2 - 1 else nm.xT_free, 1)
                for u in range(2):
                    i = pair + u
                    pe.wait_ge(h_done, MF // 2 * (i + 2))
                    pe.wait_ge(x_added, i + 1)
                    for t in range(TI):
                        for m in range(MF):
                            mm = nc.tensor.matmul(psY[u][:, t * C:(t + 1) * C], hT[u][:, m, t * P:(t + 1) * P], W2[:, m, :], start=(m == 0), stop=(m == MF - 1))
                    mm.then_inc(y_full, 1)

        @block.scalar
        def _(act):
            act.sem_inc(y_full, 2)
            act.wait_ge(c_in, 16 * 6)
            with images(act) as pair:
                for u in range(2):
                    nm.scalar(nc, act, pair + u, u)
                for u in range(2):
                    i = pair + u
                    act.wait_ge(y_full, i + 1)
                    for k2 in range(MF // 2):
                        if k2 < MF // 2 - 1:
                            act.wait_ge(h_mm, (MF // 2 - 1) * i + k2 + 1)
                        else:
                            act.wait_ge(nm.xT_free, i + 3)
                        for m in (2 * k2, 2 * k2 + 1):
                            ge = nc.scalar.activation(hT[u][:, m, :], psH[k2][:, m % 2 * T:(m % 2 + 1) * T], ACT.Gelu, bias=b1[:, m:m + 1])
                        ge.then_inc(h_done, 1)

        @block.vector
        def _(dve):
            with images(dve) as pair:
                for u in range(2):
                    nm.vector(nc, dve, pair + u, u)
                for u in range(2):
                    i = pair + u
                    dve.wait_ge(y_full, i + 3)
                    dve.wait_ge(x_biased, i + 1)
                    X = G["X"][:, bass.ds(TI * i, TI), :]
                    nc.vector.tensor_tensor(X, psY[u][:, 0:TI * C].rearrange("p (t c) -> p t c", t=TI), X, ALU.add).then_inc(x_added, 1)


NB, BS, LAMBDA = 8, 24, 0.01
WF = WW // 2 + 1
NF = HH * WF
F1 = NF - SR
GROUPS, GC = 32, C // 32


def l1_afno(nc, G, w, consts):
    with Stage(nc, "l1") as st:
        ones = st.sb("ones", [P, P])
        DF = st.sb("DF", [P, TI, 2 * NF])
        IV = st.sb("IV", [SR, 2, 2, T])
        W1 = st.sb("W1", [CH, 2, 2, CH])
        W2 = st.sb("W2", [CH, 2, 3, CH])
        b1, b2 = st.sb("b1", [CH, 2, 2]), st.sb("b2", [SR, 2, 2, CH])
        w2n = st.sb("w2n", [CH, 2, CH])
        half = st.sb("half", [P, GROUPS])
        two = lambda name, shape: [st.sb(f"{name}{u}", shape) for u in range(2)]
        mean, var, rstd = two("mean", [P, GROUPS]), two("var", [P, GROUPS]), two("rstd", [P, GROUPS])
        XC, SQ, XN, XS = two("XC", [P, TI, C]), two("SQ", [P, TI, C]), two("XN", [P, TI, C]), two("XS", [P, TI, C])
        FX, Z1, C1 = two("FX", [CH, 2, 3 * NF]), two("Z1", [CH, 2, 2 * NF]), two("C1", [CH, 2, 2 * NF])
        Z2, C2 = two("Z2", [SR, 2, 2, 2, CH]), two("C2", [SR, 2, 2, 2, CH])
        stats = LnStats(st, G, 1e-5)
        psA = [st.ps(f"psA{u}") for u in range(2)]
        psB = [[st.ps(f"psB{u}{a}") for a in range(2)] for u in range(2)]
        c_in, zeroed, mean_mm, mean_done, xc_done, sq_done, var_mm, var_done, eps_done, rstd_done, xn_done, xs_done = st.sems(
            "c_in zeroed mean_mm mean_done xc_done sq_done var_mm var_done eps_done rstd_done xn_done xs_done")
        f_mm, f_done, z1_mm, z1_done, c1_done, o1_done, z2_mm, z2_done, c2_done, o2_done, y_mm, x_done = st.sems(
            "f_mm f_done z1_mm z1_done c1_done o1_done z2_mm z2_done c2_done o2_done y_mm x_done")
        block = st.block()
        N_IN = 16 * (4 + 4 * 8 + 2 + 4)

        @block.sync
        def _(sp):
            for dst, src in ((ones, "gnones"), (DF, "dft"), (IV, "idft")):
                sp.dma_start(dst[:], consts[src]).then_inc(c_in, 16)
            sp.dma_start(half[:, :], consts["minushalf"]).then_inc(c_in, 16)
            sp.wait_ge(zeroed, 2)
            for n in range(NB):
                a, k = n // 4, n % 4
                r = slice(k * BS, (k + 1) * BS)
                for part in range(2):
                    sp.dma_start(W1[r, part, a, r], w["w1"][part, n]).then_inc(c_in, 16)
                    sp.dma_start(W2[r, a, 1 + part, r], w["w2"][part, n]).then_inc(c_in, 16)
            for part in range(2):
                sp.dma_start(b1[:, part, :], rows(w["b1"], part * C, [1, CH], [CH, 2]), allow_slow_non_contiguous=True).then_inc(c_in, 16)
                for a in range(2):
                    sp.dma_start(b2[:, a, part, :], rows(w["b2"], part * C + a * CH, [0, SR], [1, CH])).then_inc(c_in, 16)

        @block.gpsimd
        def _(pool):
            nc.gpsimd.memset(W1[:], 0.0).then_inc(zeroed, 1)
            nc.gpsimd.memset(W2[:], 0.0).then_inc(zeroed, 1)
            stats.init(pool)
            pool.wait_ge(c_in, N_IN)
            pool.sem_inc(rstd_done, 2)
            with images(pool) as pair:
                for u in range(2):
                    i = pair + u
                    wait_all(pool, G["steady"], (var_done, i + 1))
                    nc.gpsimd.tensor_scalar(var[u][:, :], var[u][:, :], 1e-5, None, ALU.add).then_inc(eps_done, 1)
                    pool.wait_ge(eps_done, i + 1)
                    nc.gpsimd.tensor_tensor(rstd[u][:, :], var[u][:, :], half[:, :], ALU.pow).then_inc(rstd_done, 1)
                for u in range(2):
                    i = pair + u
                    pool.wait_ge(xn_done, i + 1)
                    pool.wait_ge(x_done, i + 1)
                    nc.gpsimd.tensor_tensor(XS[u][:], G["X"][:, bass.ds(TI * i, TI), :], XN[u][:], ALU.add).then_inc(xs_done, 1)
                for u in range(2):
                    i = pair + u
                    pool.wait_ge(c1_done, i + 1)
                    nc.gpsimd.tensor_tensor(C1[u][:], Z1[u][:], C1[u][:], ALU.subtract).then_inc(o1_done, 1)
                for u in range(2):
                    i = pair + u
                    pool.wait_ge(c2_done, i + 1)
                    nc.gpsimd.tensor_tensor(C2[u][:], Z2[u][:], C2[u][:], ALU.subtract).then_inc(o2_done, 1)
                for u in range(2):
                    stats.gpsimd(nc, pool, pair + u, u)

        @block.tensor
        def _(pe):
            pe.sem_inc(x_done, 2)
            pe.sem_inc(y_mm, 2)
            pe.wait_ge(c_in, N_IN)
            pe.wait_ge(zeroed, 3)
            with images(pe) as pair:
                for u in range(2):
                    i = pair + u
                    pe.wait_ge(x_done, i + 1)
                    for t in range(TI):
                        mm = nc.tensor.matmul(psA[u][:, 0:C], ones[:, :], G["X"][:, bass.ds(TI * i + t, 1), :].rearrange("p a c -> p (a c)"), start=(t == 0), stop=(t == 1))
                    mm.then_inc(mean_mm, 1)
                for u in range(2):
                    i = pair + u
                    pe.wait_ge(sq_done, i + 1)
                    for t in range(TI):
                        mm = nc.tensor.matmul(psA[u][:, 0:C], ones[:, :], SQ[u][:, t, :], start=(t == 0), stop=(t == 1))
                    mm.then_inc(var_mm, 1)
                for u in range(2):
                    i = pair + u
                    pe.wait_ge(xn_done, i + 1)
                    for a in range(2):
                        for t in range(TI):
                            mm = nc.tensor.matmul(psB[u][a][0:CH, 0:2 * NF], XN[u][:, t, a * CH:(a + 1) * CH], DF[:, t, :], start=(t == 0), stop=(t == 1))
                    mm.then_inc(f_mm, 1)
                for u in range(2):
                    i = pair + u
                    pe.wait_ge(f_done, i + 1)
                    for a in range(2):
                        nc.tensor.matmul(psB[u][a][0:CH, 0:2 * NF], W1[:, 0, a, :], FX[u][:, a, NF:3 * NF], start=True, stop=False)
                        mm = nc.tensor.matmul(psB[u][a][0:CH, 0:2 * NF], W1[:, 1, a, :], FX[u][:, a, 0:2 * NF], start=False, stop=True)
                    mm.then_inc(z1_mm, 1)
                for u in range(2):
                    i = pair + u
                    pe.wait_ge(o1_done, i + 1)
                    for f in range(2):
                        f0 = f * F1
                        for a in range(2):
                            o = psB[u][f][0:SR, 2 * a * CH:2 * (a + 1) * CH]
                            nc.tensor.matmul(o, C1[u][:, a, f0:f0 + SR], W2[:, a, 1:3, :].rearrange("p k c -> p (k c)"), start=True, stop=False)
                            mm = nc.tensor.matmul(o, C1[u][:, a, NF + f0:NF + f0 + SR], W2[:, a, 0:2, :].rearrange("p k c -> p (k c)"), start=False, stop=True)
                    mm.then_inc(z2_mm, 1)
                for u in range(2):
                    i = pair + u
                    pe.wait_ge(o2_done, i + 1)
                    for t in range(TI):
                        for f in range(2):
                            for part in range(2):
                                mm = nc.tensor.matmul(psA[u][:, t * C:(t + 1) * C], IV[:, f, part, t * P:(t + 1) * P], C2[u][:, f, :, part, :],
                                                      start=(f == 0 and part == 0), stop=(f == 1 and part == 1))
                    mm.then_inc(y_mm, 1)

        @block.scalar
        def _(act):
            act.wait_ge(c_in, N_IN)
            nc.scalar.activation(W2[:, :, 0, :], W2[:, :, 2, :], ACT.Copy, scale=-1.0).then_inc(zeroed, 1)
            with images(act) as pair:
                for u in range(2):
                    i = pair + u
                    act.wait_ge(xc_done, i + 1)
                    nc.scalar.activation(SQ[u][:], XC[u][:], ACT.Square).then_inc(sq_done, 1)
                for u in range(2):
                    i = pair + u
                    act.wait_ge(f_mm, i + 1)
                    for a in range(2):
                        nc.scalar.activation(FX[u][:, a, NF:3 * NF], psB[u][a][0:CH, 0:2 * NF], ACT.Copy)
                        ev = nc.scalar.activation(FX[u][:, a, 0:NF], psB[u][a][0:CH, NF:2 * NF], ACT.Copy, scale=-1.0)
                    ev.then_inc(f_done, 1)
                for u in range(2):
                    i = pair + u
                    act.wait_ge(z1_mm, i + 1)
                    for a in range(2):
                        for part in range(2):
                            ev = nc.scalar.activation(Z1[u][:, a, part * NF:(part + 1) * NF], psB[u][a][0:CH, part * NF:(part + 1) * NF], ACT.Identity, bias=b1[:, part, a:a + 1])
                    ev.then_inc(z1_done, 1)

        @block.vector
        def _(dve):
            per_group = lambda ap: ap.rearrange("p (g c) -> p g c", g=GROUPS)
            dve.wait_ge(c_in, N_IN)
            with images(dve) as pair:
                for u in range(2):
                    i = pair + u
                    dve.wait_ge(mean_mm, i + 1)
                    nc.vector.tensor_reduce(mean[u][:, :], per_group(psA[u][:, 0:C]), AX.X, ALU.add).then_inc(mean_done, 1)
                    dve.wait_ge(mean_done, i + 1)
                    for t in range(TI):
                        ins = nc.vector.tensor_tensor(per_group(XC[u][:, t, :]), per_group(G["X"][:, bass.ds(TI * i + t, 1), :].rearrange("p a c -> p (a c)")),
                                                      free(mean[u][:, 0:1], [1, GROUPS], [0, GC]), ALU.subtract)
                    ins.then_inc(xc_done, 1)
                for u in range(2):
                    i = pair + u
                    dve.wait_ge(var_mm, i + 1)
                    nc.vector.tensor_reduce(var[u][:, :], per_group(psA[u][:, 0:C]), AX.X, ALU.add).then_inc(var_done, 1)
                for u in range(2):
                    i = pair + u
                    dve.wait_ge(rstd_done, i + 3)
                    for t in range(TI):
                        ins = nc.vector.tensor_tensor(per_group(XN[u][:, t, :]), per_group(XC[u][:, t, :]), free(rstd[u][:, 0:1], [1, GROUPS], [0, GC]), ALU.mult)
                    ins.then_inc(xn_done, 1)
                for u in range(2):
                    i = pair + u
                    dve.wait_ge(z1_done, i + 1)
                    nc.vector.tensor_scalar(C1[u][:], Z1[u][:], -LAMBDA, LAMBDA, ALU.max, ALU.min).then_inc(c1_done, 1)
                for u in range(2):
                    i = pair + u
                    dve.wait_ge(z2_mm, i + 1)
                    for f in range(2):
                        ins = nc.vector.tensor_tensor(Z2[u][:, f], psB[u][f][0:SR, 0:4 * CH].rearrange("p (a k c) -> p a k c", a=2, k=2), b2[:], ALU.add)
                    ins.then_inc(z2_done, 1)
                    dve.wait_ge(z2_done, i + 1)
                    nc.vector.tensor_scalar(C2[u][:], Z2[u][:], -LAMBDA, LAMBDA, ALU.max, ALU.min).then_inc(c2_done, 1)
                for u in range(2):
                    i = pair + u
                    dve.wait_ge(y_mm, i + 3)
                    dve.wait_ge(xs_done, i + 1)
                    nc.vector.tensor_tensor(G["X"][:, bass.ds(TI * i, TI), :], psA[u][:, 0:TI * C].rearrange("p (t c) -> p t c", t=TI), XS[u][:], ALU.add).then_inc(x_done, 1)
                    stats.vector(nc, dve, i, u, (x_done, i + 3))



LM = 16
SEG = T // LM
NG = 2 * B


def l2_features(nc, G, w, consts):
    with Stage(nc, "l2p") as st:
        W, qkb = st.sb("W", [CH, 2, 3 * C]), st.sb("qkb", [CH, 4])
        vb, hm = st.sb("vb", [P, C]), st.sb("hm", [CH, HB])
        hms = st.sb("hms", [CH, HB])
        toep = st.sb("toep", [P, NH, TW])
        two = lambda name, shape: [st.sb(f"{name}{u}", shape) for u in range(2)]
        QT, KT, VZ = two("QT", [CH, 2, T]), two("KT", [CH, 2, T]), two("VZ", [P, TI, NH, 2 * HD])
        sums, kl = two("sums", [CH, 2, 2, LM]), two("kl", [CH, 2, LM])
        qlbd, klbd = two("qlbd", [CH, 2, HB, LM]), two("klbd", [CH, 2, HB, LM])
        A1, m1, d1, r1 = two("A1", [P, TI * NH, LM]), two("m1", [P, TI * NH]), two("d1", [P, TI * NH]), two("r1", [P, TI * NH])
        A3, A3T, m3, d3, r3 = two("A3", [CH, 2, T]), two("A3T", [P, TI, 2, CH]), two("m3", [CH, 2]), two("d3", [CH, 2]), two("r3", [CH, 2])
        nm = Normed(st, G)
        psQ, psK, psV, ps1, ps3, psC = (st.ps(n) for n in ("psQ", "psK", "psV", "ps1", "ps3", "psC"))
        c_in, cleared, ms_done = st.sems("c_in cleared ms_done")
        q_mm, q_done, k_mm, k_done, v_done, sum_done, lm_done = st.sems("q_mm q_done k_mm k_done v_done sum_done lm_done")
        l1_mm, m1_done, z1_done, e1_done, d1_done, r1_done, p1_done = st.sems("l1_mm m1_done z1_done e1_done d1_done r1_done p1_done")
        l3_mm, m3_done, e3_done, r3_done, t3_mm, t3_done, k3_mm, k3_done = st.sems("l3_mm m3_done e3_done r3_done t3_mm t3_done k3_mm k3_done")
        t1_mm, t1_done, c_mm, cv_done, k2_mm, k2_done, tp_in = st.sems("t1_mm t1_done c_mm cv_done k2_mm k2_done tp_in")
        K1T, CV, K3, K2L = G["K1T"], G["CV"], G["K3"], G["K2L"]
        block = st.block()

        @block.sync
        def _(sp):
            sp.dma_start(W[:, :, :], w["Wqkv"].rearrange("(k p) n -> p k n", p=CH)).then_inc(c_in, 16)
            sp.dma_start(qkb[:, :], rows(w["bqkv"], 0, [1, CH], [CH, 4]), allow_slow_non_contiguous=True).then_inc(c_in, 16)
            sp.dma_start(vb[:, :], rows(w["bqkv"], 2 * C, [0, P], [1, C])).then_inc(c_in, 16)
            sp.dma_start(hm[:, :], consts["headmask"]).then_inc(c_in, 16)
            sp.dma_start(toep[:, :, :], rows(G["band"], 0, [TW, P], [P * TW, NH], [1, TW])).then_inc(tp_in, 16)

        @block.gpsimd
        def _(pool):
            for u in range(2):
                nc.gpsimd.memset(VZ[u][:], 0.0).then_inc(cleared, 1)
            with images(pool) as pair:
                for u in range(2):
                    i = pair + u
                    pool.wait_ge(r1_done, i + 1)
                    nc.gpsimd.tensor_tensor(A1[u][:], A1[u][:], free(r1[u][:, 0:1], [1, TI * NH], [0, LM]), ALU.mult).then_inc(p1_done, 1)

        @block.tensor
        def _(pe):
            nm.init_credit(pe)
            for s in (q_done, k_done, v_done, k3_done, cv_done):
                pe.sem_inc(s, 1)
            pe.sem_inc(k3_done, 1)
            pe.wait_ge(c_in, 64)
            pe.wait_ge(tp_in, 16)
            reach = ((0, 0, P + KS // 2), (1, P - KS // 2, T))
            ident = G["ident"]
            with images(pe) as pair:
                for u in range(2):
                    nm.tensor(nc, pe, pair + u, u)
                for u in range(2):
                    i = pair + u
                    pe.wait_ge(nm.xT_done, i + 3)
                    for ps, m0, done, mm_done in ((psQ, 0, q_done, q_mm), (psK, 2, k_done, k_mm)):
                        pe.wait_ge(done, i + 1)
                        for a in range(2):
                            for k in range(2):
                                mm = nc.tensor.matmul(ps[0:CH, a * T:(a + 1) * T], W[:, k, (m0 + a) * CH:(m0 + a + 1) * CH], nm.xT[u][:, k, :], start=(k == 0), stop=(k == 1))
                        mm.then_inc(mm_done, 1)
                    pe.wait_ge(v_done, i + 1)
                    for t in range(TI):
                        for k in range(2):
                            mm = nc.tensor.matmul(psV[:, t * C:(t + 1) * C], nm.xT[u][:, k, t * P:(t + 1) * P], W[:, k, 2 * C:], start=(k == 0), stop=(k == 1))
                    mm.then_inc(nm.xT_free, 1)
                for u in range(2):
                    i = pair + u
                    pe.wait_ge(lm_done, 3 * i + 3)
                    pe.wait_ge(q_done, i + 2)
                    pe.wait_ge(k_done, i + 2)
                    pe.wait_ge(ms_done, i + 1)
                    for t in range(TI):
                        for a in range(2):
                            mm = nc.tensor.matmul(ps1[:, t * C + a * CH:t * C + (a + 1) * CH], QT[u][:, a, t * P:(t + 1) * P], klbd[u][:, a].rearrange("p h m -> p (h m)"), start=True, stop=True)
                    mm.then_inc(l1_mm, 1)
                    pe.wait_ge(k3_done, i + 2)
                    for a in range(2):
                        mm = nc.tensor.matmul(ps3[0:CH, a * T:(a + 1) * T], qlbd[u][:, a].rearrange("p h m -> p (h m)"), KT[u][:, a, :], start=True, stop=True)
                    mm.then_inc(l3_mm, 1)
                    pe.wait_ge(v_done, i + 2)
                    pe.wait_ge(cv_done, i + 1)
                    for a in range(2):
                        for s in range(3):
                            for hh in range(2):
                                h = a * HB + 2 * s + hh
                                for t, n0, n1 in reach:
                                    mm = nc.tensor.matmul(psC[32 * s:32 * s + 32, a * T + n0:a * T + n1], VZ[u][:, t, h, :],
                                                          toep[:, h, n0 - t * P + KS // 2:n1 - t * P + KS // 2],
                                                          start=(hh == 0 and t == 0), stop=(hh == 1), skip_group_check=True)
                    mm.then_inc(c_mm, 1)
                    pe.wait_ge(e3_done, i + 1)
                    for t in range(TI):
                        for a in range(2):
                            mm = nc.tensor.transpose(ps3[:, (2 * t + a) * CH:(2 * t + a + 1) * CH], A3[u][:, a, t * P:(t + 1) * P], ident[0:CH, 0:CH])
                    mm.then_inc(t3_mm, 1)
                    pe.wait_ge(p1_done, i + 1)
                    for a in range(2):
                        for t in range(TI):
                            mm = nc.tensor.transpose(ps1[0:CH, a * T + t * P:a * T + (t + 1) * P], A1[u][:, :, :].rearrange("p (t h) m -> p t (h m)", t=TI)[:, t, a * CH:(a + 1) * CH], ident[:, :])
                    mm.then_inc(t1_mm, 1)
                    pe.wait_ge(t3_done, i + 1)
                    for a in range(2):
                        for t in range(TI):
                            v = free(VZ[u][:, t, a * HB, 0:1], [4 * HD, HB // 2], [3 * HD, 2], [1, HD])
                            nc.tensor.matmul(ps3[0:CH, a * CH:(a + 1) * CH], A3T[u][:, t, a, :], v, start=(t == 0), stop=(t == 1))
                    for a in range(2):
                        mm = nc.tensor.matmul(ps3[0:CH, 2 * CH + a * LM:2 * CH + (a + 1) * LM], qlbd[u][:, a].rearrange("p h m -> p (h m)"), kl[u][:, a, :], start=True, stop=True)
                    mm.then_inc(k3_mm, 1)

        @block.scalar
        def _(act):
            act.wait_ge(c_in, 64)
            with images(act) as pair:
                for u in range(2):
                    nm.scalar(nc, act, pair + u, u)
                for u in range(2):
                    i = pair + u
                    for ps, dst, b0, mm_done, done in ((psQ, QT, 0, q_mm, q_done), (psK, KT, 2, k_mm, k_done)):
                        act.wait_ge(mm_done, i + 1)
                        if b0 == 0:
                            act.wait_ge(k3_done, i + 1)
                        for a in range(2):
                            ev = nc.scalar.activation(dst[u][:, a, :], ps[0:CH, a * T:(a + 1) * T], ACT.Identity, bias=qkb[:, b0 + a:b0 + a + 1])
                        ev.then_inc(done, 1)
                for u in range(2):
                    i = pair + u
                    act.wait_ge(z1_done, i + 1)
                    nc.scalar.activation(A1[u][:], A1[u][:], ACT.Exp).then_inc(e1_done, 1)
                    act.wait_ge(m3_done, i + 1)
                    for a in range(2):
                        ev = nc.scalar.activation(A3[u][:, a, :], ps3[0:CH, a * T:(a + 1) * T], ACT.Exp, bias=m3[u][:, a:a + 1], accum_out=d3[u][:, a:a + 1])
                    ev.then_inc(e3_done, 1)
                    wait_all(act, G["steady"], (c_mm, i + 1))
                    nc.scalar.activation(CV[:, :, bass.ds(i * T, T)], psC[0:CH, :].rearrange("p (a n) -> p a n", a=2), ACT.Copy).then_inc(cv_done, 1)
                    act.wait_ge(t3_mm, i + 1)
                    nc.scalar.activation(A3T[u][:], ps3[:, 0:4 * CH].rearrange("p (t a c) -> p t a c", t=TI, a=2), ACT.Copy).then_inc(t3_done, 1)
                    wait_all(act, G["steady"], (t1_mm, i + 1))
                    nc.scalar.activation(K1T[:, :, bass.ds(i * T, T)], ps1[0:CH, :].rearrange("p (a n) -> p a n", a=2), ACT.Copy).then_inc(ms_done, 1)

        @block.vector
        def _(dve):
            dve.sem_inc(ms_done, 1)
            dve.wait_ge(c_in, 64)
            dve.wait_ge(cleared, 2)
            nc.vector.tensor_scalar(hms[:, :], hm[:, :], 1.0 / (SEG * HD ** 0.5), None, ALU.mult).then_inc(cleared, 1)
            dve.wait_ge(cleared, 3)
            with images(dve) as pair:
                for u in range(2):
                    nm.vector(nc, dve, pair + u, u)
                for u in range(2):
                    i = pair + u
                    dve.wait_ge(nm.xT_free, i + 3)
                    for hh in range(2):
                        for t in range(TI):
                            ins = nc.vector.tensor_tensor(VZ[u][:, t, hh::2, hh * HD:(hh + 1) * HD],
                                                          psV[:, t * C:(t + 1) * C].rearrange("p (s h d) -> p s h d", s=HB, h=2)[:, :, hh, :],
                                                          vb[:, :].rearrange("p (s h d) -> p s h d", s=HB, h=2)[:, :, hh, :], ALU.add)
                    ins.then_inc(v_done, 1)
                    dve.wait_ge(q_done, i + 2)
                    dve.wait_ge(k_done, i + 2)
                    nc.vector.tensor_reduce(sums[u][:, 0], QT[u][:].rearrange("p a (m s) -> p a m s", m=LM), AX.X, ALU.add)
                    nc.vector.tensor_reduce(sums[u][:, 1], KT[u][:].rearrange("p a (m s) -> p a m s", m=LM), AX.X, ALU.add).then_inc(sum_done, 1)
                    dve.wait_ge(sum_done, i + 1)
                    nc.vector.tensor_scalar(kl[u][:], sums[u][:, 1], 1.0 / SEG, None, ALU.mult).then_inc(lm_done, 1)
                    for k, dst in ((0, qlbd), (1, klbd)):
                        nc.vector.tensor_tensor(dst[u][:], free(sums[u][:, k, 0, 0:1], [LM, 2], [0, HB], [1, LM]), free(hms[:, 0:1], [0, 2], [1, HB], [0, LM]), ALU.mult).then_inc(lm_done, 1)
                for u in range(2):
                    i = pair + u
                    dve.wait_ge(l1_mm, i + 1)
                    logits = ps1[:, 0:TI * C].rearrange("p (g m) -> p g m", m=LM)
                    nc.vector.tensor_reduce(m1[u][:, :], logits, AX.X, ALU.max).then_inc(m1_done, 1)
                    dve.wait_ge(m1_done, i + 1)
                    nc.vector.tensor_tensor(A1[u][:], logits, free(m1[u][:, 0:1], [1, TI * NH], [0, LM]), ALU.subtract).then_inc(z1_done, 1)
                    dve.wait_ge(l3_mm, i + 1)
                    nc.vector.tensor_reduce(m3[u][:, :], ps3[0:CH, :].rearrange("p (a n) -> p a n", a=2), AX.X, ALU.max, negate=True).then_inc(m3_done, 1)
                    dve.wait_ge(e1_done, i + 1)
                    nc.vector.tensor_reduce(d1[u][:, :], A1[u][:], AX.X, ALU.add).then_inc(d1_done, 1)
                    dve.wait_ge(d1_done, i + 1)
                    nc.vector.reciprocal(r1[u][:, :], d1[u][:, :]).then_inc(r1_done, 1)
                    dve.wait_ge(e3_done, i + 1)
                    nc.vector.reciprocal(r3[u][:, :], d3[u][:, :]).then_inc(r3_done, 1)
                    dve.wait_ge(r3_done, i + 1)
                    dve.wait_ge(k3_mm, i + 1)
                    for a in range(2):
                        nc.vector.scalar_tensor_tensor(K3[:, bass.ds(2 * i + a, 1), :].rearrange("p a (h d) -> p (a h) d", h=HB), ps3[0:CH, a * CH:(a + 1) * CH].rearrange("p (h d) -> p h d", h=HB),
                                                       r3[u][:, a:a + 1], free(hm[:, 0:1], [1, HB], [0, HD]), ALU.mult, ALU.mult)
                    nc.vector.tensor_copy(K2L[:, bass.ds(2 * i, 2), :], ps3[0:CH, 2 * CH:2 * CH + 2 * LM].rearrange("p (a m) -> p a m", a=2)).then_inc(k3_done, 1)


def l2_inverse(nc, G, consts):
    with Stage(nc, "l2i") as st:
        hm, bones = st.sb("hm", [CH, HB]), st.sb("bones", [CH, CH])
        eyes = st.sb("eyes", [CH, 3, CH])
        K2L, K3, MB = G["K2L"], G["K3"], G["MB"]
        mx, den, inv = st.sb("mx", [CH, NG]), st.sb("den", [CH, NG]), st.sb("inv", [CH, NG])
        big = lambda name: st.sb(name, [CH, NG, CH])
        K2, K2T, AT, D7, D15, D13, Vm, VT = (big(n) for n in ("K2", "K2T", "AT", "D7", "D15", "D13", "Vm", "VT"))
        ps = [st.ps(f"ps{b}") for b in range(8)]
        c_in, sm, exp_done, col_mm, col_done, bd_done, k2t_mm, k2t_done, start_done = st.sems("c_in sm exp_done col_mm col_done bd_done k2t_mm k2t_done start_done")
        a_mm, at_mm, at_done, d7_done, b_mm, d15_done, c_mm, d13_done, v_mm, vt_mm, v_done, vt_done = st.sems(
            "a_mm at_mm at_done d7_done b_mm d15_done c_mm d13_done v_mm vt_mm v_done vt_done")
        mb_mm, mb_done = st.sems("mb_mm mb_done")
        block = st.block()
        GB = 4
        NBK = NG // GB
        bank = lambda b: ps[b][0:CH, 0:GB * CH].rearrange("p (g c) -> p g c", g=GB)
        gs = lambda b: slice(b * GB, (b + 1) * GB)
        ITERATIONS = 6

        @block.sync
        def _(sp):
            sp.dma_start(hm[:, :], consts["headmask"]).then_inc(c_in, 16)
            sp.dma_start(bones[:, :], consts["blockones"]).then_inc(c_in, 16)
            sp.dma_start(eyes[:], consts["eyes"]).then_inc(c_in, 16)

        def product(pe, b0, lhs, rhs, gate, gate_at, done):
            for b in range(NBK):
                for s, at in zip(gate, gate_at):
                    pe.wait_ge(s, at + b)
                for g in range(b * GB, (b + 1) * GB):
                    mm = nc.tensor.matmul(ps[b0 + b][0:CH, (g % GB) * CH:(g % GB + 1) * CH], lhs[:, g, :], rhs[:, g, :], start=True, stop=True)
                mm.then_inc(done, 1)

        @block.tensor
        def _(pe):
            pe.wait_ge(c_in, 48)
            pe.wait_ge(sm, 5)
            nc.tensor.matmul(ps[0][0:CH, 0:NG * LM], bones[:, :], K2L[:].rearrange("p g m -> p (g m)"), start=True, stop=True).then_inc(col_mm, 1)
            pe.wait_ge(bd_done, 1)
            for b in range(NBK):
                for g in range(b * GB, (b + 1) * GB):
                    mm = nc.tensor.transpose(ps[4 + b][0:CH, (g % GB) * CH:(g % GB + 1) * CH], K2[:, g, :], G["ident"][0:CH, 0:CH])
                mm.then_inc(k2t_mm, 1)
            with pe.Fori(0, ITERATIONS) as it:
                product(pe, 0, K2T, Vm, (v_done, vt_done), (4 * it + 1, 4 * it + 1), a_mm)
                product(pe, 4, Vm, K2T, (vt_done,), (4 * it + 1,), at_mm)
                product(pe, 0, AT, D7, (at_done, d7_done), (4 * it + 1, 4 * it + 1), b_mm)
                product(pe, 4, AT, D15, (d15_done,), (4 * it + 1,), c_mm)
                product(pe, 0, VT, D13, (d13_done,), (4 * it + 1,), v_mm)
                product(pe, 4, D13, VT, (d13_done,), (4 * it + 1,), vt_mm)
            product(pe, 0, VT, K3, (v_done, vt_done), (4 * ITERATIONS + 1, 4 * ITERATIONS + 1), mb_mm)

        @block.scalar
        def _(act):
            act.wait_ge(sm, 2)
            nc.scalar.activation(K2L[:], K2L[:], ACT.Exp).then_inc(exp_done, 1)
            for b in range(NBK):
                act.wait_ge(k2t_mm, b + 1)
                nc.scalar.activation(K2T[:, gs(b), :], bank(4 + b), ACT.Copy).then_inc(k2t_done, 1)
            with act.Fori(0, ITERATIONS) as it:
                for b in range(NBK):
                    act.wait_ge(at_mm, 4 * it + b + 1)
                    nc.scalar.activation(AT[:, gs(b), :], bank(4 + b), ACT.Copy).then_inc(at_done, 1)
                for b in range(NBK):
                    act.wait_ge(vt_mm, 4 * it + b + 1)
                    nc.scalar.activation(VT[:, gs(b), :], bank(4 + b), ACT.Copy, scale=0.25).then_inc(vt_done, 1)
            for b in range(2):
                act.wait_ge(mb_mm, b + 1)
                nc.scalar.activation(MB[:, gs(b), :], bank(b), ACT.Copy).then_inc(mb_done, 1)

        @block.vector
        def _(dve):
            nc.vector.tensor_reduce(mx[:, :], K2L[:], AX.X, ALU.max).then_inc(sm, 1)
            dve.wait_ge(sm, 1)
            nc.vector.tensor_tensor(K2L[:], K2L[:], free(mx[:, 0:1], [1, NG], [0, LM]), ALU.subtract).then_inc(sm, 1)
            dve.wait_ge(exp_done, 1)
            nc.vector.tensor_reduce(den[:, :], K2L[:], AX.X, ALU.add).then_inc(sm, 1)
            dve.wait_ge(sm, 3)
            nc.vector.reciprocal(inv[:, :], den[:, :]).then_inc(sm, 1)
            dve.wait_ge(sm, 4)
            nc.vector.tensor_tensor(K2L[:], K2L[:], free(inv[:, 0:1], [1, NG], [0, LM]), ALU.mult).then_inc(sm, 1)
            dve.wait_ge(sm, 5)
            dve.wait_ge(c_in, 48)
            nc.vector.tensor_tensor(K2[:].rearrange("p g (h m) -> p g h m", h=HB), free(K2L[:, 0, 0:1], [LM, NG], [0, HB], [1, LM]),
                                    free(hm[:, 0:1], [0, NG], [1, HB], [0, LM]), ALU.mult).then_inc(bd_done, 1)
            dve.wait_ge(col_mm, 1)
            nc.vector.tensor_reduce(mx[:, :], ps[0][0:CH, 0:NG * LM].rearrange("p (g m) -> p g m", m=LM), AX.X, ALU.max).then_inc(col_done, 1)
            dve.wait_ge(col_done, 1)
            nc.vector.reciprocal(inv[:, :], mx[:, :]).then_inc(col_done, 1)
            dve.wait_ge(col_done, 2)
            dve.wait_ge(bd_done, 1)
            for b in range(NBK):
                scale = free(inv[:, b * GB:b * GB + 1], [1, GB], [0, CH])
                nc.vector.tensor_tensor(VT[:, gs(b), :], K2[:, gs(b), :], scale, ALU.mult).then_inc(vt_done, 1)
                dve.wait_ge(k2t_done, b + 1)
                nc.vector.tensor_tensor(Vm[:, gs(b), :], K2T[:, gs(b), :], scale, ALU.mult).then_inc(v_done, 1)

            def minus(dst, b0, k, gate, at, done):
                for b in range(NBK):
                    dve.wait_ge(gate, at + b)
                    nc.vector.scalar_tensor_tensor(dst[:, gs(b), :], bank(b0 + b), -1.0, free(eyes[:, k, 0:1], [0, GB], [1, CH]), ALU.mult, ALU.add).then_inc(done, 1)

            with dve.Fori(0, ITERATIONS) as it:
                minus(D7, 0, 0, a_mm, 4 * it + 1, d7_done)
                minus(D15, 0, 2, b_mm, 4 * it + 1, d15_done)
                minus(D13, 4, 1, c_mm, 4 * it + 1, d13_done)
                for b in range(NBK):
                    dve.wait_ge(v_mm, 4 * it + b + 1)
                    dve.wait_ge(vt_mm, 4 * it + b + 1)
                    nc.vector.tensor_scalar(Vm[:, gs(b), :], bank(b), 0.25, None, ALU.mult).then_inc(v_done, 1)
            for b in range(2, NBK):
                dve.wait_ge(mb_mm, b + 1)
                nc.vector.tensor_copy(MB[:, gs(b), :], bank(b)).then_inc(mb_done, 1)


def l2_output(nc, G, w):
    with Stage(nc, "l2o") as st:
        Wo, bo = st.sb("Wo", [CH, 2, C]), st.sb("bo", [P, C])
        M = [st.sb(f"M{u}", [CH, 2, CH]) for u in range(2)]
        XO = [st.sb(f"XO{u}", [CH, 2, T]) for u in range(2)]
        stats = LnStats(st, G, 1e-5)
        psO, psY = [st.ps(f"psO{u}") for u in range(2)], [st.ps(f"psY{u}") for u in range(2)]
        c_in, m_done, o_mm, o_done, y_mm, x_biased, x_done = st.sems("c_in m_done o_mm o_done y_mm x_biased x_done")
        block = st.block()

        @block.sync
        def _(sp):
            sp.dma_start(Wo[:, :, :], w["Wo"].rearrange("(k p) n -> p k n", p=CH)).then_inc(c_in, 16)
            sp.dma_start(bo[:, :], rows(w["bo"], 0, [0, P], [1, C])).then_inc(c_in, 16)

        @block.gpsimd
        def _(pool):
            stats.init(pool)
            pool.wait_ge(c_in, 32)
            with images(pool) as pair:
                for u in range(2):
                    i = pair + u
                    wait_all(pool, G["steady"], (o_mm, i + 1))
                    nc.gpsimd.tensor_copy(M[u][:], G["MB"][:, bass.ds(2 * i, 2), :]).then_inc(m_done, 1)
                    X = G["X"][:, bass.ds(TI * i, TI), :]
                    nc.gpsimd.tensor_tensor(X, X, free(bo[:, 0:1], [0, TI], [1, C]), ALU.add).then_inc(x_biased, 1)
                for u in range(2):
                    stats.gpsimd(nc, pool, pair + u, u)

        @block.tensor
        def _(pe):
            for s in (o_mm, o_done, x_done):
                pe.sem_inc(s, 2)
            pe.wait_ge(c_in, 32)
            with images(pe) as pair:
                for u in range(2):
                    i = pair + u
                    pe.wait_ge(m_done, i + 1)
                    pe.wait_ge(o_done, i + 1)
                    for a in range(2):
                        mm = nc.tensor.matmul(psO[u][0:CH, a * T:(a + 1) * T], M[u][:, a, :], G["K1T"][:, bass.ds(a, 1), bass.ds(i * T, T)].rearrange("p a n -> p (a n)"), start=True, stop=True)
                    mm.then_inc(o_mm, 1)
                for u in range(2):
                    i = pair + u
                    pe.wait_ge(o_done, i + 3)
                    pe.wait_ge(x_done, i + 1)
                    for t in range(TI):
                        for a in range(2):
                            mm = nc.tensor.matmul(psY[u][:, t * C:(t + 1) * C], XO[u][:, a, t * P:(t + 1) * P], Wo[:, a, :], start=(a == 0), stop=(a == 1))
                    mm.then_inc(y_mm, 1)

        @block.vector
        def _(dve):
            dve.sem_inc(y_mm, 2)
            with images(dve) as pair:
                for u in range(2):
                    i = pair + u
                    dve.wait_ge(o_mm, i + 3)
                    dve.wait_ge(y_mm, i + 1)
                    nc.vector.tensor_tensor(XO[u][:], psO[u][0:CH, :].rearrange("p (a n) -> p a n", a=2), G["CV"][:, :, bass.ds(i * T, T)], ALU.add).then_inc(o_done, 1)
                for u in range(2):
                    i = pair + u
                    dve.wait_ge(y_mm, i + 3)
                    dve.wait_ge(x_biased, i + 1)
                    X = G["X"][:, bass.ds(TI * i, TI), :]
                    nc.vector.tensor_tensor(X, psY[u][:, 0:TI * C].rearrange("p (t c) -> p t c", t=TI), X, ALU.add).then_inc(x_done, 1)
                    stats.vector(nc, dve, i, u, (x_done, i + 3))



E = 8
FI = 512
SLOT_TILES = -(-(2 * B * T + E * (P - 1)) // (2 * P)) * 2
CAP = B * T // E


def route(nc, G, name, w_router, transposed, top, n_slots, side=None):
    with Stage(nc, name) as st:
        RW = st.sb("RW", [CH, 2, E])
        XN = st.sb("XN", [P, NT, C])
        ones, tri = st.sb("ones", [P, P]), st.sb("tri", [P, P])
        desc, tiles_at, rowid = st.sb("desc", [P, E]), st.sb("tiles_at", [P, SLOT_TILES]), st.sb("rowid", [P, NT])
        grid = lambda name, dt=F32: st.sb(name, [P, NT, E], dt)
        L, Pb, Z, W, EQ = grid("L"), grid("Pb"), grid("Z"), grid("W"), grid("EQ")
        M = [grid(f"M{k}") for k in range(top)]
        MT, RK = grid("MT"), grid("RK")
        scan_t = [grid("scan0"), grid("scan1")]
        small = lambda name, n=NT, dt=F32: st.sb(name, [P, n], dt)
        m, den, best = small("m"), small("den"), small("best")
        gk = [small(f"gk{k}") for k in range(top)]
        slot, keep = small("slot"), small("keep")
        imp, bal, cnt = small("imp", E), small("bal", E), small("cnt", E)
        cnt_i, scan_e = small("cnt_i", E, I32), [small("scan_e0", E), small("scan_e1", E)]
        te, te_cmp = small("te", SLOT_TILES), st.sb("te_cmp", [P, SLOT_TILES, E])
        nm = Normed(st, G)
        psL = [st.ps(f"psL{u}") for u in range(2)]
        psI, psP = st.ps("psI"), st.ps("psP")
        c_in, l_mm, l_done, x_kept, exp_done, d, imp_mm, pre_mm, slot_done, scattered, chain, zero_out = st.sems(
            "c_in l_mm l_done x_kept exp_done probs imp_mm pre_mm slot_done scattered chain zero_out")
        extra = side(st) if side else None
        block = st.block()
        flat = lambda g: g[:].rearrange("p t e -> p (t e)")

        @block.sync
        def _(sp):
            if transposed:
                for k in range(2):
                    sp.dma_start(RW[:, k, :], rows(w_router, k * CH, [1, CH], [C, E]), allow_slow_non_contiguous=True).then_inc(c_in, 16)
            else:
                for k in range(2):
                    sp.dma_start(RW[:, k, :], w_router[k * CH:(k + 1) * CH, :]).then_inc(c_in, 16)
            for dst, src in ((ones, "ones"), (tri, "tri"), (desc, "desc"), (tiles_at, "tiles_at"), (rowid, "rowid")):
                sp.dma_start(dst[:, :], G["consts"][src]).then_inc(c_in, 16)
            for r in range(0, n_slots, n_slots // 4):
                sp.dma_start(rows(G["xs"], r * C, [8 * C, n_slots // 32], [1, 8 * C]), rows(G["consts"]["zeros"], 0, [0, n_slots // 32], [1, 8 * C])).then_inc(zero_out, 16)
            if extra:
                extra.sync(sp)

        @block.gpsimd
        def _(pool):
            with images(pool) as pair:
                for u in range(2):
                    i = pair + u
                    wait_all(pool, G["steady"], (nm.normed, TI * (i + 1)))
                    nc.gpsimd.tensor_copy(XN[:, bass.ds(TI * i, TI), :], nm.xn[:, u]).then_inc(x_kept, 1)
            pool.wait_ge(x_kept, B + 2)
            pool.wait_ge(zero_out, 64)
            for k in range(top):
                pool.wait_ge(slot_done, k + 1)
                for t in range(NT):
                    pool.indirect_dma_start(out=G["xs"], out_offset=bass.IndirectOffsetOnAxis(ap=G["slots"][k][:, t:t + 1], axis=0),
                                            in_=XN[:, t, :], in_offset=None).then_inc(scattered, 16)
            pool.wait_ge(scattered, 16 * NT * top)

        @block.tensor
        def _(pe):
            nm.init_credit(pe)
            pe.sem_inc(l_done, 2)
            pe.wait_ge(c_in, 16 * 7)
            with images(pe) as pair:
                for u in range(2):
                    nm.tensor(nc, pe, pair + u, u)
                for u in range(2):
                    i = pair + u
                    pe.wait_ge(nm.xT_done, i + 3)
                    pe.wait_ge(l_done, i + 1)
                    for t in range(TI):
                        for k in range(2):
                            mm = nc.tensor.matmul(psL[u][:, t * E:(t + 1) * E], nm.xT[u][:, k, t * P:(t + 1) * P], RW[:, k, :], start=(k == 0), stop=(k == 1))
                    mm.then_inc(nm.xT_free, 1)
            if top == 2:
                pe.wait_ge(d, 1)
                nc.tensor.matmul(psI[:, 0:NT * E], ones[:, :], flat(Pb), start=True, stop=True).then_inc(imp_mm, 1)
            pe.wait_ge(d, 2)
            nc.tensor.matmul(psP[:, 0:NT * E], tri[:, :], flat(MT), start=True, stop=True)
            nc.tensor.matmul(psP[:, NT * E:2 * NT * E], ones[:, :], flat(MT), start=True, stop=True).then_inc(pre_mm, 1)
            if extra:
                extra.tensor(pe)

        @block.scalar
        def _(act):
            with images(act) as pair:
                for u in range(2):
                    nm.scalar(nc, act, pair + u, u)
            act.wait_ge(chain, 2)
            nc.scalar.activation(flat(Z), flat(Z), ACT.Exp).then_inc(exp_done, 1)
            if extra:
                extra.scalar(act)

        @block.vector
        def _(dve):
            dve.sem_inc(x_kept, 2)
            with images(dve) as pair:
                for u in range(2):
                    dve.wait_ge(x_kept, pair + u + 1)
                    nm.vector(nc, dve, pair + u, u)
                for u in range(2):
                    i = pair + u
                    dve.wait_ge(nm.xT_free, i + 3)
                    nc.vector.tensor_copy(L[:, bass.ds(TI * i, TI), :], psL[u][:, 0:TI * E].rearrange("p (t e) -> p t e", t=TI)).then_inc(l_done, 1)
            dve.wait_ge(l_done, B + 2)
            dve.wait_ge(c_in, 16 * 7)
            steps = [0]

            def link(ins):
                steps[0] += 1
                ins.then_inc(chain, 1)
                dve.wait_ge(chain, steps[0])

            V = nc.vector
            over_e = lambda v: free(v[:, 0:1], [1, NT], [0, E])
            over_t = lambda v: free(v[:, 0:1], [0, NT], [1, E])
            link(V.tensor_reduce(m[:, :], L[:], AX.X, ALU.max))
            link(V.tensor_tensor(Z[:], L[:], over_e(m), ALU.subtract))
            dve.wait_ge(exp_done, 1)
            link(V.tensor_reduce(den[:, :], Z[:], AX.X, ALU.add))
            link(V.reciprocal(den[:, :], den[:, :]))
            V.tensor_tensor(Pb[:], Z[:], over_e(den), ALU.mult).then_inc(d, 1)
            dve.wait_ge(d, 1)
            src = Pb
            for k in range(top):
                link(V.tensor_reduce(best[:, :], src[:], AX.X, ALU.max))
                link(V.tensor_tensor(EQ[:], src[:], over_e(best), ALU.is_equal))
                link(V.tensor_tensor(W[:], EQ[:], over_t(desc), ALU.mult))
                link(V.tensor_reduce(m[:, :], W[:], AX.X, ALU.max))
                link(V.tensor_tensor(M[k][:], W[:], over_e(m), ALU.is_equal))
                if k + 1 < top:
                    link(V.scalar_tensor_tensor(W[:], M[k][:], -2.0, Pb[:], ALU.mult, ALU.add))
                    link(V.tensor_copy(Z[:], W[:]))
                    src = Z
            if top == 2:
                V.tensor_tensor(MT[:], M[0][:], M[1][:], ALU.add).then_inc(d, 1)
                dve.wait_ge(imp_mm, 1)
                link(V.tensor_reduce(imp[:, :], psI[:, 0:NT * E].rearrange("p (t e) -> p e t", t=NT), AX.X, ALU.add))
                link(V.tensor_scalar(bal[:, :], imp[:, :], 1.0, 1.0 - 0.9, ALU.subtract, ALU.mult))
                link(V.tensor_scalar(bal[:, :], bal[:, :], 1.0, None, ALU.add))
                link(V.tensor_scalar(bal[:, :], bal[:, :], 0.01, None, ALU.add))
                link(V.reciprocal(bal[:, :], bal[:, :]))
                link(V.tensor_tensor(Pb[:], Pb[:], over_t(bal), ALU.mult))
                for k in range(2):
                    link(V.tensor_tensor(W[:], Pb[:], M[k][:], ALU.mult))
                    link(V.tensor_reduce(gk[k][:, :], W[:], AX.X, ALU.add))
                link(V.tensor_tensor(den[:, :], gk[0][:, :], gk[1][:, :], ALU.add))
                link(V.reciprocal(den[:, :], den[:, :]))
                for k in range(2):
                    link(V.tensor_tensor(G["gates"][k][:, :], gk[k][:, :], den[:, :], ALU.mult))
            else:
                V.tensor_copy(MT[:], M[0][:]).then_inc(d, 1)

            def scan(bufs, n, at):
                k, s = 0, 1
                while s < n:
                    V.tensor_copy(at(bufs[1 - k], 0, s), at(bufs[k], 0, s))
                    link(V.tensor_tensor(at(bufs[1 - k], s, n), at(bufs[k], s, n), at(bufs[k], 0, n - s), ALU.add))
                    k, s = 1 - k, 2 * s
                return bufs[k]

            dve.wait_ge(pre_mm, 1)
            totals = psP[:, NT * E:2 * NT * E].rearrange("p (t e) -> p t e", t=NT)
            link(V.tensor_copy(scan_t[0][:], totals))
            upto = scan(scan_t, NT, lambda b, lo, hi: b[:, lo:hi, :])
            link(V.tensor_tensor(RK[:], upto[:], totals, ALU.subtract))
            link(V.tensor_tensor(RK[:], RK[:], psP[:, 0:NT * E].rearrange("p (t e) -> p t e", t=NT), ALU.add))
            if top == 2:
                link(V.tensor_scalar(cnt[:, :], upto[:, NT - 1, :], float(P - 1), None, ALU.add))
                link(V.tensor_copy(cnt_i[:, :], cnt[:, :]))
                link(V.tensor_scalar(cnt_i[:, :], cnt_i[:, :], 7, None, ALU.arith_shift_right))
                link(V.tensor_copy(cnt[:, :], cnt_i[:, :]))
                link(V.tensor_copy(scan_e[0][:, :], cnt[:, :]))
                ends = scan(scan_e, E, lambda b, lo, hi: b[:, lo:hi])
                link(V.tensor_tensor(te_cmp[:], free(tiles_at[:, 0:1], [1, SLOT_TILES], [0, E]), free(ends[:, 0:1], [0, SLOT_TILES], [1, E]), ALU.is_ge))
                link(V.tensor_reduce(te[:, :], te_cmp[:], AX.X, ALU.add))
                link(V.tensor_scalar(te[:, :], te[:, :], float(E - 1), None, ALU.min))
                link(V.tensor_copy(G["tile_expert"][:, :], te[:, :]))
                link(V.tensor_tensor(bal[:, :], ends[:, :], cnt[:, :], ALU.subtract))
                link(V.tensor_scalar(bal[:, :], bal[:, :], float(P), -1.0, ALU.mult, ALU.add))
                link(V.tensor_tensor(RK[:], RK[:], over_t(bal), ALU.add))
                for k in range(2):
                    link(V.tensor_tensor(W[:], RK[:], M[k][:], ALU.mult))
                    link(V.tensor_reduce(slot[:, :], W[:], AX.X, ALU.add))
                    V.tensor_copy(G["slots"][k][:, :], slot[:, :]).then_inc(slot_done, 1)
                    dve.wait_ge(slot_done, k + 1)
            else:
                link(V.tensor_tensor(W[:], RK[:], M[0][:], ALU.mult))
                link(V.tensor_reduce(slot[:, :], W[:], AX.X, ALU.add))
                link(V.tensor_scalar(keep[:, :], slot[:, :], float(CAP), None, ALU.is_lt))
                link(V.tensor_scalar(m[:, :], m[:, :], -float(CAP), float(CAP * E), ALU.mult, ALU.add))
                link(V.tensor_tensor(slot[:, :], slot[:, :], m[:, :], ALU.add))
                link(V.tensor_tensor(G["gates"][0][:, :], best[:, :], keep[:, :], ALU.mult))
                link(V.tensor_tensor(slot[:, :], slot[:, :], keep[:, :], ALU.mult))
                link(V.tensor_copy(G["slots"][1][:, :], slot[:, :]))
                link(V.tensor_scalar(keep[:, :], keep[:, :], -1.0, 1.0, ALU.mult, ALU.add))
                link(V.tensor_tensor(keep[:, :], keep[:, :], rowid[:, :], ALU.mult))
                link(V.tensor_tensor(slot[:, :], slot[:, :], keep[:, :], ALU.add))
                V.tensor_copy(G["slots"][0][:, :], slot[:, :]).then_inc(slot_done, 1)
            if extra:
                extra.vector(dve)


class ExpertWeights:

    NM = FI // P

    def __init__(self, nc, G, w1, w2):
        self.nc, self.G, self.w1, self.w2 = nc, G, w1, w2

    def __call__(self, st):
        NM = self.NM
        self.raw1 = [st.sb(f"raw1{b}", [P, NM, C]) for b in range(2)]
        self.raw2 = [st.sb(f"raw2{b}", [CH, 2, FI]) for b in range(2)]
        self.ps1 = [st.ps(f"psw{b}") for b in range(2)]
        self.raw_in = [st.sem(f"raw_in{b}") for b in range(2)]
        self.turned, self.kept, self.raw_free = st.sems("w_turned w_kept raw_free")
        return self

    def sync(self, sp):
        for e in range(E):
            b = e % 2
            if e >= 2:
                sp.wait_ge(self.turned, 4 * (e - 1))
            sp.dma_start(self.raw1[b][:], rows(self.w1, e * FI * C, [C, P], [P * C, self.NM], [1, C])).then_inc(self.raw_in[b], 16)
            sp.dma_start(self.raw2[b][:], rows(self.w2, e * C * FI, [FI, CH], [CH * FI, 2], [1, FI])).then_inc(self.raw_in[b], 16)

    def tensor(self, pe):
        n = 0
        for e in range(E):
            b = e % 2
            pe.wait_ge(self.raw_in[b], 32 * (e // 2 + 1))
            for part in range(4):
                if n >= 2:
                    pe.wait_ge(self.kept, n - 1)
                ps = self.ps1[n % 2]
                for mb in range(self.NM):
                    if part < 2:
                        mm = self.nc.tensor.transpose(ps[0:CH, mb * P:(mb + 1) * P], self.raw1[b][:, mb, part * CH:(part + 1) * CH], self.G["ident"][:, :])
                    else:
                        mm = self.nc.tensor.transpose(ps[:, mb * CH:(mb + 1) * CH], self.raw2[b][:, part - 2, mb * P:(mb + 1) * P], self.G["ident"][0:CH, 0:CH])
                mm.then_inc(self.turned, 1)
                n += 1

    def scalar(self, act):
        for n in range(4 * E):
            e, part = n // 4, n % 4
            act.wait_ge(self.turned, n + 1)
            if part < 2:
                dst, src = self.G["W1T"][:, part, e * FI:(e + 1) * FI], self.ps1[n % 2][0:CH, :]
            else:
                dst = self.G["W2T"][:, e * self.NM:(e + 1) * self.NM, (part - 2) * CH:(part - 1) * CH]
                src = self.ps1[n % 2][:, 0:self.NM * CH].rearrange("p (m c) -> p m c", m=self.NM)
            self.nc.scalar.activation(dst, src, ACT.Copy).then_inc(self.kept, 1)

    def vector(self, dve):
        pass


def slots_of_tiles(eng, slot):
    for s in range(-3, 0):
        slot(0, s, lambda ahead: s + ahead >= 0)
    with eng.Fori(0, SLOT_TILES // 2 - 2) as pair:
        for s in range(2):
            slot(pair, s, lambda ahead: True)
    for s in range(4):
        slot(SLOT_TILES // 2 - 2, s, lambda ahead: s + ahead < 4)


def experts_any(nc, G):
    with Stage(nc, "l2e") as st:
        NM = FI // P
        two = lambda name, shape: [st.sb(f"{name}{b}", shape) for b in range(2)]
        X, XT, H, HT, Y = two("X", [P, C]), two("XT", [CH, 2, P]), two("H", [P, FI]), two("HT", [P, NM, P]), two("Y", [P, C])
        psX, psH, psT, psY = ([st.ps(f"{n}{b}") for b in range(2)] for n in ("psX", "psH", "psT", "psY"))
        x_in, y_out = st.sems("x_in0 x_in1"), st.sems("y_out0 y_out1")
        xt_mm, xt_done, h_mm, h_done, ht_mm, ht_done, y_mm, y_done = st.sems("xt_mm xt_done h_mm h_done ht_mm ht_done y_mm y_done")
        block = st.block()
        PAIRS = SLOT_TILES // 2

        @block.sync
        def _(sp):
            of_tile = lambda buf, j: image_of(buf.rearrange("(j n) c -> j (n c)", n=P), j, 0, [C, P], [1, C])

            def load(pair):
                for b in range(2):
                    sp.wait_ge(xt_mm, pair * 2 + b + 1)
                    sp.dma_start(X[b][:, :], of_tile(G["xs"], pair * 2 + b)).then_inc(x_in[b], 16)

            def store(pair):
                for b in range(2):
                    sp.wait_ge(y_done, pair * 2 + b + 1)
                    sp.dma_start(of_tile(G["ys"], pair * 2 + b), Y[b][:, :]).then_inc(y_out[b], 16)

            for b in range(2):
                sp.sem_inc(y_out[b], 16)
            load(0)
            load(1)
            with sp.Fori(0, PAIRS - 2) as pair:
                load(pair + 2)
                store(pair)
            store(PAIRS - 2)
            store(PAIRS - 1)
            for b in range(2):
                sp.wait_ge(y_out[b], 16 * (PAIRS + 1))

        @block.tensor
        def _(pe):
            for s in (xt_mm, xt_done, h_mm, h_done, ht_mm, ht_done, y_mm):
                pe.sem_inc(s, 2)

            def expert(j):
                return pe.value_load(G["tile_expert"][0:1, bass.ds(j, 1)], min_val=0, max_val=E - 1)

            def turn_tokens(p, s):
                j, b = p * 2 + s, s % 2
                pe.wait_ge(x_in[b], (p + s // 2) * 16 + 16)
                pe.wait_ge(xt_done, j + 1)
                for k in range(2):
                    mm = nc.tensor.transpose(psX[b][0:CH, k * P:(k + 1) * P], X[b][:, k * CH:(k + 1) * CH], G["ident"][:, :])
                mm.then_inc(xt_mm, 1)

            def first_layer(p, s):
                j, b = p * 2 + s, s % 2
                e = expert(j)
                pe.wait_ge(xt_done, j + 3)
                pe.wait_ge(h_done, j + 1)
                for k in range(2):
                    mm = nc.tensor.matmul(psH[b][:, :], XT[b][:, k, :], G["W1T"][:, k, bass.ds(e * FI, FI)], start=(k == 0), stop=(k == 1))
                mm.then_inc(h_mm, 1)

            def turn_hidden(p, s):
                j, b = p * 2 + s, s % 2
                pe.wait_ge(h_done, j + 3)
                pe.wait_ge(ht_done, j + 1)
                for mb in range(NM):
                    mm = nc.tensor.transpose(psT[b][:, mb * P:(mb + 1) * P], H[b][:, mb * P:(mb + 1) * P], G["ident"][:, :])
                mm.then_inc(ht_mm, 1)

            def second_layer(p, s):
                j, b = p * 2 + s, s % 2
                e = expert(j)
                pe.wait_ge(ht_done, j + 3)
                for mb in range(NM):
                    mm = nc.tensor.matmul(psY[b][:, 0:C], HT[b][:, mb, :], G["W2T"][:, bass.ds(e * NM + mb, 1), :].rearrange("p a c -> p (a c)"), start=(mb == 0), stop=(mb == NM - 1))
                mm.then_inc(y_mm, 1)

            def slot(p, s, has):
                for ahead, step in ((3, turn_tokens), (2, first_layer), (1, turn_hidden), (0, second_layer)):
                    if has(ahead):
                        step(p, s + ahead)

            slots_of_tiles(pe, slot)

        @block.scalar
        def _(act):
            def slot(p, s, has):
                if has(2):
                    j, b = p * 2 + s + 2, s % 2
                    act.wait_ge(h_mm, j + 3)
                    act.wait_ge(ht_mm, j + 1)
                    nc.scalar.activation(H[b][:, :], psH[b][:, :], ACT.Silu).then_inc(h_done, 1)

            slots_of_tiles(act, slot)

        @block.vector
        def _(dve):
            def slot(p, s, has):
                if has(3):
                    j, b = p * 2 + s + 3, (s + 3) % 2
                    dve.wait_ge(xt_mm, j + 3)
                    dve.wait_ge(h_mm, j + 1)
                    nc.vector.tensor_copy(XT[b][:], psX[b][0:CH, 0:2 * P].rearrange("p (k n) -> p k n", k=2)).then_inc(xt_done, 1)
                if has(1):
                    j, b = p * 2 + s + 1, (s + 1) % 2
                    dve.wait_ge(ht_mm, j + 3)
                    dve.wait_ge(y_mm, j + 1)
                    nc.vector.tensor_copy(HT[b][:], psT[b][:, :].rearrange("p (m n) -> p m n", m=NM)).then_inc(ht_done, 1)
                if has(0):
                    j, b = p * 2 + s, s % 2
                    dve.wait_ge(y_mm, j + 3)
                    dve.wait_ge(y_out[b], (p + s // 2) * 16 + 16)
                    nc.vector.tensor_copy(Y[b][:, :], psY[b][:, 0:C]).then_inc(y_done, 1)

            slots_of_tiles(dve, slot)


def experts_each(nc, G, w):
    with Stage(nc, "l3e") as st:
        two = lambda name, shape: [st.sb(f"{name}{b}", shape) for b in range(2)]
        X, XT, HT, Z, Y = two("X", [P, TI, C]), two("XT", [CH, 2, CAP]), two("HT", [P, MF, CAP]), two("Z", [P, TI, C]), two("Y", [P, TI, C])
        W1, b1, W2, b2 = two("W1", [CH, 2, FF]), two("b1", [P, MF]), two("W2", [P, MF, C]), two("b2", [P, C])
        psX, psY = [st.ps(f"psX{b}") for b in range(2)], [st.ps(f"psY{b}") for b in range(2)]
        psH = [st.ps(f"psH{k}") for k in range(MF // 2)]
        x_in, w_in, y_out = st.sems("x_in0 x_in1"), st.sems("w_in0 w_in1"), st.sems("y_out0 y_out1")
        xt_mm, xt_done, h_mm, h_done, y_mm, z_done, y_done = st.sems("xt_mm xt_done h_mm h_done y_mm z_done y_done")
        H3 = MF // 2
        block = st.block()
        TC = CAP // P

        @block.sync
        def _(sp):
            of_expert = lambda buf, e, *dims: image_of(buf, e, 0, *dims)
            slots = lambda buf: buf.rearrange("(e n) c -> e (n c)", n=CAP)
            tiles = ([C, P], [P * C, TC], [1, C])

            def load(pair):
                for b in range(2):
                    e = pair * 2 + b
                    sp.wait_ge(y_done, e + 1)
                    sp.dma_start(X[b][:], of_expert(slots(G["xs"]), e, *tiles)).then_inc(x_in[b], 16)
                    sp.dma_start(W1[b][:], of_expert(w["w1"].rearrange("e d m -> e (d m)"), e, [FF, CH], [CH * FF, 2], [1, FF])).then_inc(w_in[b], 16)
                    sp.dma_start(b1[b][:, :], of_expert(w["b1"], e, [1, P], [P, MF]), allow_slow_non_contiguous=True).then_inc(w_in[b], 16)
                    sp.dma_start(W2[b][:], of_expert(w["w2"].rearrange("e m d -> e (m d)"), e, [C, P], [P * C, MF], [1, C])).then_inc(w_in[b], 16)
                    sp.dma_start(b2[b][:, :], of_expert(w["b2"], e, [0, P], [1, C])).then_inc(w_in[b], 16)

            def store(pair):
                for b in range(2):
                    e = pair * 2 + b
                    sp.wait_ge(y_done, e + 3)
                    sp.dma_start(of_expert(slots(G["ys"]), e, *tiles), Y[b][:]).then_inc(y_out[b], 16)

            for b in range(2):
                sp.sem_inc(y_out[b], 16)
            load(0)
            with sp.Fori(0, E // 2 - 1) as pair:
                load(pair + 1)
                store(pair)
            store(E // 2 - 1)
            for b in range(2):
                sp.wait_ge(y_out[b], 16 * (E // 2 + 1))

        @block.tensor
        def _(pe):
            for s, k in ((xt_done, 2), (h_done, H3), (z_done, 2), (y_done, 2)):
                pe.sem_inc(s, k)
            with pe.Fori(0, E // 2) as pair:
                for b in range(2):
                    e = pair * 2 + b
                    pe.wait_ge(x_in[b], pair * 16 + 16)
                    pe.wait_ge(xt_done, e + 1)
                    for t in range(TC):
                        for k in range(2):
                            mm = nc.tensor.transpose(psX[b][0:CH, k * CAP + t * P:k * CAP + (t + 1) * P], X[b][:, t, k * CH:(k + 1) * CH], G["ident"][:, :])
                    mm.then_inc(xt_mm, 1)
                for b in range(2):
                    e = pair * 2 + b
                    pe.wait_ge(xt_done, e + 3)
                    pe.wait_ge(w_in[b], pair * 64 + 64)
                    for k2 in range(H3):
                        pe.wait_ge(h_done, H3 * e + k2 + 1)
                        for m in (2 * k2, 2 * k2 + 1):
                            for k in range(2):
                                mm = nc.tensor.matmul(psH[k2][:, m % 2 * CAP:(m % 2 + 1) * CAP], W1[b][:, k, m * P:(m + 1) * P], XT[b][:, k, :], start=(k == 0), stop=(k == 1))
                        mm.then_inc(h_mm, 1)
                for b in range(2):
                    e = pair * 2 + b
                    pe.wait_ge(h_done, H3 * (e + 2))
                    pe.wait_ge(z_done, e + 1)
                    for t in range(TC):
                        for m in range(MF):
                            mm = nc.tensor.matmul(psY[b][:, t * C:(t + 1) * C], HT[b][:, m, t * P:(t + 1) * P], W2[b][:, m, :], start=(m == 0), stop=(m == MF - 1))
                    mm.then_inc(y_mm, 1)

        @block.scalar
        def _(act):
            with act.Fori(0, E // 2) as pair:
                for b in range(2):
                    e = pair * 2 + b
                    act.wait_ge(y_done, e + 1)
                    act.wait_ge(w_in[b], pair * 64 + 64)
                    for k2 in range(H3):
                        act.wait_ge(h_mm, H3 * e + k2 + 1)
                        for m in (2 * k2, 2 * k2 + 1):
                            ge = nc.scalar.activation(HT[b][:, m, :], psH[k2][:, m % 2 * CAP:(m % 2 + 1) * CAP], ACT.Gelu_apprx_tanh, bias=b1[b][:, m:m + 1])
                        ge.then_inc(h_done, 1)
                for b in range(2):
                    e = pair * 2 + b
                    act.wait_ge(z_done, e + 3)
                    act.wait_ge(y_out[b], pair * 16 + 16)
                    nc.scalar.activation(Y[b][:], Z[b][:], ACT.Gelu_apprx_tanh).then_inc(y_done, 1)

        @block.vector
        def _(dve):
            with dve.Fori(0, E // 2) as pair:
                for b in range(2):
                    e = pair * 2 + b
                    dve.wait_ge(xt_mm, e + 1)
                    dve.wait_ge(y_done, e + 1)
                    nc.vector.tensor_copy(XT[b][:], psX[b][0:CH, 0:2 * CAP].rearrange("p (k n) -> p k n", k=2)).then_inc(xt_done, 1)
                for b in range(2):
                    e = pair * 2 + b
                    dve.wait_ge(y_mm, e + 1)
                    nc.vector.tensor_tensor(Z[b][:], psY[b][:, 0:TC * C].rearrange("p (t c) -> p t c", t=TC), free(b2[b][:, 0:1], [0, TC], [1, C]), ALU.add).then_inc(z_done, 1)


def combine(nc, G, name, slots, gates, stats_eps, out=None):
    with Stage(nc, name) as st:
        Yg = [[st.sb(f"Y{b}{k}", [P, C]) for k in range(len(slots))] for b in range(4)]
        y_in = [st.sem(f"y_in{b}") for b in range(4)]
        stats = LnStats(st, G, stats_eps) if stats_eps else None
        added, x_done, written = st.sems("added x_done written")
        block = st.block()
        K = len(slots)

        @block.sync
        def _(sp):
            if out is not None:
                for t in range(0, NT, 4):
                    sp.wait_ge(added, K * (t + 4))
                    sp.dma_start(rows(out, t * P * C, [C, P], [P * C, 4], [1, C]), G["X"][:, t:t + 4, :]).then_inc(written, 16)
                sp.wait_ge(written, 16 * (NT // 4))

        @block.gpsimd
        def _(pool):
            if stats:
                stats.init(pool)
            for t in range(NT):
                b = t % 4
                if t >= 4:
                    pool.wait_ge(added, K * (t - 3))
                for k in range(K):
                    pool.indirect_dma_start(out=Yg[b][k][:, :], out_offset=None, in_=G["ys"],
                                            in_offset=bass.IndirectOffsetOnAxis(ap=slots[k][:, t:t + 1], axis=0)).then_inc(y_in[b], 16)
                if stats and t % 2 and t >= 3:
                    stats.gpsimd(nc, pool, t // 2 - 1, (t // 2 - 1) % 2)
            if stats:
                stats.gpsimd(nc, pool, B - 1, (B - 1) % 2)

        @block.vector
        def _(dve):
            n = 0
            for t in range(NT):
                b = t % 4
                dve.wait_ge(y_in[b], 16 * K * (t // 4 + 1))
                for k in range(K):
                    X = G["X"][:, t, :]
                    nc.vector.scalar_tensor_tensor(X, Yg[b][k][:, :], gates[k][:, t:t + 1], X, ALU.mult, ALU.add).then_inc(added, 1)
                    n += 1
                    dve.wait_ge(added, n)
                if stats and t % 2:
                    stats.vector(nc, dve, t // 2, t // 2 % 2)


def constants():
    import numpy as np

    f32 = lambda a: np.ascontiguousarray(a, dtype=np.float32)
    n = np.arange(W0)
    pos = [(k // WS, k % WS) for k in n]
    ext = [(r, c, w) for w, (_, _, h, wd, _) in enumerate(WINDOWS) if w for r in range(h) for c in range(wd)]
    pads = [(r, c) for r, c in pos if r >= HH - WS or c >= WW - WS]
    one = np.zeros((REL, W0 + EK), np.float32)
    win = np.zeros((12, W0 + EK), np.float32)
    for col, (r, c) in enumerate(pos + [e[:2] for e in ext] + pads):
        one[r, col] = one[WS + c, col] = 1
    for w in (1, 2, 3):
        for k, e in enumerate(ext):
            if e[2] != w:
                win[w - 1, W0 + k] = -1e30
        _, _, h, wd, _ = WINDOWS[w]
        for k, (r, c) in enumerate(pads):
            if r < h and c < wd:
                win[w - 1, T + k] = -1e30
    rowsq = np.zeros((12, T), np.float32)
    for k, e in enumerate(ext):
        rowsq[e[2] - 1, W0 + k] = 1
    head = np.zeros((CH, HB), np.float32)
    head[np.arange(CH), np.arange(CH) // HD] = 1
    unit = np.eye(T).reshape(T, HH, WW)
    freq = np.fft.rfft2(unit, norm="ortho").reshape(T, NF)
    dft = np.concatenate([freq.real, freq.imag], 1).reshape(TI, P, 2 * NF).transpose(1, 0, 2)
    eye = np.eye(NF).reshape(NF, HH, WF)
    inv = np.stack([np.fft.irfft2(eye * z, s=(HH, WW), norm="ortho").reshape(NF, T) for z in (1, 1j)])
    idft = np.zeros((SR, 2, 2, T))
    idft[:, 0] = inv[:, :SR].transpose(1, 0, 2)
    idft[SR - F1:, 1] = inv[:, SR:].transpose(1, 0, 2)
    bf = np.dtype("bfloat16")
    return {"ident": np.eye(P, dtype=np.float32), "reverse": f32(np.eye(KS)[::-1]), "headmask": head,
            "gnones": np.full((P, P), 1 / (T * GC), np.float32), "dft": f32(dft), "idft": f32(idft),
            "zeros": np.zeros((8 * C,), np.float32), "ones": np.ones((P, P), np.float32),
            "tri": np.triu(np.ones((P, P), np.float32)), "desc": np.tile(f32(E - np.arange(E)), (P, 1)),
            "tiles_at": np.tile(f32(np.arange(SLOT_TILES)), (P, 1)),
            "rowid": f32(B * T + np.arange(NT)[None, :] * P + np.arange(P)[:, None]), "blockones": head @ head.T,
            "eyes": f32(np.stack([k * np.eye(CH) for k in (7, 13, 15)], 1)),
            "minushalf": np.full((P, GROUPS), -0.5, np.float32),
            "koh": np.concatenate([one, one, one, win]).astype(bf), "winrows": rowsq.astype(bf)}


class Network:

    def __init__(self, nc, w, consts, ctx):
        self.nc, self.w, self.consts, self.ctx = nc, w, consts, ctx
        self.G = {"consts": consts, "steady": ctx.enter_context(nc.semaphore("steady"))}
        self.sb(ctx, X=(P, NT, C), MEAN=(P, NT), RSTD=(P, NT), ident=(P, P))
        self.dram(xw=(B * T, C), xr=(B * T, C), band=(NH, P * TW))
        self.dram(BF16, qd=(B, 3 * C * T), kd=(B, 3 * C * T))

    def sb(self, ctx, **shapes):
        for name, shape in shapes.items():
            self.G[name] = ctx.enter_context(self.nc.sbuf_tensor(name, list(shape), F32))

    def dram(self, dt=F32, **shapes):
        for name, shape in shapes.items():
            self.G[name] = self.nc.dram_tensor(name, list(shape), dt).ap()

    def part(self, name):
        return {k[len(name):]: v for k, v in self.w.items() if k.startswith(name)}

    def window_attention(self):
        nc, G, w = self.nc, self.G, self.part("L0_conv_")
        with ExitStack() as ctx:
            self.sb(ctx, QF=(CH, 2, B * T), Vall=(WQ, 3 * B, C), vb=(P, C), pb=(P, C))
            self.dram(BF16, kbd=(3, C), rd=(B, 3 * REL * NH * T))
            load_x(nc, G, self.w["x"].rearrange("b h w c -> (b h w) c"), self.w["L2_attn_Wconv"], self.consts)
            attention_inputs(nc, G, "l0p", w["qkv_w"], (w["norm1_w"], w["norm1_b"], w["qkv_b"], w["proj_b"]),
                             ((0, WQ), (WQ, WQ), (W0, EXT)))
            l0_rel(nc, G, w, self.consts)
            l0_attention(nc, G, w)

    def window_mlp(self):
        l0_mlp(self.nc, self.G, self.part("L0_conv_"))

    def fourier(self):
        l1_afno(self.nc, self.G, self.part("L1_conv_"), self.consts)

    def landmark_attention(self):
        nc, G, w = self.nc, self.G, self.part("L2_attn_")
        with ExitStack() as ctx:
            self.sb(ctx, K1T=(CH, 2, B * T), CV=(CH, 2, B * T), K3=(CH, NG, CH), K2L=(CH, NG, LM), MB=(CH, NG, CH))
            l2_features(nc, G, w, self.consts)
            l2_inverse(nc, G, self.consts)
            l2_output(nc, G, w)

    def routing(self):
        G, alloc = self.G, lambda name, n, dt: self.ctx.enter_context(self.nc.sbuf_tensor(name, [P, n], dt))
        G["gates"] = [alloc(f"gate{k}", NT, F32) for k in range(2)]
        G["slots"] = [alloc(f"slots{k}", NT, U32) for k in range(2)]
        G["tile_expert"] = alloc("tile_expert", SLOT_TILES, I32)

    def two_experts(self):
        nc, G, w = self.nc, self.G, self.part("L2_ffn_")
        slots = SLOT_TILES * P
        G["xs"], G["ys"] = (nc.dram_tensor(name, [slots, C], F32).ap() for name in ("xs2", "ys2"))
        with ExitStack() as ctx:
            self.sb(ctx, W1T=(CH, 2, E * FI), W2T=(P, E * FI // P, C))
            route(nc, G, "l2r", w["router_w"], True, 2, slots, ExpertWeights(nc, G, w["w1"], w["w2"]))
            experts_any(nc, G)
        combine(nc, G, "l2c", G["slots"], G["gates"], 1e-5)

    def full_attention(self):
        with ExitStack() as ctx:
            self.G.pop("Vall", None)
            G = dict(self.G, Vall=ctx.enter_context(self.nc.sbuf_tensor("Vall3", [P, NT, C], F32)))
            attention_inputs(self.nc, G, "l3p", self.w["L3_attn_w_qkv"], None, ((0, P), (P, P)))
            attention(self.nc, G, "l3a", self.w["L3_attn_w_proj"], None, L3_REGIONS, ((0, 0, 2, P, 0),), 2, 1e-5)

    def one_expert(self, out):
        nc, G, w = self.nc, self.G, self.part("L3_ffn_")
        G["xs"], G["ys"] = nc.dram_tensor("xs3", [2 * B * T, C], F32).ap(), nc.dram_tensor("ys3", [B * T, C], F32).ap()
        route(nc, G, "l3r", w["router_w"], False, 1, B * T)
        experts_each(nc, G, w)
        combine(nc, G, "l3c", G["slots"][1:], G["gates"][:1], None, out)


def build(nc, w, consts, out):
    with ExitStack() as ctx:
        net = Network(nc, w, consts, ctx)
        net.window_attention()
        net.window_mlp()
        net.fourier()
        net.landmark_attention()
        net.routing()
        net.two_experts()
        net.full_attention()
        net.one_expert(out.rearrange("b h w c -> (b h w) c"))


def kernel(**inputs):
    import concourse.bacc as bacc
    import numpy as np
    from concourse.bass_utils import run_bass_kernel_spmd

    nc = bacc.Bacc("TRN2", target_bir_lowering=False, num_devices=1)
    arrays = {}

    def dram_input(name, a):
        arrays[name] = np.ascontiguousarray(a)
        return nc.dram_tensor(name, arrays[name].shape, mybir.dt.from_np(arrays[name].dtype), kind="ExternalInput").ap()

    w = {name: dram_input(f"in_{name}", a) for name, a in inputs.items()}
    consts = {name: dram_input(f"const_{name}", a) for name, a in constants().items()}
    out = nc.dram_tensor("out", [B, HH, WW, C], F32, kind="ExternalOutput").ap()
    build(nc, w, consts, out)
    return run_bass_kernel_spmd(nc, [arrays], core_ids=[0]).results[0]["out"]
```

```python
from contextlib import ExitStack, contextmanager

import concourse.bass as bass
from concourse import mybir

F32 = mybir.dt.float32
BF16 = mybir.dt.bfloat16
I32 = mybir.dt.int32
U32 = mybir.dt.uint32
ALU = mybir.AluOpType
ACT = mybir.ActivationFunctionType
AX = mybir.AxisListType

B, HH, WW, C = 8, 16, 16, 192
T = HH * WW
P = 128
NT = B * T // P
TI = T // P
NH, HD = 12, 16
CH = C // 2
HB = CH // HD
WS = 14
W0 = WS * WS
WQ = W0 // 2
EXT = T - W0
PADS = W0 - 4
EK = EXT + PADS
EKT = EK // 2
REL = 2 * WS
SR = 96
FF = 768
MF = FF // P
Q_TERM = (0, 0, 1, 1, 0, 2)
K_TERM = (0, 1, 0, 1, 2, 0)


def free(ap, *dims):
    return bass.AP(tensor=ap.tensor, offset=ap.offset, ap=[list(ap.ap[0])] + [list(d) for d in dims])


def rows(ap, offset, *dims):
    return bass.AP(tensor=ap.tensor, offset=offset, ap=[list(d) for d in dims])


def wait_all(eng, steady, *waits):
    values = [value if isinstance(value, int) else eng.to_reg(value) for _, value in waits]
    eng.wait_ge(waits[0][0], 1)
    eng.wait_ge(steady, 1)
    for (sem, _), value in zip(waits, values):
        eng.wait_ge(sem, value)


class Stage:

    def __init__(self, nc, name):
        self.nc, self.name, self.ctx, self.used = nc, name, ExitStack(), []

    def __enter__(self):
        self.ctx.__enter__()
        return self

    def __exit__(self, *e):
        left = self.ctx.__exit__(*e)
        numbers = sorted(self.used)
        first = 0
        for k in range(1, len(numbers) + 1):
            if k == len(numbers) or numbers[k] != numbers[k - 1] + 1:
                self.nc.gpsimd.sem_clear(range(numbers[first], numbers[k - 1] + 1))
                first = k
        return left

    def sb(self, name, shape, dt=F32):
        return self.ctx.enter_context(self.nc.sbuf_tensor(f"{self.name}_{name}", shape, dt))

    def ps(self, name, shape=(P, 512), dt=F32):
        return self.ctx.enter_context(self.nc.psum_tensor(f"{self.name}_{name}", list(shape), dt))

    def sem(self, name):
        sem = self.ctx.enter_context(self.nc.semaphore(f"{self.name}_{name}"))
        self.used.append(sem.num)
        return sem

    def sems(self, names):
        return [self.sem(n) for n in names.split()]

    def block(self):
        return self.ctx.enter_context(self.nc.Block())


class LnStats:

    def __init__(self, st, G, eps):
        self.nc, self.G, self.eps = st.nc, G, eps
        self.part = st.sb("stat_part", [P, 2, TI, 6])
        self.mv = st.sb("stat_mv", [P, 2, TI, 2])
        self.ve = st.sb("stat_ve", [P, 2, TI])
        self.rstd = st.sb("stat_rstd", [P, 2, TI])
        self.exponent = st.sb("stat_exponent", [P, TI])
        self.parts_done, self.mv_done, self.pow_done, self.kept = st.sems("stat_parts stat_mv stat_pow stat_kept")

    def init(self, pool):
        pool.sem_inc(self.kept, 2)
        self.nc.gpsimd.memset(self.exponent[:, :], -0.5).then_inc(self.pow_done, 1)

    def vector(self, nc, dve, i, u, *ready):
        wait_all(dve, self.G["steady"], *ready, (self.kept, i + 1))
        for t in range(TI):
            nc.vector.bn_stats(self.part[:, u, t, :], self.G["X"][:, bass.ds(TI * i + t, 1), :].rearrange("p a c -> p (a c)")).then_inc(self.parts_done, 1)
        wait_all(dve, self.G["steady"], (self.parts_done, TI * (i + 1)))
        for t in range(TI):
            nc.vector.bn_aggr(self.mv[:, u, t, :], self.part[:, u, t, :]).then_inc(self.mv_done, 1)

    def gpsimd(self, nc, pool, i, u):
        wait_all(pool, self.G["steady"], (self.mv_done, TI * (i + 1)))
        nc.gpsimd.tensor_scalar(self.ve[:, u, :], self.mv[:, u, :, 1], self.eps, None, ALU.add).then_inc(self.pow_done, 1)
        pool.wait_ge(self.pow_done, 2 * i + 2)
        nc.gpsimd.tensor_tensor(self.rstd[:, u, :], self.ve[:, u, :], self.exponent[:, :], ALU.pow).then_inc(self.pow_done, 1)
        wait_all(pool, self.G["steady"], (self.pow_done, 2 * i + 3))
        nc.gpsimd.tensor_copy(self.G["MEAN"][:, bass.ds(TI * i, TI)], self.mv[:, u, :, 0])
        nc.gpsimd.tensor_copy(self.G["RSTD"][:, bass.ds(TI * i, TI)], self.rstd[:, u, :]).then_inc(self.kept, 1)


class Normed:

    def __init__(self, st, G, weights=None):
        self.st, self.G, self.weights = st, G, weights
        self.xn = st.sb("xn", [P, 2, TI, C])
        self.xT = [st.sb(f"xT{u}", [CH, 2, T]) for u in range(2)]
        self.psT = [st.ps(f"psT{u}") for u in range(2)]
        self.normed, self.turned, self.xT_done, self.xT_free = st.sems("xn_done xn_turned xT_done xT_free")

    def vector(self, nc, dve, i, u):
        dve.wait_ge(self.turned, i + 1)
        for t in range(TI):
            k = TI * i + t
            nc.vector.tensor_scalar(self.xn[:, u, t, :], self.G["X"][:, bass.ds(k, 1), :].rearrange("p a c -> p (a c)"),
                                    self.G["MEAN"][:, bass.ds(k, 1)], self.G["RSTD"][:, bass.ds(k, 1)],
                                    ALU.subtract, ALU.mult).then_inc(self.normed, 1)

    def tensor(self, nc, pe, i, u):
        pe.wait_ge(self.normed, TI * (i + 1))
        pe.wait_ge(self.xT_done, i + 1)
        ps = self.psT[u][0:CH, :].rearrange("p (k n) -> p k n", k=2)
        for t in range(TI):
            for k in range(2):
                mm = nc.tensor.transpose(ps[:, k, t * P:(t + 1) * P], self.xn[:, u, t, k * CH:(k + 1) * CH], self.G["ident"][:, :])
        mm.then_inc(self.turned, 1)

    def scalar(self, nc, act, i, u):
        act.wait_ge(self.turned, i + 3)
        act.wait_ge(self.xT_free, i + 1)
        ps = self.psT[u][0:CH, :].rearrange("p (k n) -> p k n", k=2)
        if self.weights is None:
            nc.scalar.activation(self.xT[u][:, :, :], ps, ACT.Copy).then_inc(self.xT_done, 1)
        else:
            w, b = self.weights
            nc.scalar.activation(self.xT[u][:, 0, :], ps[:, 0, :], ACT.Identity, bias=b[:, 0:1], scale=w[:, 0:1])
            nc.scalar.activation(self.xT[u][:, 1, :], ps[:, 1, :], ACT.Identity, bias=b[:, 1:2], scale=w[:, 1:2]).then_inc(self.xT_done, 1)

    def init_credit(self, eng):
        eng.sem_inc(self.turned, 2)
        eng.sem_inc(self.xT_done, 2)
        eng.sem_inc(self.xT_free, 2)


@contextmanager
def images(eng):
    with eng.Fori(0, B // 2) as pair:
        yield pair * 2


def ahead(eng, first, rest):
    first(0)
    with eng.Fori(0, B // 2 - 1) as pair:
        rest(pair * 2, False)
    rest(B - 2, True)


KS = 33
TW = P + KS - 1


FOUR, FOURS = 4, B // 4


def load_x(nc, G, x, w_conv, rel_tables, consts):
    with Stage(nc, "load") as st:
        taps, rev, backwards = st.sb("taps", [KS, NH]), st.sb("rev", [KS, KS]), st.sb("backwards", [NH, KS])
        psR = st.ps("psR")
        taps_in, rev_mm, rev_done, band_out = st.sems("taps_in rev_mm rev_done band_out")
        stats = LnStats(st, G, 1e-6)
        ordered, loaded, const_in, tables_in = st.sems("ordered loaded const_in tables_in")
        xw = G["xw"]
        block = st.block()

        @block.sync
        def _(sp):
            for r0, c0, h, w, n0 in WINDOWS:
                sp.dma_start(rows(xw, n0 * C, [T * C, B], [w * C, h], [1, w * C]),
                             rows(x, (r0 * WW + c0) * C, [T * C, B], [WW * C, h], [1, w * C])).then_inc(ordered, 16)
            sp.wait_ge(ordered, 16 * len(WINDOWS))
            for i in range(0, B, 2):
                sp.dma_start(G["X"][:, TI * i:TI * (i + 2), :], rows(xw, i * T * C, [C, P], [P * C, 2 * TI], [1, C])).then_inc(loaded, 16)

        @block.scalar
        def _(act):
            act.sem_inc(G["steady"], 1)
            act.dma_start(taps[:, :], rows(w_conv, 0, [1, KS], [KS, NH]), allow_slow_non_contiguous=True).then_inc(taps_in, 16)
            act.dma_start(rev[:, :], consts["reverse"]).then_inc(taps_in, 16)
            act.dma_start(G["ident"][:, :], consts["ident"]).then_inc(const_in, 16)
            act.dma_start(rows(G["band"], 0, [P * TW, NH], [8 * TW, P // 8], [1, 8 * TW]), rows(consts["zeros"], 0, [0, NH], [0, P // 8], [1, 8 * TW])).then_inc(band_out, 16)
            for k, table in enumerate(rel_tables):
                for hh in range(HB):
                    act.dma_start(G["RT"][hh * HD:(hh + 1) * HD, k, :], rows(table, 0, [1, HD], [HD, 2 * WS - 1]), allow_slow_non_contiguous=True).then_inc(tables_in, 16)
            act.dma_start(G["hm"][:, :], consts["headmask"]).then_inc(tables_in, 16)
            act.wait_ge(rev_mm, 1)
            nc.scalar.activation(backwards[:, :], psR[0:NH, 0:KS], ACT.Copy).then_inc(rev_done, 1)
            act.wait_ge(band_out, 16)
            act.wait_ge(rev_done, 1)
            act.dma_start(rows(G["band"], 0, [P * TW, NH], [TW + 1, P], [1, KS]), free(backwards[:, 0:1], [0, P], [1, KS])).then_inc(band_out, 16)
            act.wait_ge(band_out, 32)
            act.wait_ge(const_in, 16)
            act.wait_ge(tables_in, 16 * (2 * HB + 1))

        @block.tensor
        def _(pe):
            pe.wait_ge(taps_in, 32)
            nc.tensor.matmul(psR[0:NH, 0:KS], taps[:, :], rev[:, :], start=True, stop=True).then_inc(rev_mm, 1)

        @block.vector
        def _(dve):
            dve.wait_ge(loaded, 8 * B)
            with images(dve) as i:
                for u in range(2):
                    stats.vector(nc, dve, i + u, u)

        @block.gpsimd
        def _(pool):
            stats.init(pool)
            with images(pool) as i:
                for u in range(2):
                    stats.gpsimd(nc, pool, i + u, u)


WINDOWS = ((0, 0, WS, WS, 0), (0, WS, WS, WW - WS, W0), (WS, 0, HH - WS, WS, W0 + WS * (WW - WS)),
           (WS, WS, HH - WS, WW - WS, T - (HH - WS) * (WW - WS)))


class Pieces:

    def __init__(self, st, G, name, prt, dims, n=2):
        self.G, self.n = G, n
        self.p = [st.sb(f"{name}_p{u}", [prt, 3, *dims], BF16) for u in range(n)]
        self.r = [st.sb(f"{name}_r{u}", [prt, *dims]) for u in range(n)]
        self.p0, self.rest, self.p1, self.p2 = st.sems(f"{name}_p0 {name}_rest {name}_p1 {name}_p2")
        self.out = [st.sem(f"{name}_out{u}") for u in range(n)]

    def scalar(self, nc, act, src, i, u, *ready):
        wait_all(act, self.G["steady"], *ready, (self.out[u], 16 // self.n * (i - u) + 16))
        nc.scalar.activation(self.p[u][:, 0], src, ACT.Copy).then_inc(self.p0, 1)

    def init(self, act):
        for u in range(self.n):
            act.sem_inc(self.out[u], 16)

    def finish(self, sp):
        for u in range(self.n):
            sp.wait_ge(self.out[u], 16 * B // self.n + 16)

    def vector(self, nc, dve, src, i, u):
        dve.wait_ge(self.p0, i + 1)
        nc.vector.tensor_tensor(self.r[u][:], src, self.p[u][:, 0], ALU.subtract).then_inc(self.rest, 1)

    def second(self, nc, act, i, u):
        act.wait_ge(self.rest, i + 1)
        nc.scalar.activation(self.p[u][:, 1], self.r[u][:], ACT.Copy).then_inc(self.p1, 1)

    def gpsimd(self, nc, pool, i, u):
        pool.wait_ge(self.p1, i + 1)
        nc.gpsimd.tensor_tensor(self.p[u][:, 2], self.r[u][:], self.p[u][:, 1], ALU.subtract).then_inc(self.p2, 1)

    def sync(self, sp, dst, i, u):
        sp.wait_ge(self.p2, i + 1)
        sp.dma_start(dst, self.p[u][:]).then_inc(self.out[u], 16)


def image_of(ap, i, size, *dims):
    base = ap[bass.ds(i, 1), :]
    return bass.AP(tensor=base.tensor, offset=base.offset, ap=[list(d) for d in dims])


def attention_inputs(nc, G, name, w_qkv, affine, v_tiles, before=None):
    with Stage(nc, name) as st:
        before = before and before(st)
        early = before is None
        wn, bn = st.sb("wn", [CH, 2]), st.sb("bn", [CH, 2])
        W = st.sb("W", [CH, 2, 3 * C])
        qkb = st.sb("qkb", [CH, 6])
        kb4 = st.sb("kb4", [CH, 2])
        KF = [st.sb(f"KF{u}", [CH, 2, T]) for u in range(2)]
        kbp = st.sb("kbp", [CH, 3, 2], BF16)
        kbr = st.sb("kbr", [CH, 2])
        nm = Normed(st, G, (wn, bn) if affine else None)
        QFu = None if affine else [st.sb(f"QF{u}", [CH, 2, T]) for u in range(2)]
        qp, kp = Pieces(st, G, "q", CH, (2, T)), Pieces(st, G, "k", CH, (2, T))
        psQ, psK = st.ps("psQ"), st.ps("psK")
        psV, psE = [st.ps(f"psV{u}") for u in range(2)], [st.ps(f"psE{u}") for u in range(2)]
        vn, nv = v_tiles[0][1], len(v_tiles)
        w_in, b_in, q_mm, q_free, k_mm, k_free, v_free = st.sems("w_in b_in q_mm q_free k_mm k_free v_free")
        kb_step, kb_out, kf_free, qf_free = st.sems("kb_step kb_out kf_free qf_free")
        Vall = G["Vall"]
        q_of = lambda i, u: G["QF"][:, :, bass.ds(i * T, T)] if affine else QFu[u][:, :, :]
        block = st.block()

        @block.sync
        def _(sp):
            sp.dma_start(W[:, :, :], w_qkv.rearrange("(k p) n -> p k n", p=CH)).then_inc(w_in, 16)
            if affine:
                norm_w, norm_b, b_qkv, b_out = affine
                sp.dma_start(wn[:, :], norm_w.rearrange("(k p) -> p k", p=CH), allow_slow_non_contiguous=True).then_inc(b_in, 16)
                sp.dma_start(bn[:, :], norm_b.rearrange("(k p) -> p k", p=CH), allow_slow_non_contiguous=True).then_inc(b_in, 16)
                sp.dma_start(qkb[:, :], b_qkv.rearrange("(m p) -> p m", p=CH), allow_slow_non_contiguous=True).then_inc(b_in, 16)
                sp.dma_start(G["vb"][:, :], rows(b_qkv, 2 * C, [0, P], [1, C])).then_inc(b_in, 16)
                sp.dma_start(G["pb"][:, :], rows(b_out, 0, [0, P], [1, C])).then_inc(b_in, 16)
                sp.wait_ge(kb_step, 5)
                sp.dma_start(rows(G["kbd"], 0, [1, CH], [2 * CH, 3], [CH, 2]), kbp[:, :, :],
                             allow_slow_non_contiguous=True).then_inc(kb_out, 16)
            with images(sp) as i:
                for u in range(2):
                    qp.sync(sp, image_of(G["qd"], i + u, 0, [T, CH], [C * T, 3], [CH * T, 2], [1, T]), i + u, u)
                    kp.sync(sp, image_of(G["kd"], i + u, 0, [T, CH], [C * T, 3], [CH * T, 2], [1, T]), i + u, u)
            if affine:
                sp.wait_ge(kb_out, 16)
            qp.finish(sp)
            kp.finish(sp)

        @block.gpsimd
        def _(pool):
            def thirds(i):
                for u in range(2):
                    qp.gpsimd(nc, pool, i + u, u)
                    kp.gpsimd(nc, pool, i + u, u)

            if before:
                before.init(pool)
                before.gather(pool, 0)
                before.stats(pool, 0)
                before.gather(pool, 2)
                for i in range(0, B, 2):
                    if i + 2 < B:
                        before.stats(pool, i + 2)
                    if i + 4 < B:
                        before.gather(pool, i + 4)
                    thirds(i)
            else:
                with images(pool) as i:
                    thirds(i)

        @block.tensor
        def _(pe):
            nm.init_credit(pe)
            for s in (q_free, k_free):
                pe.sem_inc(s, 1)
            pe.sem_inc(v_free, 2)
            pe.wait_ge(w_in, 16)
            with images(pe) as i:
                for u in range(2):
                    nm.tensor(nc, pe, i + u, u)
                for u in range(2):
                    pe.wait_ge(nm.xT_done, i + u + 3)
                    for ps, m0, is_free, done in ((psQ, 0, q_free, q_mm), (psK, 2, k_free, k_mm)):
                        pe.wait_ge(is_free, i + u + 1)
                        for a in range(2):
                            for k in range(2):
                                mm = nc.tensor.matmul(ps[0:CH, a * T:(a + 1) * T], W[:, k, (m0 + a) * CH:(m0 + a + 1) * CH],
                                                      nm.xT[u][:, k, :], start=(k == 0), stop=(k == 1))
                        mm.then_inc(done, 1)
                    pe.wait_ge(v_free, i + u + 1)
                    for t, (n0, n) in enumerate(v_tiles):
                        ps = psE[u][0:n, 0:C] if t == 2 else psV[u][0:n, t * C:(t + 1) * C]
                        for k in range(2):
                            mm = nc.tensor.matmul(ps, nm.xT[u][:, k, n0:n0 + n], W[:, k, 2 * C:], start=(k == 0), stop=(k == 1))
                    mm.then_inc(nm.xT_free, 1)

        @block.scalar
        def _(act):
            qp.init(act)
            kp.init(act)
            act.sem_inc(kf_free, 2)
            act.sem_inc(qf_free, 2)
            if affine:
                act.wait_ge(b_in, 80)
                nc.scalar.activation(kb4[:, :], qkb[:, 2:4], ACT.Copy, scale=HD ** -0.5).then_inc(kb_step, 1)
                act.wait_ge(kb_step, 1)

            def evacuate(dst, ps, bias, scale):
                if affine:
                    for a in range(2):
                        ev = nc.scalar.activation(dst[:, a, :], ps[0:CH, a * T:(a + 1) * T], ACT.Identity, bias=bias[:, a:a + 1], scale=scale)
                    return ev
                return nc.scalar.activation(dst, ps[0:CH, :].rearrange("p (a n) -> p a n", a=2), ACT.Copy, scale=scale)

            def norm(i):
                for u in range(2):
                    nm.scalar(nc, act, i + u, u)

            def products(i, last):
                for u in range(2):
                    act.wait_ge(q_mm, i + u + 1)
                    if not affine:
                        act.wait_ge(qf_free, i + u + 1)
                    evacuate(q_of(i + u, u), psQ, qkb[:, 0:2], 1.0).then_inc(q_free, 1)
                    act.wait_ge(k_mm, i + u + 1)
                    act.wait_ge(kf_free, i + u + 1)
                    evacuate(KF[u][:, :, :], psK, kb4, HD ** -0.5).then_inc(k_free, 1)
                    qp.scalar(nc, act, q_of(i + u, u), i + u, u, (q_free, i + u + 2))
                    kp.scalar(nc, act, KF[u][:, :, :], i + u, u, (k_free, i + u + 2))
                if early and not last:
                    norm(i + 2)
                for u in range(2):
                    qp.second(nc, act, i + u, u)
                    kp.second(nc, act, i + u, u)
                if not early and not last:
                    norm(i + 2)

            ahead(act, norm, products)

        @block.vector
        def _(dve):
            if affine:
                dve.wait_ge(kb_step, 1)
                nc.vector.tensor_copy(kbp[:, 0, :], kb4[:, :]).then_inc(kb_step, 1)
                dve.wait_ge(kb_step, 2)
                nc.vector.tensor_tensor(kbr[:, :], kb4[:, :], kbp[:, 0, :], ALU.subtract).then_inc(kb_step, 1)
                dve.wait_ge(kb_step, 3)
                nc.vector.tensor_copy(kbp[:, 1, :], kbr[:, :]).then_inc(kb_step, 1)
                dve.wait_ge(kb_step, 4)
                nc.vector.tensor_tensor(kbp[:, 2, :], kbr[:, :], kbp[:, 1, :], ALU.subtract).then_inc(kb_step, 1)
                dve.wait_ge(b_in, 80)
            def norm(i):
                if before:
                    before.ready(dve, i)
                for u in range(2):
                    nm.vector(nc, dve, i + u, u)

            def products(i, last):
                if before and not last:
                    before.vector(dve, i + 2)
                if early and not last:
                    norm(i + 2)
                for u in range(2):
                    qp.vector(nc, dve, q_of(i + u, u), i + u, u)
                    kp.vector(nc, dve, KF[u][:, :, :], i + u, u)
                    dve.wait_ge(kp.rest, i + u + 1)
                    dve.sem_inc(kf_free, 1)
                    dve.sem_inc(qf_free, 1)
                    dve.wait_ge(nm.xT_free, i + u + 3)
                    V = Vall[0:vn, bass.ds((i + u) * nv, 2), :]
                    ps = psV[u][0:vn, 0:2 * C].rearrange("p (t c) -> p t c", t=2)
                    if not affine:
                        nc.vector.tensor_copy(V, ps).then_inc(v_free, 1)
                    else:
                        nc.vector.tensor_tensor(V, ps, free(G["vb"][0:vn, :], [0, 2], [1, C]), ALU.add)
                        nc.vector.tensor_tensor(Vall[0:EXT, bass.ds((i + u) * nv + 2, 1), :], psE[u][0:EXT, 0:C].rearrange("p (t c) -> p t c", t=1),
                                                free(G["vb"][0:EXT, :], [C, 1], [1, C]), ALU.add).then_inc(v_free, 1)
                if not early and not last:
                    norm(i + 2)

            if before:
                before.vector(dve, 0)
            ahead(dve, norm, products)


def runs(axis):
    for r0, c0, h, w, n0 in WINDOWS:
        yield (h, n0, w, w, 1) if axis == 0 else (w, n0, 1, h, w)


def l0_rel(nc, G):
    with Stage(nc, "l0r") as st:
        RT, hm = G["RT"], G["hm"]
        Rbd = st.sb("Rbd", [CH, 2, WS, HB * WS])
        RHW = st.sb("RHW", [HB * WS, 4, B * T])
        rp = Pieces(st, G, "r", HB * WS, (1, FOUR * T), 2 * FOURS)
        ps = [st.ps(f"ps{c}") for c in range(5)]
        full, emptied = [st.sem(f"full{c}") for c in range(5)], [st.sem(f"emptied{c}") for c in range(5)]
        rbd_done, = st.sems("rbd_done")
        QF = G["QF"]

        def fills(axis):
            first, *rest = runs(axis)
            out = [[(0, first, i0, min(4, WS - i0))] for i0 in range(0, WS, 4)]
            col, last = 0, []
            for run in rest:
                last.append((col, run, 0, run[0]))
                col += run[0] * B * run[3]
            return out + [last]

        def evacuate(copy, bank, axis, a):
            for col, (n, base, si, cnt, step), i0, ni in fills(axis)[bank]:
                dst = RHW[:, bass.ds(a + 2 * axis, 1), base + si * i0:base + si * i0 + 1]
                ins = copy(free(dst, [si, ni], [T, B], [step, cnt]),
                           ps[bank][0:HB * WS, col:col + ni * B * cnt].rearrange("p (i b c) -> p i b c", i=ni, b=B))
            return ins

        def part(a, axis, u):
            return 2 * FOURS * a + FOURS * axis + u, FOURS * axis + u

        def columns(a, axis, u):
            return RHW[:, bass.ds(a + 2 * axis, 1), u * FOUR * T:(u + 1) * FOUR * T]

        block = st.block()

        @block.sync
        def _(sp):
            with sp.Fori(0, 2) as a:
                for axis in range(2):
                    for u in range(FOURS):
                        base = G["rd"][bass.ds((a + 2 * axis) * HB * WS, 1), u * FOUR * T:u * FOUR * T + 1]
                        rp.sync(sp, bass.AP(tensor=base.tensor, offset=base.offset, ap=[[B * T, HB * WS], [REL * NH * B * T, 3], [1, FOUR * T]]),
                                *part(a, axis, u))
            rp.finish(sp)

        @block.gpsimd
        def _(pool):
            with pool.Fori(0, 2) as a:
                for axis in range(2):
                    for u in range(FOURS):
                        rp.gpsimd(nc, pool, *part(a, axis, u))

        @block.tensor
        def _(pe):
            for c in range(5):
                pe.sem_inc(emptied[c], 1)
            pe.wait_ge(rbd_done, 2)
            with pe.Fori(0, 2) as a:
                for axis in range(2):
                    for bank, fill in enumerate(fills(axis)):
                        pe.wait_ge(emptied[bank], 2 * a + axis + 1)
                        for col, (n, base, si, cnt, step), i0, ni in fill:
                            for k in range(ni):
                                src = QF[:, bass.ds(a, 1), base + si * (i0 + k):base + si * (i0 + k) + 1]
                                mm = nc.tensor.matmul(ps[bank][0:HB * WS, col + k * B * cnt:col + (k + 1) * B * cnt], Rbd[:, axis, i0 + k, :],
                                                      free(src, [T, B], [step, cnt]), start=True, stop=True)
                        mm.then_inc(full[bank], 1)

        @block.scalar
        def _(act):
            rp.init(act)
            with act.Fori(0, 2) as a:
                for axis in range(2):
                    for bank in (0, 2):
                        act.wait_ge(full[bank], 2 * a + axis + 1)
                        evacuate(lambda o, i: nc.scalar.activation(o, i, ACT.Copy), bank, axis, a).then_inc(emptied[bank], 1)
                    ready = [(emptied[bank], 2 * a + axis + 2) for bank in range(5)]
                    for u in range(FOURS):
                        rp.scalar(nc, act, columns(a, axis, u), *part(a, axis, u), *(ready if u == 0 else ()))
                        if u:
                            rp.second(nc, act, *part(a, axis, u - 1))
                    rp.second(nc, act, *part(a, axis, FOURS - 1))

        @block.vector
        def _(dve):
            for axis in range(2):
                nc.vector.tensor_tensor(Rbd[:, axis].rearrange("p i (h k) -> p i h k", h=HB), free(RT[:, axis, WS - 1:WS], [1, WS], [0, HB], [-1, WS]),
                                        free(hm[:, 0:1], [0, WS], [1, HB], [0, WS]), ALU.mult).then_inc(rbd_done, 1)
            with dve.Fori(0, 2) as a:
                for axis in range(2):
                    for bank in (1, 3, 4):
                        dve.wait_ge(full[bank], 2 * a + axis + 1)
                        evacuate(nc.vector.tensor_copy, bank, axis, a).then_inc(emptied[bank], 1)
                    for u in range(FOURS):
                        rp.vector(nc, dve, columns(a, axis, u), *part(a, axis, u))


class Region:

    def __init__(self, q0, qn, qt, k0, kn, pcol):
        self.q0, self.qn, self.qt, self.k0, self.kn, self.pcol = q0, qn, qt, k0, kn, pcol
        self.kt, self.nq = kn // 2, qn * qt


def stack_rows(sp, dst, row, pitch, blocks, size, sem):
    for t, block in enumerate(blocks):
        base = row(block * size * NH)
        sp.dma_start(dst[t * size:(t + 1) * size, :, 0:T],
                     bass.AP(tensor=base.tensor, offset=base.offset, ap=[[pitch, size], [size * pitch, NH], [1, T]])).then_inc(sem, 16)


def slots_of_pairs(eng, lead, slot):
    for s in range(-lead, 0):
        slot(0, s)
    with eng.Fori(0, B // 2 - 1) as pair:
        for s in range(2 * NH):
            if s >= 2 * NH - lead:
                slot(pair * 2 + 2, s - 2 * NH)
            slot(pair * 2, s)
    for s in range(2 * NH):
        slot(B - 2, s)


TURN = 7


def head_at(s, ahead):
    n = s + ahead
    return divmod(n, NH) if 0 <= n < 2 * NH else None


def group_at(s, ahead):
    n = s + ahead
    return divmod(n // 4, NH // 4) if n % 4 == 0 and 0 <= n < 2 * NH else None


def attention(nc, G, name, w_out, b_out, regions, v_copies, vt, stats_eps, rel=None, setup=None):
    with Stage(nc, name) as st:
        setup = setup and setup(st, G)
        nb = 2
        lead = TURN + nb
        kw = max(r.k0 + r.kn for r in regions)
        QS = [st.sb(f"QS{u}", [SR, NH, T], BF16) for u in range(2)]
        KS = [st.sb(f"KS{u}", [SR, NH, kw], BF16) for u in range(2)]
        RS = [st.sb(f"RS{u}", [SR, NH, T], BF16) for u in range(2)] if rel else None
        KOH = st.sb("KOH", [SR, kw], BF16) if rel else None
        V = [[st.sb(f"V{u}{r}", [R.kt, 2, NH, 32]) for r, R in enumerate(regions)] for u in range(2)]
        Pr = [[st.sb(f"P{b}{r}", [R.qn, R.qt, R.kn]) for r, R in enumerate(regions)] for b in range(nb)]
        PT = [[st.sb(f"PT{b}{r}", [R.kt, 2, R.nq]) for r, R in enumerate(regions)] for b in range(2)]
        ncol = sum(R.qt for R in regions)
        nmax = [st.sb(f"nmax{b}", [P, ncol]) for b in range(nb)]
        G3 = NH // 4
        sums = st.sb("sums", [P, T])
        inv = st.sb("inv", [P, TI * 4])
        O = st.sb("O", [P, TI, C])
        OT = st.sb("OT", [CH, 2, T])
        Wo = st.sb("Wo", [CH, 2, C])
        stats = LnStats(st, G, stats_eps)
        psS = [[st.ps(f"psS{r}{b}") for b in range(nb)] for r in range(len(regions))]
        psT = [st.ps(f"psT{b}") for b in range(2)]
        psO, psG = st.ps("psO"), st.ps("psG")
        s_full, m_done, e_done, t_full, av_done = st.sems("s_full max_done exp_done t_full av_done")
        pt_done = st.sems("ptv_done pta_done")
        o_copied, grouped, inverted, norm_done = st.sems("o_copied grouped inverted norm_done")
        o_turned, o_done, y_full, x_added = st.sems("o_turned o_done y_full x_added")
        stack_in = [st.sem(f"stack_in{u}") for u in range(2)]
        c_in, w_in, v_done, v_init, x_biased, own = st.sems("c_in w_in v_done v_init x_biased own")
        n_stack = (len(Q_TERM) + len(K_TERM) + (6 if rel else 0)) * 16
        block = st.block()

        def scores(b, r, R, t=None):
            if t is None:
                return psS[r][b][0:R.qn, 0:R.qt * R.kn].rearrange("p (t k) -> p t k", t=R.qt)
            return psS[r][b][0:R.qn, t * R.kn:(t + 1) * R.kn]

        def evacuate(eng, copy, i, h):
            n, b = NH * i + h, h % 2
            eng.wait_ge(t_full, n + 1 + nb)
            eng.wait_ge(av_done, n + 1)
            for r, R in enumerate(regions):
                cp = copy(PT[b][r][:, :, :], psT[b][0:R.kt, R.pcol:R.pcol + 2 * R.nq].rearrange("p (k q) -> p k q", k=2))
            cp.then_inc(pt_done[b], 1)

        @block.sync
        def _(sp):
            with images(sp) as i:
                for u in range(2):
                    sp.wait_ge(s_full, NH * (i + u + 1))
                    stack_rows(sp, QS[u], lambda n: G["qd"][bass.ds(i + u, 1), n * T:n * T + 1], T, Q_TERM, HD, stack_in[u])
                    stack_rows(sp, KS[u], lambda n: G["kd"][bass.ds(i + u, 1), n * T:n * T + 1], T, K_TERM, HD, stack_in[u])
                    if rel:
                        stack_rows(sp, RS[u], lambda n: G["rd"][n:n + 1, bass.ds((i + u) * T, 1)], B * T, range(6), WS, stack_in[u])

        @block.gpsimd
        def _(pool):
            stats.init(pool)
            for u in range(2):
                for r, R in enumerate(regions):
                    nc.gpsimd.memset(V[u][r][:, :, :, HD:], 0.0).then_inc(own, 1)
            n = 2 * len(regions)
            pool.wait_ge(own, n)
            for u in range(2):
                for r, R in enumerate(regions):
                    nc.gpsimd.memset(V[u][r][:, :, :, HD:HD + 1], 1.0).then_inc(v_init, 1)
                    if r:
                        for k in range(2):
                            nc.gpsimd.tensor_copy(V[u][r][:, k, :, 0:HD], G["vb"][0:R.kt, :].rearrange("p (h d) -> p h d", h=NH)).then_inc(own, 1)
                            n += 1
            pool.wait_ge(own, n)

            def values(i, u):
                wait_all(pool, G["steady"], (norm_done, G3 * i + 1))
                for r, k0, nk, prt, t0 in v_copies:
                    for k in range(nk):
                        cp = nc.gpsimd.tensor_copy(V[u][r][0:prt, k0 + k, :, 0:HD],
                                                   G["Vall"][0:prt, bass.ds(i * vt + t0 + k, 1), :].rearrange("p a (h d) -> p (a h) d", h=NH))
                cp.then_inc(v_done, 1)

            def finish(i, last):
                for u in range(2):
                    if not last:
                        values(i + u + 2, u)
                    stats.gpsimd(nc, pool, i + u, u)

            for u in range(2):
                values(u, u)
            if b_out is not None:
                nc.gpsimd.tensor_tensor(G["X"][:, :, :], G["X"][:, :, :], free(b_out[:, 0:1], [0, NT], [1, C]), ALU.add).then_inc(x_biased, 1)
            with pool.Fori(0, B // 2 - 1) as pair:
                finish(pair * 2, False)
            finish(B - 2, True)

        @block.tensor
        def _(pe):
            for s, k in ((e_done, nb), (pt_done[0], 1), (pt_done[1], 1), (t_full, nb), (av_done, 2), (s_full, 2 * NH),
                         (o_copied, 1), (grouped, 1), (norm_done, 4), (o_turned, 1), (o_done, 1), (y_full, 1), (x_added, 1)):
                pe.sem_inc(s, k)
            if rel:
                pe.wait_ge(c_in, 16 * 3)
            pe.wait_ge(v_init, 2 * len(regions) + (2 if rel else 0))

            def score(i, u, h):
                n, b = NH * i + h, h % nb
                pe.wait_ge(e_done, n + 1)
                for r, R in enumerate(regions):
                    for t in range(R.qt):
                        q = slice(R.q0 + t * R.qn, R.q0 + (t + 1) * R.qn)
                        mm = nc.tensor.matmul(scores(b, r, R, t), QS[u][:, h, q], KS[u][:, h, R.k0:R.k0 + R.kn], start=True, stop=not rel)
                        if rel:
                            mm = nc.tensor.matmul(scores(b, r, R, t), RS[u][:, h, q], KOH[:, R.k0:R.k0 + R.kn], start=False, stop=True)
                mm.then_inc(s_full, 1)

            def turn(i, h):
                n, b = NH * i + h, h % 2
                pe.wait_ge(e_done, n + 1 + nb)
                pe.wait_ge(pt_done[b], NH // 2 * i + h // 2 + 1)
                if h == 6:
                    pe.wait_ge(o_done, i + 1)
                if h == 7:
                    pe.wait_ge(x_added, i + 1)
                for r, R in enumerate(regions):
                    for k in range(2):
                        for t in range(R.qt):
                            col = R.pcol + k * R.nq + t * R.qn
                            mm = nc.tensor.transpose(psT[b][0:R.kt, col:col + R.qn], Pr[h % nb][r][:, t, k * R.kt:(k + 1) * R.kt], G["ident"][0:R.qn, 0:R.qn])
                mm.then_inc(t_full, 1)

            def av(i, u, h):
                n, b, g, s = NH * i + h, h % 2, h // 4, h % 4
                if h == 0:
                    pe.wait_ge(v_done, i + 1)
                pe.wait_ge(pt_done[b], NH // 2 * i + h // 2 + 2)
                if s == 0:
                    pe.wait_ge(o_copied, G3 * i + g + 1)
                for r, R in enumerate(regions):
                    o = psO[32 * s:32 * s + 32, R.q0:R.q0 + R.nq]
                    for k in range(2):
                        mm = nc.tensor.matmul(o, V[u][r][:, k, h, :], PT[b][r][:, k, :], start=(k == 0), stop=(k == 1), skip_group_check=True)
                mm.then_inc(av_done, 1)

            def turn_group(i, g):
                pe.wait_ge(o_copied, G3 * i + g + 2)
                pe.wait_ge(norm_done, G3 * i + g + 4)
                for t in range(TI):
                    mm = nc.tensor.transpose(psG[:, t * P:(t + 1) * P], sums[:, t * P:(t + 1) * P], G["ident"][:, :])
                mm.then_inc(grouped, 1)

            def turn_out(i, last):
                pe.wait_ge(norm_done, G3 * i + G3 + 4)
                pe.wait_ge(pt_done[0], NH // 2 * (i + 1) + (1 if last else 4))
                for t in range(TI):
                    for a in range(2):
                        mm = nc.tensor.transpose(psT[0][0:CH, a * T + t * P:a * T + (t + 1) * P], O[:, t, a * CH:(a + 1) * CH], G["ident"][:, :])
                mm.then_inc(o_turned, 1)

            def project(i, last):
                pe.wait_ge(w_in, 16)
                pe.wait_ge(o_done, i + 2)
                pe.wait_ge(pt_done[1], NH // 2 * (i + 1) + (1 if last else 4))
                for t in range(TI):
                    for a in range(2):
                        mm = nc.tensor.matmul(psT[1][:, t * C:(t + 1) * C], OT[:, a, t * P:(t + 1) * P], Wo[:, a, :], start=(a == 0), stop=(a == 1))
                mm.then_inc(y_full, 1)

            def slot(i, s):
                if at := head_at(s, lead):
                    u, h = at
                    if h == 0:
                        pe.wait_ge(stack_in[u], (n_stack // 2) * i + n_stack)
                    score(i + u, u, h)
                if at := head_at(s, TURN):
                    turn(i + at[0], at[1])
                if at := head_at(s, TURN - 1):
                    u, h = at
                    av(i + u, u, h)
                if at := group_at(s, 1):
                    turn_group(i + at[0], at[1])
                last = isinstance(i, int) and i == B - 2 and s >= NH
                if s in (10, NH + 10):
                    turn_out(i + s // NH, last)
                if s in (11, NH + 11):
                    project(i + s // NH, last)

            slots_of_pairs(pe, lead, slot)

        @block.scalar
        def _(act):
            if setup:
                setup.load(act)
            if rel:
                for u in range(2):
                    act.dma_start(RS[u][SR - 12:SR, :, :], rows(G["consts"]["winrows"], 0, [T, 12], [0, NH], [1, T])).then_inc(c_in, 16)
                act.dma_start(KOH[:, :], G["consts"]["koh"]).then_inc(c_in, 16)
            act.dma_start(Wo[:, :, :], w_out.rearrange("(a p) n -> p a n", p=CH)).then_inc(w_in, 16)

            def exps(i, h):
                n, b, c = NH * i + h, h % nb, 0
                act.wait_ge(m_done, n + 1)
                act.wait_ge(t_full, n + 1)
                for r, R in enumerate(regions):
                    for t in range(R.qt):
                        ex = nc.scalar.activation(Pr[b][r][:, t, :], scores(b, r, R, t), ACT.Exp, bias=nmax[b][0:R.qn, c:c + 1])
                        c += 1
                ex.then_inc(e_done, 1)

            def copy_out(i, g):
                act.wait_ge(av_done, NH * i + 4 * g + 6)
                act.wait_ge(grouped, G3 * i + g + 1)
                nc.scalar.activation(sums[:, :], psO[:, 0:T], ACT.Copy).then_inc(o_copied, 1)

            def evacuate_out(i):
                act.wait_ge(o_turned, i + 2)
                act.wait_ge(y_full, i + 1)
                nc.scalar.activation(OT[:, :, :], psT[0][0:CH, :].rearrange("p (a n) -> p a n", a=2), ACT.Copy).then_inc(o_done, 1)

            def slot(i, s):
                if at := group_at(s, 2):
                    copy_out(i + at[0], at[1])
                if at := head_at(s, lead):
                    exps(i + at[0], at[1])
                if (at := head_at(s, TURN)) and at[1] % 2:
                    evacuate(act, lambda o, x: nc.scalar.activation(o, x, ACT.Copy), i + at[0], at[1])
                if s in (10, NH + 10):
                    evacuate_out(i + s // NH)

            slots_of_pairs(act, lead, slot)

        @block.vector
        def _(dve):
            if setup:
                setup.vector(nc, dve, KS, v_init)

            def maxima(i, h):
                n, b, c = NH * i + h, h % nb, 0
                dve.wait_ge(s_full, n + 1 + 2 * NH)
                for r, R in enumerate(regions):
                    mx = nc.vector.tensor_reduce(nmax[b][0:R.qn, c:c + R.qt], scores(b, r, R), AX.X, ALU.max, negate=True)
                    c += R.qt
                mx.then_inc(m_done, 1)

            def normalise(i, g):
                dve.wait_ge(grouped, G3 * i + g + 2)
                if g == 0:
                    dve.wait_ge(o_turned, i + 1)
                of_heads = psG[:, 0:T].rearrange("p (h d) -> p h d", d=32)
                nc.vector.reciprocal(inv[:, :], of_heads[:, :, HD]).then_inc(inverted, 1)
                dve.wait_ge(inverted, G3 * i + g + 1)
                nc.vector.tensor_tensor(O[:, :, 4 * g * HD:4 * (g + 1) * HD].rearrange("p t (h d) -> p t h d", h=4),
                                        of_heads[:, :, 0:HD].rearrange("p (t h) d -> p t h d", t=TI),
                                        free(inv[:, 0:1], [4, TI], [1, 4], [0, HD]), ALU.mult).then_inc(norm_done, 1)

            def residual(i, u):
                dve.wait_ge(y_full, i + 2)
                X = G["X"][:, bass.ds(TI * i, TI), :]
                nc.vector.tensor_tensor(X, psT[1][:, 0:TI * C].rearrange("p (t c) -> p t c", t=TI), X, ALU.add).then_inc(x_added, 1)
                stats.vector(nc, dve, i, u, (x_added, i + 2))

            def slot(i, s):
                if at := head_at(s, lead):
                    maxima(i + at[0], at[1])
                if (at := head_at(s, TURN)) and at[1] % 2 == 0:
                    evacuate(dve, nc.vector.tensor_copy, i + at[0], at[1])
                if at := group_at(s, 0):
                    normalise(i + at[0], at[1])
                if s in (11, NH + 11):
                    residual(i + s // NH, s // NH)

            if b_out is not None:
                dve.wait_ge(x_biased, 1)
            slots_of_pairs(dve, lead, slot)


L0_REGIONS = (Region(0, WQ, 2, 0, W0, 0), Region(W0, EXT, 1, W0, EK, 2 * W0))
L3_REGIONS = (Region(0, P, 2, 0, T, 0),)


def l0_attention(nc, G, w):
    attention(nc, G, "l0a", w["proj_w"], G["pb"], L0_REGIONS, ((0, 0, 2, WQ, 0), (1, 0, 1, EXT, 2)), 3, 1e-6, rel=True,
              setup=PaddingKeys)


class PaddingKeys:

    def __init__(self, st, G):
        self.G = G
        self.kb = st.sb("kb", [SR, NH], BF16)
        self.kb_in = st.sem("kb_in")

    def load(self, act):
        for t, piece in enumerate(K_TERM):
            act.dma_start(self.kb[t * HD:(t + 1) * HD, :], rows(self.G["kbd"], piece * C, [1, HD], [HD, NH]),
                         allow_slow_non_contiguous=True).then_inc(self.kb_in, 16)

    def vector(self, nc, dve, KS, done):
        dve.wait_ge(self.kb_in, 16 * len(K_TERM))
        for u in range(2):
            nc.vector.tensor_copy(KS[u][:, :, T:], free(self.kb[:, 0:1], [1, NH], [0, PADS])).then_inc(done, 1)



def l0_mlp(nc, G, w):
    with Stage(nc, "l0m") as st:
        wn, bn = st.sb("wn", [CH, 2]), st.sb("bn", [CH, 2])
        W1, b1 = st.sb("W1", [CH, 2, FF]), st.sb("b1", [P, MF])
        W2, b2 = st.sb("W2", [P, MF, C]), st.sb("b2", [P, C])
        hT = [st.sb(f"hT{u}", [P, MF, T]) for u in range(2)]
        nm = Normed(st, G, (wn, bn))
        psH = [st.ps(f"psH{k}") for k in range(MF // 2)]
        psY = [st.ps(f"psY{u}") for u in range(2)]
        c_in, h_mm, h_done, y_full, x_added, x_biased = st.sems("c_in h_mm h_done y_full x_added x_biased")
        xw_out, permuted, x_in = st.sems("xw_out permuted x_in")
        xw, xr = G["xw"], G["xr"]
        block = st.block()

        @block.sync
        def _(sp):
            sp.dma_start(wn[:, :], w["norm2_w"].rearrange("(k p) -> p k", p=CH), allow_slow_non_contiguous=True).then_inc(c_in, 16)
            sp.dma_start(bn[:, :], w["norm2_b"].rearrange("(k p) -> p k", p=CH), allow_slow_non_contiguous=True).then_inc(c_in, 16)
            sp.dma_start(W1[:, :, :], w["fc1_w"].rearrange("(k p) n -> p k n", p=CH)).then_inc(c_in, 16)
            sp.dma_start(b1[:, :], w["fc1_b"].rearrange("(m p) -> p m", p=P), allow_slow_non_contiguous=True).then_inc(c_in, 16)
            sp.dma_start(W2[:, :, :], w["fc2_w"].rearrange("(m p) n -> p m n", p=P)).then_inc(c_in, 16)
            sp.dma_start(b2[:, :], rows(w["fc2_b"], 0, [0, P], [1, C])).then_inc(c_in, 16)
            with images(sp) as pair:
                X = G["X"][:, bass.ds(TI * pair, 2 * TI), :]
                of_pair = lambda buf: buf.rearrange("(b n) c -> b (n c)", b=B)
                sp.wait_ge(x_added, pair + 2 + 2)
                sp.dma_start(image_of(of_pair(xw), pair, 0, [C, P], [P * C, 2 * TI], [1, C]), X).then_inc(xw_out, 16)
                wait_all(sp, G["steady"], (xw_out, 8 * pair + 16))
                for r0, c0, h, wd, n0 in WINDOWS:
                    o = (r0 * WW + c0) * C
                    dst = of_pair(xr)[bass.ds(pair, 1), o:o + 1]
                    src = of_pair(xw)[bass.ds(pair, 1), n0 * C:n0 * C + 1]
                    sp.dma_start(bass.AP(tensor=dst.tensor, offset=dst.offset, ap=[[T * C, 2], [WW * C, h], [1, wd * C]]),
                                 bass.AP(tensor=src.tensor, offset=src.offset, ap=[[T * C, 2], [wd * C, h], [1, wd * C]])).then_inc(permuted, 16)
                sp.wait_ge(permuted, 8 * len(WINDOWS) * pair + 16 * len(WINDOWS))
                sp.dma_start(X, image_of(of_pair(xr), pair, 0, [C, P], [P * C, 2 * TI], [1, C])).then_inc(x_in, 16)
                wait_all(sp, G["steady"], (x_in, 8 * pair + 16))

        @block.gpsimd
        def _(pool):
            pool.wait_ge(c_in, 16 * 6)
            with images(pool) as pair:
                for u in range(2):
                    i = pair + u
                    pool.wait_ge(nm.normed, TI * (i + 1))
                    X = G["X"][:, bass.ds(TI * i, TI), :]
                    nc.gpsimd.tensor_tensor(X, X, free(b2[:, 0:1], [0, TI], [1, C]), ALU.add).then_inc(x_biased, 1)

        @block.tensor
        def _(pe):
            nm.init_credit(pe)
            for s, k in ((h_done, MF // 2), (x_added, 2)):
                pe.sem_inc(s, k)
            pe.wait_ge(c_in, 16 * 6)
            def norm(pair):
                for u in range(2):
                    nm.tensor(nc, pe, pair + u, u)

            def layers(pair, last):
                for u in range(2):
                    i = pair + u
                    pe.wait_ge(nm.xT_done, i + 3)
                    for k2 in range(MF // 2):
                        pe.wait_ge(h_done, MF // 2 * i + k2 + 1)
                        for m in (2 * k2, 2 * k2 + 1):
                            for k in range(2):
                                mm = nc.tensor.matmul(psH[k2][:, m % 2 * T:(m % 2 + 1) * T], W1[:, k, m * P:(m + 1) * P], nm.xT[u][:, k, :],
                                                      start=(k == 0), stop=(k == 1))
                        mm.then_inc(h_mm if k2 < MF // 2 - 1 else nm.xT_free, 1)
                if not last:
                    norm(pair + 2)
                for u in range(2):
                    i = pair + u
                    pe.wait_ge(h_done, MF // 2 * (i + 2))
                    pe.wait_ge(x_added, i + 1)
                    for t in range(TI):
                        for m in range(MF):
                            mm = nc.tensor.matmul(psY[u][:, t * C:(t + 1) * C], hT[u][:, m, t * P:(t + 1) * P], W2[:, m, :], start=(m == 0), stop=(m == MF - 1))
                    mm.then_inc(y_full, 1)

            ahead(pe, norm, layers)

        @block.scalar
        def _(act):
            act.sem_inc(y_full, 2)
            act.wait_ge(c_in, 16 * 6)
            def norm(pair):
                for u in range(2):
                    nm.scalar(nc, act, pair + u, u)

            def layers(pair, last):
                for u in range(2):
                    i = pair + u
                    act.wait_ge(y_full, i + 1)
                    for k2 in range(MF // 2):
                        if k2 < MF // 2 - 1:
                            act.wait_ge(h_mm, (MF // 2 - 1) * i + k2 + 1)
                        else:
                            act.wait_ge(nm.xT_free, i + 3)
                        for m in (2 * k2, 2 * k2 + 1):
                            ge = nc.scalar.activation(hT[u][:, m, :], psH[k2][:, m % 2 * T:(m % 2 + 1) * T], ACT.Gelu, bias=b1[:, m:m + 1])
                        ge.then_inc(h_done, 1)
                if not last:
                    norm(pair + 2)

            ahead(act, norm, layers)

        @block.vector
        def _(dve):
            def norm(pair):
                for u in range(2):
                    nm.vector(nc, dve, pair + u, u)

            def layers(pair, last):
                if not last:
                    norm(pair + 2)
                for u in range(2):
                    i = pair + u
                    dve.wait_ge(y_full, i + 3)
                    dve.wait_ge(x_biased, i + 1)
                    X = G["X"][:, bass.ds(TI * i, TI), :]
                    nc.vector.tensor_tensor(X, psY[u][:, 0:TI * C].rearrange("p (t c) -> p t c", t=TI), X, ALU.add).then_inc(x_added, 1)

            ahead(dve, norm, layers)

NB, BS, LAMBDA = 8, 24, 0.01
WF = WW // 2 + 1
NF = HH * WF
F1 = NF - SR
GROUPS, GC = 32, C // 32


def l1_afno(nc, G, w, consts):
    with Stage(nc, "l1") as st:
        ones = st.sb("ones", [P, P])
        DF = st.sb("DF", [P, TI, 2 * NF])
        IV = st.sb("IV", [SR, 2, 2, T])
        W1 = st.sb("W1", [CH, 2, 2, CH])
        W2 = st.sb("W2", [CH, 2, 3, CH])
        b1, b2 = st.sb("b1", [CH, 2, 2]), st.sb("b2", [SR, 2, 2, CH])
        w2n = st.sb("w2n", [CH, 2, CH])
        two = lambda name, shape: [st.sb(f"{name}{u}", shape) for u in range(2)]
        mean, var, std, rstd = two("mean", [P, GROUPS]), two("var", [P, GROUPS]), two("std", [P, GROUPS]), two("rstd", [P, GROUPS])
        XC, SQ, XN, XS = two("XC", [P, TI, C]), two("SQ", [P, TI, C]), two("XN", [P, TI, C]), two("XS", [P, TI, C])
        FX, Z1, C1 = two("FX", [CH, 2, 3 * NF]), two("Z1", [CH, 2, 2 * NF]), two("C1", [CH, 2, 2 * NF])
        Z2, C2 = two("Z2", [SR, 2, 2, 2, CH]), two("C2", [SR, 2, 2, 2, CH])
        stats = LnStats(st, G, 1e-5)
        psA = [st.ps(f"psA{u}") for u in range(2)]
        psB = [[st.ps(f"psB{u}{a}") for a in range(2)] for u in range(2)]
        c_in, w_in, f_in, zeroed, mean_mm, mean_done, xc_done, sq_done, var_mm, var_done, eps_done, std_done, rstd_done, xn_done, xs_done = st.sems(
            "c_in w_in f_in zeroed mean_mm mean_done xc_done sq_done var_mm var_done eps_done std_done rstd_done xn_done xs_done")
        f_mm, f_done, z1_mm, z1_done, c1_done, o1_done, z2_mm, z2_done, c2_done, o2_done, y_mm, x_done = st.sems(
            "f_mm f_done z1_mm z1_done c1_done o1_done z2_mm z2_done c2_done o2_done y_mm x_done")
        block = st.block()
        N_IN = 16 * (4 + 2 * NB)

        @block.sync
        def _(sp):
            sp.dma_start(ones[:], consts["gnones"]).then_inc(c_in, 16)
            for dst, src in ((DF, "dft"), (IV, "idft")):
                sp.dma_start(dst[:], consts[src]).then_inc(f_in, 16)
            for part in range(2):
                sp.dma_start(b1[:, part, :], rows(w["b1"], part * C, [1, CH], [CH, 2]), allow_slow_non_contiguous=True).then_inc(w_in, 16)
                sp.dma_start(b2[:, part, :, :], rows(w["b2"], part * CH, [0, SR], [C, 2], [1, CH])).then_inc(w_in, 16)
            sp.wait_ge(zeroed, 2)
            for n in range(NB):
                a, k = n // 4, n % 4
                r = slice(k * BS, (k + 1) * BS)
                of_block = lambda ap: rows(ap, n * BS * BS, [BS, BS], [NB * BS * BS, 2], [1, BS])
                sp.dma_start(W1[r, :, a, r], of_block(w["w1"])).then_inc(w_in, 16)
                sp.dma_start(W2[r, a, 1:3, r], of_block(w["w2"])).then_inc(w_in, 16)

        @block.gpsimd
        def _(pool):
            nc.gpsimd.memset(W1[:], 0.0).then_inc(zeroed, 1)
            nc.gpsimd.memset(W2[:], 0.0).then_inc(zeroed, 1)
            stats.init(pool)
            pool.wait_ge(w_in, N_IN)
            nc.gpsimd.tensor_scalar(W2[:, :, 0, :], W2[:, :, 2, :], -1.0, None, ALU.mult).then_inc(zeroed, 1)
            with images(pool) as pair:
                for u in range(2):
                    i = pair + u
                    pool.wait_ge(xn_done, i + 1)
                    pool.wait_ge(x_done, i + 1)
                    nc.gpsimd.tensor_tensor(XS[u][:], G["X"][:, bass.ds(TI * i, TI), :], XN[u][:], ALU.add).then_inc(xs_done, 1)
                for u in range(2):
                    stats.gpsimd(nc, pool, pair + u, u)

        @block.tensor
        def _(pe):
            pe.sem_inc(x_done, 2)
            pe.sem_inc(y_mm, 2)
            pe.wait_ge(c_in, 16)
            with images(pe) as pair:
                for u in range(2):
                    i = pair + u
                    pe.wait_ge(x_done, i + 1)
                    for t in range(TI):
                        mm = nc.tensor.matmul(psA[u][:, 0:C], ones[:, :], G["X"][:, bass.ds(TI * i + t, 1), :].rearrange("p a c -> p (a c)"), start=(t == 0), stop=(t == 1))
                    mm.then_inc(mean_mm, 1)
                for u in range(2):
                    i = pair + u
                    pe.wait_ge(sq_done, i + 1)
                    for t in range(TI):
                        mm = nc.tensor.matmul(psA[u][:, 0:C], ones[:, :], SQ[u][:, t, :], start=(t == 0), stop=(t == 1))
                    mm.then_inc(var_mm, 1)
                for u in range(2):
                    i = pair + u
                    pe.wait_ge(xn_done, i + 1)
                    pe.wait_ge(f_in, 32)
                    for a in range(2):
                        for t in range(TI):
                            mm = nc.tensor.matmul(psB[u][a][0:CH, 0:2 * NF], XN[u][:, t, a * CH:(a + 1) * CH], DF[:, t, :], start=(t == 0), stop=(t == 1))
                    mm.then_inc(f_mm, 1)
                for u in range(2):
                    i = pair + u
                    pe.wait_ge(f_done, i + 1)
                    pe.wait_ge(zeroed, 3)
                    for a in range(2):
                        nc.tensor.matmul(psB[u][a][0:CH, 0:2 * NF], W1[:, 0, a, :], FX[u][:, a, NF:3 * NF], start=True, stop=False)
                        mm = nc.tensor.matmul(psB[u][a][0:CH, 0:2 * NF], W1[:, 1, a, :], FX[u][:, a, 0:2 * NF], start=False, stop=True)
                    mm.then_inc(z1_mm, 1)
                for u in range(2):
                    i = pair + u
                    pe.wait_ge(o1_done, i + 1)
                    for f in range(2):
                        f0 = f * F1
                        for a in range(2):
                            o = psB[u][f][0:SR, 2 * a * CH:2 * (a + 1) * CH]
                            nc.tensor.matmul(o, C1[u][:, a, f0:f0 + SR], W2[:, a, 1:3, :].rearrange("p k c -> p (k c)"), start=True, stop=False)
                            mm = nc.tensor.matmul(o, C1[u][:, a, NF + f0:NF + f0 + SR], W2[:, a, 0:2, :].rearrange("p k c -> p (k c)"), start=False, stop=True)
                    mm.then_inc(z2_mm, 1)
                for u in range(2):
                    i = pair + u
                    pe.wait_ge(o2_done, i + 1)
                    for t in range(TI):
                        for f in range(2):
                            for part in range(2):
                                mm = nc.tensor.matmul(psA[u][:, t * C:(t + 1) * C], IV[:, f, part, t * P:(t + 1) * P], C2[u][:, f, :, part, :],
                                                      start=(f == 0 and part == 0), stop=(f == 1 and part == 1))
                    mm.then_inc(y_mm, 1)

        @block.scalar
        def _(act):
            with images(act) as pair:
                for u in range(2):
                    i = pair + u
                    act.wait_ge(xc_done, i + 1)
                    nc.scalar.activation(SQ[u][:], XC[u][:], ACT.Square).then_inc(sq_done, 1)
                for u in range(2):
                    i = pair + u
                    act.wait_ge(eps_done, i + 1)
                    nc.scalar.activation(std[u][:, :], var[u][:, :], ACT.Sqrt).then_inc(std_done, 1)
                for u in range(2):
                    i = pair + u
                    act.wait_ge(f_mm, i + 1)
                    for a in range(2):
                        nc.scalar.activation(FX[u][:, a, NF:3 * NF], psB[u][a][0:CH, 0:2 * NF], ACT.Copy)
                        ev = nc.scalar.activation(FX[u][:, a, 0:NF], psB[u][a][0:CH, NF:2 * NF], ACT.Copy, scale=-1.0)
                    ev.then_inc(f_done, 1)
                for u in range(2):
                    i = pair + u
                    act.wait_ge(z1_mm, i + 1)
                    for a in range(2):
                        for part in range(2):
                            ev = nc.scalar.activation(Z1[u][:, a, part * NF:(part + 1) * NF], psB[u][a][0:CH, part * NF:(part + 1) * NF], ACT.Identity, bias=b1[:, part, a:a + 1])
                    ev.then_inc(z1_done, 1)

        @block.vector
        def _(dve):
            per_group = lambda ap: ap.rearrange("p (g c) -> p g c", g=GROUPS)
            with images(dve) as pair:
                for u in range(2):
                    i = pair + u
                    dve.wait_ge(mean_mm, i + 1)
                    nc.vector.tensor_reduce(mean[u][:, :], per_group(psA[u][:, 0:C]), AX.X, ALU.add).then_inc(mean_done, 1)
                    dve.wait_ge(mean_done, i + 1)
                    for t in range(TI):
                        ins = nc.vector.tensor_tensor(per_group(XC[u][:, t, :]), per_group(G["X"][:, bass.ds(TI * i + t, 1), :].rearrange("p a c -> p (a c)")),
                                                      free(mean[u][:, 0:1], [1, GROUPS], [0, GC]), ALU.subtract)
                    ins.then_inc(xc_done, 1)
                for u in range(2):
                    i = pair + u
                    dve.wait_ge(var_mm, i + 1)
                    nc.vector.tensor_reduce(var[u][:, :], per_group(psA[u][:, 0:C]), AX.X, ALU.add).then_inc(var_done, 1)
                    dve.wait_ge(var_done, i + 1)
                    nc.vector.tensor_scalar(var[u][:, :], var[u][:, :], 1e-5, None, ALU.add).then_inc(eps_done, 1)
                for u in range(2):
                    i = pair + u
                    dve.wait_ge(std_done, i + 1)
                    nc.vector.reciprocal(rstd[u][:, :], std[u][:, :]).then_inc(rstd_done, 1)
                    dve.wait_ge(rstd_done, 4 * i + 1)
                    nc.vector.tensor_tensor(std[u][:, :], rstd[u][:, :], rstd[u][:, :], ALU.mult).then_inc(rstd_done, 1)
                    dve.wait_ge(rstd_done, 4 * i + 2)
                    nc.vector.scalar_tensor_tensor(std[u][:, :], std[u][:, :], -0.5, var[u][:, :], ALU.mult, ALU.mult).then_inc(rstd_done, 1)
                    dve.wait_ge(rstd_done, 4 * i + 3)
                    nc.vector.scalar_tensor_tensor(rstd[u][:, :], std[u][:, :], 1.5, rstd[u][:, :], ALU.add, ALU.mult).then_inc(rstd_done, 1)
                    dve.wait_ge(rstd_done, 4 * i + 4)
                    for t in range(TI):
                        ins = nc.vector.tensor_tensor(per_group(XN[u][:, t, :]), per_group(XC[u][:, t, :]), free(rstd[u][:, 0:1], [1, GROUPS], [0, GC]), ALU.mult)
                    ins.then_inc(xn_done, 1)
                for u in range(2):
                    i = pair + u
                    dve.wait_ge(z1_done, i + 1)
                    nc.vector.tensor_scalar(C1[u][:], Z1[u][:], -LAMBDA, LAMBDA, ALU.max, ALU.min).then_inc(c1_done, 1)
                    dve.wait_ge(c1_done, i + 1)
                    nc.vector.tensor_tensor(C1[u][:], Z1[u][:], C1[u][:], ALU.subtract).then_inc(o1_done, 1)
                for u in range(2):
                    i = pair + u
                    dve.wait_ge(z2_mm, i + 1)
                    dve.wait_ge(w_in, N_IN)
                    for f in range(2):
                        ins = nc.vector.tensor_tensor(Z2[u][:, f], psB[u][f][0:SR, 0:4 * CH].rearrange("p (a k c) -> p a k c", a=2, k=2), b2[:], ALU.add)
                    ins.then_inc(z2_done, 1)
                    dve.wait_ge(z2_done, i + 1)
                    nc.vector.tensor_scalar(C2[u][:], Z2[u][:], -LAMBDA, LAMBDA, ALU.max, ALU.min).then_inc(c2_done, 1)
                    dve.wait_ge(c2_done, i + 1)
                    nc.vector.tensor_tensor(C2[u][:], Z2[u][:], C2[u][:], ALU.subtract).then_inc(o2_done, 1)
                for u in range(2):
                    i = pair + u
                    dve.wait_ge(y_mm, i + 3)
                    dve.wait_ge(xs_done, i + 1)
                    nc.vector.tensor_tensor(G["X"][:, bass.ds(TI * i, TI), :], psA[u][:, 0:TI * C].rearrange("p (t c) -> p t c", t=TI), XS[u][:], ALU.add).then_inc(x_done, 1)
                    stats.vector(nc, dve, i, u, (x_done, i + 3))



LM = 16
SEG = T // LM
NG = 2 * B


def l2_features(nc, G, w, consts):
    with Stage(nc, "l2p") as st:
        W, qkb = st.sb("W", [CH, 2, 3 * C]), st.sb("qkb", [CH, 4])
        vb, hm = st.sb("vb", [P, C]), st.sb("hm", [CH, HB])
        hms = st.sb("hms", [CH, HB])
        toep = st.sb("toep", [P, NH, TW])
        two = lambda name, shape: [st.sb(f"{name}{u}", shape) for u in range(2)]
        QT, KT, VZ = two("QT", [CH, 2, T]), two("KT", [CH, 2, T]), two("VZ", [P, TI, NH, 2 * HD])
        sums, kl = two("sums", [CH, 2, 2, LM]), two("kl", [CH, 2, LM])
        qlbd, klbd = two("qlbd", [CH, 2, HB, LM]), two("klbd", [CH, 2, HB, LM])
        A1, m1, d1, r1 = two("A1", [P, TI * NH, LM]), two("m1", [P, TI * NH]), two("d1", [P, TI * NH]), two("r1", [P, TI * NH])
        A3, A3T, m3, d3, r3 = two("A3", [CH, 2, T]), two("A3T", [P, TI, 2, CH]), two("m3", [CH, 2]), two("d3", [CH, 2]), two("r3", [CH, 2])
        nm = Normed(st, G)
        psQ, psK, psV, ps1, ps3, psC = (st.ps(n) for n in ("psQ", "psK", "psV", "ps1", "ps3", "psC"))
        c_in, cleared, ms_done = st.sems("c_in cleared ms_done")
        q_mm, q_done, k_mm, k_done, v_done, sum_done, lm_done = st.sems("q_mm q_done k_mm k_done v_done sum_done lm_done")
        l1_mm, m1_done, z1_done, e1_done, d1_done, r1_done, p1_done = st.sems("l1_mm m1_done z1_done e1_done d1_done r1_done p1_done")
        l3_mm, m3_done, e3_done, r3_done, t3_mm, t3_done, k3_mm, k3_done = st.sems("l3_mm m3_done e3_done r3_done t3_mm t3_done k3_mm k3_done")
        t1_mm, t1_done, c_mm, cv_done, k2_mm, k2_done, tp_in = st.sems("t1_mm t1_done c_mm cv_done k2_mm k2_done tp_in")
        K1T, CV, K3, K2L = G["K1T"], G["CV"], G["K3"], G["K2L"]
        block = st.block()

        @block.sync
        def _(sp):
            sp.dma_start(W[:, :, :], w["Wqkv"].rearrange("(k p) n -> p k n", p=CH)).then_inc(c_in, 16)
            sp.dma_start(qkb[:, :], rows(w["bqkv"], 0, [1, CH], [CH, 4]), allow_slow_non_contiguous=True).then_inc(c_in, 16)
            sp.dma_start(vb[:, :], rows(w["bqkv"], 2 * C, [0, P], [1, C])).then_inc(c_in, 16)
            sp.dma_start(hm[:, :], consts["headmask"]).then_inc(c_in, 16)
            sp.dma_start(toep[:, :, :], rows(G["band"], 0, [TW, P], [P * TW, NH], [1, TW])).then_inc(tp_in, 16)

        @block.gpsimd
        def _(pool):
            for u in range(2):
                nc.gpsimd.memset(VZ[u][:], 0.0).then_inc(cleared, 1)
            with images(pool) as pair:
                for u in range(2):
                    i = pair + u
                    pool.wait_ge(r1_done, i + 1)
                    nc.gpsimd.tensor_tensor(A1[u][:], A1[u][:], free(r1[u][:, 0:1], [1, TI * NH], [0, LM]), ALU.mult).then_inc(p1_done, 1)

        @block.tensor
        def _(pe):
            nm.init_credit(pe)
            for s in (q_done, k_done, v_done, k3_done, cv_done):
                pe.sem_inc(s, 1)
            pe.sem_inc(k3_done, 1)
            pe.wait_ge(c_in, 64)
            pe.wait_ge(tp_in, 16)
            reach = ((0, 0, P + KS // 2), (1, P - KS // 2, T))
            ident = G["ident"]
            with images(pe) as pair:
                for u in range(2):
                    nm.tensor(nc, pe, pair + u, u)
                for u in range(2):
                    i = pair + u
                    pe.wait_ge(nm.xT_done, i + 3)
                    for ps, m0, done, mm_done in ((psQ, 0, q_done, q_mm), (psK, 2, k_done, k_mm)):
                        pe.wait_ge(done, i + 1)
                        for a in range(2):
                            for k in range(2):
                                mm = nc.tensor.matmul(ps[0:CH, a * T:(a + 1) * T], W[:, k, (m0 + a) * CH:(m0 + a + 1) * CH], nm.xT[u][:, k, :], start=(k == 0), stop=(k == 1))
                        mm.then_inc(mm_done, 1)
                    pe.wait_ge(v_done, i + 1)
                    for t in range(TI):
                        for k in range(2):
                            mm = nc.tensor.matmul(psV[:, t * C:(t + 1) * C], nm.xT[u][:, k, t * P:(t + 1) * P], W[:, k, 2 * C:], start=(k == 0), stop=(k == 1))
                    mm.then_inc(nm.xT_free, 1)
                for u in range(2):
                    i = pair + u
                    pe.wait_ge(lm_done, 3 * i + 3)
                    pe.wait_ge(q_done, i + 2)
                    pe.wait_ge(k_done, i + 2)
                    pe.wait_ge(ms_done, i + 1)
                    for t in range(TI):
                        for a in range(2):
                            mm = nc.tensor.matmul(ps1[:, t * C + a * CH:t * C + (a + 1) * CH], QT[u][:, a, t * P:(t + 1) * P], klbd[u][:, a].rearrange("p h m -> p (h m)"), start=True, stop=True)
                    mm.then_inc(l1_mm, 1)
                    pe.wait_ge(k3_done, i + 2)
                    for a in range(2):
                        mm = nc.tensor.matmul(ps3[0:CH, a * T:(a + 1) * T], qlbd[u][:, a].rearrange("p h m -> p (h m)"), KT[u][:, a, :], start=True, stop=True)
                    mm.then_inc(l3_mm, 1)
                    pe.wait_ge(v_done, i + 2)
                    pe.wait_ge(cv_done, i + 1)
                    for a in range(2):
                        for s in range(3):
                            for hh in range(2):
                                h = a * HB + 2 * s + hh
                                for t, n0, n1 in reach:
                                    mm = nc.tensor.matmul(psC[32 * s:32 * s + 32, a * T + n0:a * T + n1], VZ[u][:, t, h, :],
                                                          toep[:, h, n0 - t * P + KS // 2:n1 - t * P + KS // 2],
                                                          start=(hh == 0 and t == 0), stop=(hh == 1), skip_group_check=True)
                    mm.then_inc(c_mm, 1)
                    pe.wait_ge(e3_done, i + 1)
                    for t in range(TI):
                        for a in range(2):
                            mm = nc.tensor.transpose(ps3[:, (2 * t + a) * CH:(2 * t + a + 1) * CH], A3[u][:, a, t * P:(t + 1) * P], ident[0:CH, 0:CH])
                    mm.then_inc(t3_mm, 1)
                    pe.wait_ge(p1_done, i + 1)
                    for a in range(2):
                        for t in range(TI):
                            mm = nc.tensor.transpose(ps1[0:CH, a * T + t * P:a * T + (t + 1) * P], A1[u][:, :, :].rearrange("p (t h) m -> p t (h m)", t=TI)[:, t, a * CH:(a + 1) * CH], ident[:, :])
                    mm.then_inc(t1_mm, 1)
                    pe.wait_ge(t3_done, i + 1)
                    for a in range(2):
                        for t in range(TI):
                            v = free(VZ[u][:, t, a * HB, 0:1], [4 * HD, HB // 2], [3 * HD, 2], [1, HD])
                            nc.tensor.matmul(ps3[0:CH, a * CH:(a + 1) * CH], A3T[u][:, t, a, :], v, start=(t == 0), stop=(t == 1))
                    for a in range(2):
                        mm = nc.tensor.matmul(ps3[0:CH, 2 * CH + a * LM:2 * CH + (a + 1) * LM], qlbd[u][:, a].rearrange("p h m -> p (h m)"), kl[u][:, a, :], start=True, stop=True)
                    mm.then_inc(k3_mm, 1)

        @block.scalar
        def _(act):
            act.wait_ge(c_in, 64)
            with images(act) as pair:
                for u in range(2):
                    nm.scalar(nc, act, pair + u, u)
                for u in range(2):
                    i = pair + u
                    for ps, dst, b0, mm_done, done in ((psQ, QT, 0, q_mm, q_done), (psK, KT, 2, k_mm, k_done)):
                        act.wait_ge(mm_done, i + 1)
                        if b0 == 0:
                            act.wait_ge(k3_done, i + 1)
                        for a in range(2):
                            ev = nc.scalar.activation(dst[u][:, a, :], ps[0:CH, a * T:(a + 1) * T], ACT.Identity, bias=qkb[:, b0 + a:b0 + a + 1])
                        ev.then_inc(done, 1)
                for u in range(2):
                    i = pair + u
                    act.wait_ge(z1_done, i + 1)
                    nc.scalar.activation(A1[u][:], A1[u][:], ACT.Exp).then_inc(e1_done, 1)
                    act.wait_ge(m3_done, i + 1)
                    for a in range(2):
                        ev = nc.scalar.activation(A3[u][:, a, :], ps3[0:CH, a * T:(a + 1) * T], ACT.Exp, bias=m3[u][:, a:a + 1], accum_out=d3[u][:, a:a + 1])
                    ev.then_inc(e3_done, 1)
                    wait_all(act, G["steady"], (c_mm, i + 1))
                    nc.scalar.activation(CV[:, :, bass.ds(i * T, T)], psC[0:CH, :].rearrange("p (a n) -> p a n", a=2), ACT.Copy).then_inc(cv_done, 1)
                    act.wait_ge(t3_mm, i + 1)
                    nc.scalar.activation(A3T[u][:], ps3[:, 0:4 * CH].rearrange("p (t a c) -> p t a c", t=TI, a=2), ACT.Copy).then_inc(t3_done, 1)
                    wait_all(act, G["steady"], (t1_mm, i + 1))
                    nc.scalar.activation(K1T[:, :, bass.ds(i * T, T)], ps1[0:CH, :].rearrange("p (a n) -> p a n", a=2), ACT.Copy).then_inc(ms_done, 1)

        @block.vector
        def _(dve):
            dve.sem_inc(ms_done, 1)
            dve.wait_ge(c_in, 64)
            dve.wait_ge(cleared, 2)
            nc.vector.tensor_scalar(hms[:, :], hm[:, :], 1.0 / (SEG * HD ** 0.5), None, ALU.mult).then_inc(cleared, 1)
            dve.wait_ge(cleared, 3)
            with images(dve) as pair:
                for u in range(2):
                    nm.vector(nc, dve, pair + u, u)
                for u in range(2):
                    i = pair + u
                    dve.wait_ge(nm.xT_free, i + 3)
                    for hh in range(2):
                        for t in range(TI):
                            ins = nc.vector.tensor_tensor(VZ[u][:, t, hh::2, hh * HD:(hh + 1) * HD],
                                                          psV[:, t * C:(t + 1) * C].rearrange("p (s h d) -> p s h d", s=HB, h=2)[:, :, hh, :],
                                                          vb[:, :].rearrange("p (s h d) -> p s h d", s=HB, h=2)[:, :, hh, :], ALU.add)
                    ins.then_inc(v_done, 1)
                    dve.wait_ge(q_done, i + 2)
                    dve.wait_ge(k_done, i + 2)
                    nc.vector.tensor_reduce(sums[u][:, 0], QT[u][:].rearrange("p a (m s) -> p a m s", m=LM), AX.X, ALU.add)
                    nc.vector.tensor_reduce(sums[u][:, 1], KT[u][:].rearrange("p a (m s) -> p a m s", m=LM), AX.X, ALU.add).then_inc(sum_done, 1)
                    dve.wait_ge(sum_done, i + 1)
                    nc.vector.tensor_scalar(kl[u][:], sums[u][:, 1], 1.0 / SEG, None, ALU.mult).then_inc(lm_done, 1)
                    for k, dst in ((0, qlbd), (1, klbd)):
                        nc.vector.tensor_tensor(dst[u][:], free(sums[u][:, k, 0, 0:1], [LM, 2], [0, HB], [1, LM]), free(hms[:, 0:1], [0, 2], [1, HB], [0, LM]), ALU.mult).then_inc(lm_done, 1)
                for u in range(2):
                    i = pair + u
                    dve.wait_ge(l1_mm, i + 1)
                    logits = ps1[:, 0:TI * C].rearrange("p (g m) -> p g m", m=LM)
                    nc.vector.tensor_reduce(m1[u][:, :], logits, AX.X, ALU.max).then_inc(m1_done, 1)
                    dve.wait_ge(m1_done, i + 1)
                    nc.vector.tensor_tensor(A1[u][:], logits, free(m1[u][:, 0:1], [1, TI * NH], [0, LM]), ALU.subtract).then_inc(z1_done, 1)
                    dve.wait_ge(l3_mm, i + 1)
                    nc.vector.tensor_reduce(m3[u][:, :], ps3[0:CH, :].rearrange("p (a n) -> p a n", a=2), AX.X, ALU.max, negate=True).then_inc(m3_done, 1)
                    dve.wait_ge(e1_done, i + 1)
                    nc.vector.tensor_reduce(d1[u][:, :], A1[u][:], AX.X, ALU.add).then_inc(d1_done, 1)
                    dve.wait_ge(d1_done, i + 1)
                    nc.vector.reciprocal(r1[u][:, :], d1[u][:, :]).then_inc(r1_done, 1)
                    dve.wait_ge(e3_done, i + 1)
                    nc.vector.reciprocal(r3[u][:, :], d3[u][:, :]).then_inc(r3_done, 1)
                    dve.wait_ge(r3_done, i + 1)
                    dve.wait_ge(k3_mm, i + 1)
                    for a in range(2):
                        nc.vector.scalar_tensor_tensor(K3[:, bass.ds(2 * i + a, 1), :].rearrange("p a (h d) -> p (a h) d", h=HB), ps3[0:CH, a * CH:(a + 1) * CH].rearrange("p (h d) -> p h d", h=HB),
                                                       r3[u][:, a:a + 1], free(hm[:, 0:1], [1, HB], [0, HD]), ALU.mult, ALU.mult)
                    nc.vector.tensor_copy(K2L[:, bass.ds(2 * i, 2), :], ps3[0:CH, 2 * CH:2 * CH + 2 * LM].rearrange("p (a m) -> p a m", a=2)).then_inc(k3_done, 1)


def l2_inverse(nc, G, consts):
    with Stage(nc, "l2i") as st:
        hm, bones = st.sb("hm", [CH, HB]), st.sb("bones", [CH, CH])
        eyes = st.sb("eyes", [CH, 3, CH])
        K2L, K3, MB = G["K2L"], G["K3"], G["MB"]
        mx, den, inv = st.sb("mx", [CH, NG]), st.sb("den", [CH, NG]), st.sb("inv", [CH, NG])
        big = lambda name: st.sb(name, [CH, NG, CH])
        K2, K2T, AT, D7, D15, D13, Vm, VT = (big(n) for n in ("K2", "K2T", "AT", "D7", "D15", "D13", "Vm", "VT"))
        ps = [st.ps(f"ps{b}") for b in range(8)]
        c_in, sm, exp_done, col_mm, col_done, bd_done, k2t_mm, k2t_done, start_done = st.sems("c_in sm exp_done col_mm col_done bd_done k2t_mm k2t_done start_done")
        a_mm, at_mm, at_done, d7_done, b_mm, d15_done, c_mm, d13_done, v_mm, vt_mm, v_done, vt_done = st.sems(
            "a_mm at_mm at_done d7_done b_mm d15_done c_mm d13_done v_mm vt_mm v_done vt_done")
        mb_mm, mb_done = st.sems("mb_mm mb_done")
        block = st.block()
        GB = 4
        NBK = NG // GB
        bank = lambda b: ps[b][0:CH, 0:GB * CH].rearrange("p (g c) -> p g c", g=GB)
        gs = lambda b: slice(b * GB, (b + 1) * GB)
        ITERATIONS = 6

        @block.sync
        def _(sp):
            sp.dma_start(hm[:, :], consts["headmask"]).then_inc(c_in, 16)
            sp.dma_start(bones[:, :], consts["blockones"]).then_inc(c_in, 16)
            sp.dma_start(eyes[:], consts["eyes"]).then_inc(c_in, 16)

        def product(pe, b0, lhs, rhs, gate, gate_at, done):
            for b in range(NBK):
                for s, at in zip(gate, gate_at):
                    pe.wait_ge(s, at + b)
                for g in range(b * GB, (b + 1) * GB):
                    mm = nc.tensor.matmul(ps[b0 + b][0:CH, (g % GB) * CH:(g % GB + 1) * CH], lhs[:, g, :], rhs[:, g, :], start=True, stop=True)
                mm.then_inc(done, 1)

        @block.tensor
        def _(pe):
            pe.wait_ge(c_in, 48)
            pe.wait_ge(sm, 5)
            nc.tensor.matmul(ps[0][0:CH, 0:NG * LM], bones[:, :], K2L[:].rearrange("p g m -> p (g m)"), start=True, stop=True).then_inc(col_mm, 1)
            pe.wait_ge(bd_done, 1)
            for b in range(NBK):
                for g in range(b * GB, (b + 1) * GB):
                    mm = nc.tensor.transpose(ps[4 + b][0:CH, (g % GB) * CH:(g % GB + 1) * CH], K2[:, g, :], G["ident"][0:CH, 0:CH])
                mm.then_inc(k2t_mm, 1)
            with pe.Fori(0, ITERATIONS) as it:
                product(pe, 0, K2T, Vm, (v_done, vt_done), (4 * it + 1, 4 * it + 1), a_mm)
                product(pe, 4, Vm, K2T, (vt_done,), (4 * it + 1,), at_mm)
                product(pe, 0, AT, D7, (at_done, d7_done), (4 * it + 1, 4 * it + 1), b_mm)
                product(pe, 4, AT, D15, (d15_done,), (4 * it + 1,), c_mm)
                product(pe, 0, VT, D13, (d13_done,), (4 * it + 1,), v_mm)
                product(pe, 4, D13, VT, (d13_done,), (4 * it + 1,), vt_mm)
            product(pe, 0, VT, K3, (v_done, vt_done), (4 * ITERATIONS + 1, 4 * ITERATIONS + 1), mb_mm)

        @block.scalar
        def _(act):
            act.wait_ge(sm, 2)
            nc.scalar.activation(K2L[:], K2L[:], ACT.Exp).then_inc(exp_done, 1)
            for b in range(NBK):
                act.wait_ge(k2t_mm, b + 1)
                nc.scalar.activation(K2T[:, gs(b), :], bank(4 + b), ACT.Copy).then_inc(k2t_done, 1)
            with act.Fori(0, ITERATIONS) as it:
                for b in range(NBK):
                    act.wait_ge(at_mm, 4 * it + b + 1)
                    nc.scalar.activation(AT[:, gs(b), :], bank(4 + b), ACT.Copy).then_inc(at_done, 1)
                for b in range(NBK):
                    act.wait_ge(vt_mm, 4 * it + b + 1)
                    nc.scalar.activation(VT[:, gs(b), :], bank(4 + b), ACT.Copy, scale=0.25).then_inc(vt_done, 1)
            for b in range(2):
                act.wait_ge(mb_mm, b + 1)
                nc.scalar.activation(MB[:, gs(b), :], bank(b), ACT.Copy).then_inc(mb_done, 1)

        @block.vector
        def _(dve):
            nc.vector.tensor_reduce(mx[:, :], K2L[:], AX.X, ALU.max).then_inc(sm, 1)
            dve.wait_ge(sm, 1)
            nc.vector.tensor_tensor(K2L[:], K2L[:], free(mx[:, 0:1], [1, NG], [0, LM]), ALU.subtract).then_inc(sm, 1)
            dve.wait_ge(exp_done, 1)
            nc.vector.tensor_reduce(den[:, :], K2L[:], AX.X, ALU.add).then_inc(sm, 1)
            dve.wait_ge(sm, 3)
            nc.vector.reciprocal(inv[:, :], den[:, :]).then_inc(sm, 1)
            dve.wait_ge(sm, 4)
            nc.vector.tensor_tensor(K2L[:], K2L[:], free(inv[:, 0:1], [1, NG], [0, LM]), ALU.mult).then_inc(sm, 1)
            dve.wait_ge(sm, 5)
            dve.wait_ge(c_in, 48)
            nc.vector.tensor_tensor(K2[:].rearrange("p g (h m) -> p g h m", h=HB), free(K2L[:, 0, 0:1], [LM, NG], [0, HB], [1, LM]),
                                    free(hm[:, 0:1], [0, NG], [1, HB], [0, LM]), ALU.mult).then_inc(bd_done, 1)
            dve.wait_ge(col_mm, 1)
            nc.vector.tensor_reduce(mx[:, :], ps[0][0:CH, 0:NG * LM].rearrange("p (g m) -> p g m", m=LM), AX.X, ALU.max).then_inc(col_done, 1)
            dve.wait_ge(col_done, 1)
            nc.vector.reciprocal(inv[:, :], mx[:, :]).then_inc(col_done, 1)
            dve.wait_ge(col_done, 2)
            dve.wait_ge(bd_done, 1)
            for b in range(NBK):
                scale = free(inv[:, b * GB:b * GB + 1], [1, GB], [0, CH])
                nc.vector.tensor_tensor(VT[:, gs(b), :], K2[:, gs(b), :], scale, ALU.mult).then_inc(vt_done, 1)
                dve.wait_ge(k2t_done, b + 1)
                nc.vector.tensor_tensor(Vm[:, gs(b), :], K2T[:, gs(b), :], scale, ALU.mult).then_inc(v_done, 1)

            def minus(dst, b0, k, gate, at, done):
                for b in range(NBK):
                    dve.wait_ge(gate, at + b)
                    nc.vector.scalar_tensor_tensor(dst[:, gs(b), :], bank(b0 + b), -1.0, free(eyes[:, k, 0:1], [0, GB], [1, CH]), ALU.mult, ALU.add).then_inc(done, 1)

            with dve.Fori(0, ITERATIONS) as it:
                minus(D7, 0, 0, a_mm, 4 * it + 1, d7_done)
                minus(D15, 0, 2, b_mm, 4 * it + 1, d15_done)
                minus(D13, 4, 1, c_mm, 4 * it + 1, d13_done)
                for b in range(NBK):
                    dve.wait_ge(v_mm, 4 * it + b + 1)
                    dve.wait_ge(vt_mm, 4 * it + b + 1)
                    nc.vector.tensor_scalar(Vm[:, gs(b), :], bank(b), 0.25, None, ALU.mult).then_inc(v_done, 1)
            for b in range(2, NBK):
                dve.wait_ge(mb_mm, b + 1)
                nc.vector.tensor_copy(MB[:, gs(b), :], bank(b)).then_inc(mb_done, 1)


def l2_output(nc, G, w):
    with Stage(nc, "l2o") as st:
        Wo, bo = st.sb("Wo", [CH, 2, C]), st.sb("bo", [P, C])
        M = [st.sb(f"M{u}", [CH, 2, CH]) for u in range(2)]
        XO = [st.sb(f"XO{u}", [CH, 2, T]) for u in range(2)]
        stats = LnStats(st, G, 1e-5)
        psO, psY = [st.ps(f"psO{u}") for u in range(2)], [st.ps(f"psY{u}") for u in range(2)]
        c_in, m_done, o_mm, o_done, y_mm, x_biased, x_done = st.sems("c_in m_done o_mm o_done y_mm x_biased x_done")
        block = st.block()

        @block.sync
        def _(sp):
            sp.dma_start(Wo[:, :, :], w["Wo"].rearrange("(k p) n -> p k n", p=CH)).then_inc(c_in, 16)
            sp.dma_start(bo[:, :], rows(w["bo"], 0, [0, P], [1, C])).then_inc(c_in, 16)

        @block.gpsimd
        def _(pool):
            stats.init(pool)
            pool.wait_ge(c_in, 32)
            with images(pool) as pair:
                for u in range(2):
                    i = pair + u
                    wait_all(pool, G["steady"], (o_mm, i + 1))
                    nc.gpsimd.tensor_copy(M[u][:], G["MB"][:, bass.ds(2 * i, 2), :]).then_inc(m_done, 1)
                    X = G["X"][:, bass.ds(TI * i, TI), :]
                    nc.gpsimd.tensor_tensor(X, X, free(bo[:, 0:1], [0, TI], [1, C]), ALU.add).then_inc(x_biased, 1)
                for u in range(2):
                    stats.gpsimd(nc, pool, pair + u, u)

        @block.tensor
        def _(pe):
            for s in (o_mm, o_done, x_done):
                pe.sem_inc(s, 2)
            pe.wait_ge(c_in, 32)
            with images(pe) as pair:
                for u in range(2):
                    i = pair + u
                    pe.wait_ge(m_done, i + 1)
                    pe.wait_ge(o_done, i + 1)
                    for a in range(2):
                        mm = nc.tensor.matmul(psO[u][0:CH, a * T:(a + 1) * T], M[u][:, a, :], G["K1T"][:, bass.ds(a, 1), bass.ds(i * T, T)].rearrange("p a n -> p (a n)"), start=True, stop=True)
                    mm.then_inc(o_mm, 1)
                for u in range(2):
                    i = pair + u
                    pe.wait_ge(o_done, i + 3)
                    pe.wait_ge(x_done, i + 1)
                    for t in range(TI):
                        for a in range(2):
                            mm = nc.tensor.matmul(psY[u][:, t * C:(t + 1) * C], XO[u][:, a, t * P:(t + 1) * P], Wo[:, a, :], start=(a == 0), stop=(a == 1))
                    mm.then_inc(y_mm, 1)

        @block.vector
        def _(dve):
            dve.sem_inc(y_mm, 2)
            with images(dve) as pair:
                for u in range(2):
                    i = pair + u
                    dve.wait_ge(o_mm, i + 3)
                    dve.wait_ge(y_mm, i + 1)
                    nc.vector.tensor_tensor(XO[u][:], psO[u][0:CH, :].rearrange("p (a n) -> p a n", a=2), G["CV"][:, :, bass.ds(i * T, T)], ALU.add).then_inc(o_done, 1)
                for u in range(2):
                    i = pair + u
                    dve.wait_ge(y_mm, i + 3)
                    dve.wait_ge(x_biased, i + 1)
                    X = G["X"][:, bass.ds(TI * i, TI), :]
                    nc.vector.tensor_tensor(X, psY[u][:, 0:TI * C].rearrange("p (t c) -> p t c", t=TI), X, ALU.add).then_inc(x_done, 1)
                    stats.vector(nc, dve, i, u, (x_done, i + 3))



E = 8
FI = 512
SLOT_TILES = -(-(2 * B * T + E * (P - 1)) // (2 * P)) * 2
CAP = B * T // E


def route(nc, G, name, w_router, transposed, top, n_slots, side=None):
    with Stage(nc, name) as st:
        RW = st.sb("RW", [CH, 2, E])
        XN = st.sb("XN", [P, NT, C])
        ones, tri = st.sb("ones", [P, P]), st.sb("tri", [P, P])
        desc, tiles_at, rowid = st.sb("desc", [P, E]), st.sb("tiles_at", [P, SLOT_TILES]), st.sb("rowid", [P, NT])
        grid = lambda name, dt=F32: st.sb(name, [P, NT, E], dt)
        L, Pb, Z, W, EQ = grid("L"), grid("Pb"), grid("Z"), grid("W"), grid("EQ")
        M = [grid(f"M{k}") for k in range(top)]
        MT, RK = grid("MT"), grid("RK")
        scan_t = [grid("scan0"), grid("scan1")]
        small = lambda name, n=NT, dt=F32: st.sb(name, [P, n], dt)
        m, den, best = small("m"), small("den"), small("best")
        gk = [small(f"gk{k}") for k in range(top)]
        slot, keep = small("slot"), small("keep")
        imp, bal, cnt = small("imp", E), small("bal", E), small("cnt", E)
        cnt_i, scan_e = small("cnt_i", E, I32), [small("scan_e0", E), small("scan_e1", E)]
        te, te_cmp = small("te", SLOT_TILES), st.sb("te_cmp", [P, SLOT_TILES, E])
        nm = Normed(st, G)
        psL = [st.ps(f"psL{u}") for u in range(2)]
        psI, psP = st.ps("psI"), st.ps("psP")
        c_in, l_mm, l_done, x_kept, exp_done, d, imp_mm, pre_mm, slot_done, scattered, chain, zero_out = st.sems(
            "c_in l_mm l_done x_kept exp_done probs imp_mm pre_mm slot_done scattered chain zero_out")
        extra = side(st) if side else None
        block = st.block()
        flat = lambda g: g[:].rearrange("p t e -> p (t e)")

        @block.sync
        def _(sp):
            if transposed:
                for k in range(2):
                    sp.dma_start(RW[:, k, :], rows(w_router, k * CH, [1, CH], [C, E]), allow_slow_non_contiguous=True).then_inc(c_in, 16)
            else:
                for k in range(2):
                    sp.dma_start(RW[:, k, :], w_router[k * CH:(k + 1) * CH, :]).then_inc(c_in, 16)
            for dst, src in ((ones, "ones"), (tri, "tri"), (desc, "desc"), (tiles_at, "tiles_at"), (rowid, "rowid")):
                sp.dma_start(dst[:, :], G["consts"][src]).then_inc(c_in, 16)
            for r in range(0, n_slots, n_slots // 4):
                sp.dma_start(rows(G["xs"], r * C, [8 * C, n_slots // 32], [1, 8 * C]), rows(G["consts"]["zeros"], 0, [0, n_slots // 32], [1, 8 * C])).then_inc(zero_out, 16)
            if extra:
                extra.sync(sp)

        @block.gpsimd
        def _(pool):
            with images(pool) as pair:
                for u in range(2):
                    i = pair + u
                    wait_all(pool, G["steady"], (nm.normed, TI * (i + 1)))
                    nc.gpsimd.tensor_copy(XN[:, bass.ds(TI * i, TI), :], nm.xn[:, u]).then_inc(x_kept, 1)
            pool.wait_ge(x_kept, B + 2)
            pool.wait_ge(zero_out, 64)
            for k in range(top):
                pool.wait_ge(slot_done, k + 1)
                for t in range(NT):
                    pool.indirect_dma_start(out=G["xs"], out_offset=bass.IndirectOffsetOnAxis(ap=G["slots"][k][:, t:t + 1], axis=0),
                                            in_=XN[:, t, :], in_offset=None).then_inc(scattered, 16)
            pool.wait_ge(scattered, 16 * NT * top)

        @block.tensor
        def _(pe):
            nm.init_credit(pe)
            pe.sem_inc(l_done, 2)
            pe.wait_ge(c_in, 16 * 7)
            with images(pe) as pair:
                for u in range(2):
                    nm.tensor(nc, pe, pair + u, u)
                for u in range(2):
                    i = pair + u
                    pe.wait_ge(nm.xT_done, i + 3)
                    pe.wait_ge(l_done, i + 1)
                    for t in range(TI):
                        for k in range(2):
                            mm = nc.tensor.matmul(psL[u][:, t * E:(t + 1) * E], nm.xT[u][:, k, t * P:(t + 1) * P], RW[:, k, :], start=(k == 0), stop=(k == 1))
                    mm.then_inc(nm.xT_free, 1)
            if top == 2:
                pe.wait_ge(d, 1)
                nc.tensor.matmul(psI[:, 0:NT * E], ones[:, :], flat(Pb), start=True, stop=True).then_inc(imp_mm, 1)
            pe.wait_ge(d, 2)
            nc.tensor.matmul(psP[:, 0:NT * E], tri[:, :], flat(MT), start=True, stop=True)
            nc.tensor.matmul(psP[:, NT * E:2 * NT * E], ones[:, :], flat(MT), start=True, stop=True).then_inc(pre_mm, 1)
            if extra:
                extra.tensor(pe)

        @block.scalar
        def _(act):
            with images(act) as pair:
                for u in range(2):
                    nm.scalar(nc, act, pair + u, u)
            act.wait_ge(chain, 2)
            nc.scalar.activation(flat(Z), flat(Z), ACT.Exp).then_inc(exp_done, 1)
            if extra:
                extra.scalar(act)

        @block.vector
        def _(dve):
            dve.sem_inc(x_kept, 2)
            with images(dve) as pair:
                for u in range(2):
                    dve.wait_ge(x_kept, pair + u + 1)
                    nm.vector(nc, dve, pair + u, u)
                for u in range(2):
                    i = pair + u
                    dve.wait_ge(nm.xT_free, i + 3)
                    nc.vector.tensor_copy(L[:, bass.ds(TI * i, TI), :], psL[u][:, 0:TI * E].rearrange("p (t e) -> p t e", t=TI)).then_inc(l_done, 1)
            dve.wait_ge(l_done, B + 2)
            dve.wait_ge(c_in, 16 * 7)
            steps = [0]

            def link(ins):
                steps[0] += 1
                ins.then_inc(chain, 1)
                dve.wait_ge(chain, steps[0])

            V = nc.vector
            over_e = lambda v: free(v[:, 0:1], [1, NT], [0, E])
            over_t = lambda v: free(v[:, 0:1], [0, NT], [1, E])
            link(V.tensor_reduce(m[:, :], L[:], AX.X, ALU.max))
            link(V.tensor_tensor(Z[:], L[:], over_e(m), ALU.subtract))
            dve.wait_ge(exp_done, 1)
            link(V.tensor_reduce(den[:, :], Z[:], AX.X, ALU.add))
            link(V.reciprocal(den[:, :], den[:, :]))
            V.tensor_tensor(Pb[:], Z[:], over_e(den), ALU.mult).then_inc(d, 1)
            dve.wait_ge(d, 1)
            src = Pb
            for k in range(top):
                link(V.tensor_reduce(best[:, :], src[:], AX.X, ALU.max))
                link(V.tensor_tensor(EQ[:], src[:], over_e(best), ALU.is_equal))
                link(V.tensor_tensor(W[:], EQ[:], over_t(desc), ALU.mult))
                link(V.tensor_reduce(m[:, :], W[:], AX.X, ALU.max))
                link(V.tensor_tensor(M[k][:], W[:], over_e(m), ALU.is_equal))
                if k + 1 < top:
                    link(V.scalar_tensor_tensor(W[:], M[k][:], -2.0, Pb[:], ALU.mult, ALU.add))
                    link(V.tensor_copy(Z[:], W[:]))
                    src = Z
            if top == 2:
                V.tensor_tensor(MT[:], M[0][:], M[1][:], ALU.add).then_inc(d, 1)
                dve.wait_ge(imp_mm, 1)
                link(V.tensor_reduce(imp[:, :], psI[:, 0:NT * E].rearrange("p (t e) -> p e t", t=NT), AX.X, ALU.add))
                link(V.tensor_scalar(bal[:, :], imp[:, :], 1.0, 1.0 - 0.9, ALU.subtract, ALU.mult))
                link(V.tensor_scalar(bal[:, :], bal[:, :], 1.0, None, ALU.add))
                link(V.tensor_scalar(bal[:, :], bal[:, :], 0.01, None, ALU.add))
                link(V.reciprocal(bal[:, :], bal[:, :]))
                link(V.tensor_tensor(Pb[:], Pb[:], over_t(bal), ALU.mult))
                for k in range(2):
                    link(V.tensor_tensor(W[:], Pb[:], M[k][:], ALU.mult))
                    link(V.tensor_reduce(gk[k][:, :], W[:], AX.X, ALU.add))
                link(V.tensor_tensor(den[:, :], gk[0][:, :], gk[1][:, :], ALU.add))
                link(V.reciprocal(den[:, :], den[:, :]))
                for k in range(2):
                    link(V.tensor_tensor(G["gates"][k][:, :], gk[k][:, :], den[:, :], ALU.mult))
            else:
                V.tensor_copy(MT[:], M[0][:]).then_inc(d, 1)

            def scan(bufs, n, at):
                k, s = 0, 1
                while s < n:
                    V.tensor_copy(at(bufs[1 - k], 0, s), at(bufs[k], 0, s))
                    link(V.tensor_tensor(at(bufs[1 - k], s, n), at(bufs[k], s, n), at(bufs[k], 0, n - s), ALU.add))
                    k, s = 1 - k, 2 * s
                return bufs[k]

            dve.wait_ge(pre_mm, 1)
            totals = psP[:, NT * E:2 * NT * E].rearrange("p (t e) -> p t e", t=NT)
            link(V.tensor_copy(scan_t[0][:], totals))
            upto = scan(scan_t, NT, lambda b, lo, hi: b[:, lo:hi, :])
            link(V.tensor_tensor(RK[:], upto[:], totals, ALU.subtract))
            link(V.tensor_tensor(RK[:], RK[:], psP[:, 0:NT * E].rearrange("p (t e) -> p t e", t=NT), ALU.add))
            if top == 2:
                link(V.tensor_scalar(cnt[:, :], upto[:, NT - 1, :], float(P - 1), None, ALU.add))
                link(V.tensor_copy(cnt_i[:, :], cnt[:, :]))
                link(V.tensor_scalar(cnt_i[:, :], cnt_i[:, :], 7, None, ALU.arith_shift_right))
                link(V.tensor_copy(cnt[:, :], cnt_i[:, :]))
                link(V.tensor_copy(scan_e[0][:, :], cnt[:, :]))
                ends = scan(scan_e, E, lambda b, lo, hi: b[:, lo:hi])
                link(V.tensor_tensor(te_cmp[:], free(tiles_at[:, 0:1], [1, SLOT_TILES], [0, E]), free(ends[:, 0:1], [0, SLOT_TILES], [1, E]), ALU.is_ge))
                link(V.tensor_reduce(te[:, :], te_cmp[:], AX.X, ALU.add))
                link(V.tensor_scalar(te[:, :], te[:, :], float(E - 1), None, ALU.min))
                link(V.tensor_copy(G["tile_expert"][:, :], te[:, :]))
                link(V.tensor_tensor(bal[:, :], ends[:, :], cnt[:, :], ALU.subtract))
                link(V.tensor_scalar(bal[:, :], bal[:, :], float(P), -1.0, ALU.mult, ALU.add))
                link(V.tensor_tensor(RK[:], RK[:], over_t(bal), ALU.add))
                for k in range(2):
                    link(V.tensor_tensor(W[:], RK[:], M[k][:], ALU.mult))
                    link(V.tensor_reduce(slot[:, :], W[:], AX.X, ALU.add))
                    V.tensor_copy(G["slots"][k][:, :], slot[:, :]).then_inc(slot_done, 1)
                    dve.wait_ge(slot_done, k + 1)
            else:
                link(V.tensor_tensor(W[:], RK[:], M[0][:], ALU.mult))
                link(V.tensor_reduce(slot[:, :], W[:], AX.X, ALU.add))
                link(V.tensor_scalar(keep[:, :], slot[:, :], float(CAP), None, ALU.is_lt))
                link(V.tensor_scalar(m[:, :], m[:, :], -float(CAP), float(CAP * E), ALU.mult, ALU.add))
                link(V.tensor_tensor(slot[:, :], slot[:, :], m[:, :], ALU.add))
                link(V.tensor_tensor(G["gates"][0][:, :], best[:, :], keep[:, :], ALU.mult))
                link(V.tensor_tensor(slot[:, :], slot[:, :], keep[:, :], ALU.mult))
                link(V.tensor_copy(G["slots"][1][:, :], slot[:, :]))
                link(V.tensor_scalar(keep[:, :], keep[:, :], -1.0, 1.0, ALU.mult, ALU.add))
                link(V.tensor_tensor(keep[:, :], keep[:, :], rowid[:, :], ALU.mult))
                link(V.tensor_tensor(slot[:, :], slot[:, :], keep[:, :], ALU.add))
                V.tensor_copy(G["slots"][0][:, :], slot[:, :]).then_inc(slot_done, 1)
            if extra:
                extra.vector(dve)


class ExpertWeights:

    NM = FI // P

    def __init__(self, nc, G, w1, w2):
        self.nc, self.G, self.w1, self.w2 = nc, G, w1, w2

    def __call__(self, st):
        NM = self.NM
        self.raw1 = [st.sb(f"raw1{b}", [P, NM, C]) for b in range(2)]
        self.raw2 = [st.sb(f"raw2{b}", [CH, 2, FI]) for b in range(2)]
        self.ps1 = [st.ps(f"psw{b}") for b in range(2)]
        self.raw_in = [st.sem(f"raw_in{b}") for b in range(2)]
        self.turned, self.kept, self.raw_free = st.sems("w_turned w_kept raw_free")
        return self

    def sync(self, sp):
        for e in range(E):
            b = e % 2
            if e >= 2:
                sp.wait_ge(self.turned, 4 * (e - 1))
            sp.dma_start(self.raw1[b][:], rows(self.w1, e * FI * C, [C, P], [P * C, self.NM], [1, C])).then_inc(self.raw_in[b], 16)
            sp.dma_start(self.raw2[b][:], rows(self.w2, e * C * FI, [FI, CH], [CH * FI, 2], [1, FI])).then_inc(self.raw_in[b], 16)

    def tensor(self, pe):
        n = 0
        for e in range(E):
            b = e % 2
            pe.wait_ge(self.raw_in[b], 32 * (e // 2 + 1))
            for part in range(4):
                if n >= 2:
                    pe.wait_ge(self.kept, n - 1)
                ps = self.ps1[n % 2]
                for mb in range(self.NM):
                    if part < 2:
                        mm = self.nc.tensor.transpose(ps[0:CH, mb * P:(mb + 1) * P], self.raw1[b][:, mb, part * CH:(part + 1) * CH], self.G["ident"][:, :])
                    else:
                        mm = self.nc.tensor.transpose(ps[:, mb * CH:(mb + 1) * CH], self.raw2[b][:, part - 2, mb * P:(mb + 1) * P], self.G["ident"][0:CH, 0:CH])
                mm.then_inc(self.turned, 1)
                n += 1

    def scalar(self, act):
        for n in range(4 * E):
            e, part = n // 4, n % 4
            act.wait_ge(self.turned, n + 1)
            if part < 2:
                dst, src = self.G["W1T"][:, part, e * FI:(e + 1) * FI], self.ps1[n % 2][0:CH, :]
            else:
                dst = self.G["W2T"][:, e * self.NM:(e + 1) * self.NM, (part - 2) * CH:(part - 1) * CH]
                src = self.ps1[n % 2][:, 0:self.NM * CH].rearrange("p (m c) -> p m c", m=self.NM)
            self.nc.scalar.activation(dst, src, ACT.Copy).then_inc(self.kept, 1)

    def vector(self, dve):
        pass


def slots_of_tiles(eng, slot):
    for s in range(-3, 0):
        slot(0, s, lambda ahead: s + ahead >= 0)
    with eng.Fori(0, SLOT_TILES // 2 - 2) as pair:
        for s in range(2):
            slot(pair, s, lambda ahead: True)
    for s in range(4):
        slot(SLOT_TILES // 2 - 2, s, lambda ahead: s + ahead < 4)


def experts_any(nc, G):
    with Stage(nc, "l2e") as st:
        NM = FI // P
        two = lambda name, shape: [st.sb(f"{name}{b}", shape) for b in range(2)]
        X, XT, H, HT, Y = two("X", [P, C]), two("XT", [CH, 2, P]), two("H", [P, FI]), two("HT", [P, NM, P]), two("Y", [P, C])
        psX, psH, psT, psY = ([st.ps(f"{n}{b}") for b in range(2)] for n in ("psX", "psH", "psT", "psY"))
        x_in, y_out = st.sems("x_in0 x_in1"), st.sems("y_out0 y_out1")
        xt_mm, xt_done, h_mm, h_done, ht_mm, ht_done, y_mm, y_done = st.sems("xt_mm xt_done h_mm h_done ht_mm ht_done y_mm y_done")
        block = st.block()
        PAIRS = SLOT_TILES // 2

        @block.sync
        def _(sp):
            of_tile = lambda buf, j: image_of(buf.rearrange("(j n) c -> j (n c)", n=P), j, 0, [C, P], [1, C])

            def load(pair):
                for b in range(2):
                    sp.wait_ge(xt_mm, pair * 2 + b + 1)
                    sp.dma_start(X[b][:, :], of_tile(G["xs"], pair * 2 + b)).then_inc(x_in[b], 16)

            def store(pair):
                for b in range(2):
                    sp.wait_ge(y_done, pair * 2 + b + 1)
                    sp.dma_start(of_tile(G["ys"], pair * 2 + b), Y[b][:, :]).then_inc(y_out[b], 16)

            for b in range(2):
                sp.sem_inc(y_out[b], 16)
            load(0)
            load(1)
            with sp.Fori(0, PAIRS - 2) as pair:
                load(pair + 2)
                store(pair)
            store(PAIRS - 2)
            store(PAIRS - 1)
            for b in range(2):
                sp.wait_ge(y_out[b], 16 * (PAIRS + 1))

        @block.tensor
        def _(pe):
            for s in (xt_mm, xt_done, h_mm, h_done, ht_mm, ht_done, y_mm):
                pe.sem_inc(s, 2)

            def expert(j):
                return pe.value_load(G["tile_expert"][0:1, bass.ds(j, 1)], min_val=0, max_val=E - 1)

            def turn_tokens(p, s):
                j, b = p * 2 + s, s % 2
                pe.wait_ge(x_in[b], (p + s // 2) * 16 + 16)
                pe.wait_ge(xt_done, j + 1)
                for k in range(2):
                    mm = nc.tensor.transpose(psX[b][0:CH, k * P:(k + 1) * P], X[b][:, k * CH:(k + 1) * CH], G["ident"][:, :])
                mm.then_inc(xt_mm, 1)

            def first_layer(p, s):
                j, b = p * 2 + s, s % 2
                e = expert(j)
                pe.wait_ge(xt_done, j + 3)
                pe.wait_ge(h_done, j + 1)
                for k in range(2):
                    mm = nc.tensor.matmul(psH[b][:, :], XT[b][:, k, :], G["W1T"][:, k, bass.ds(e * FI, FI)], start=(k == 0), stop=(k == 1))
                mm.then_inc(h_mm, 1)

            def turn_hidden(p, s):
                j, b = p * 2 + s, s % 2
                pe.wait_ge(h_done, j + 3)
                pe.wait_ge(ht_done, j + 1)
                for mb in range(NM):
                    mm = nc.tensor.transpose(psT[b][:, mb * P:(mb + 1) * P], H[b][:, mb * P:(mb + 1) * P], G["ident"][:, :])
                mm.then_inc(ht_mm, 1)

            def second_layer(p, s):
                j, b = p * 2 + s, s % 2
                e = expert(j)
                pe.wait_ge(ht_done, j + 3)
                for mb in range(NM):
                    mm = nc.tensor.matmul(psY[b][:, 0:C], HT[b][:, mb, :], G["W2T"][:, bass.ds(e * NM + mb, 1), :].rearrange("p a c -> p (a c)"), start=(mb == 0), stop=(mb == NM - 1))
                mm.then_inc(y_mm, 1)

            def slot(p, s, has):
                for ahead, step in ((3, turn_tokens), (2, first_layer), (1, turn_hidden), (0, second_layer)):
                    if has(ahead):
                        step(p, s + ahead)

            slots_of_tiles(pe, slot)

        @block.scalar
        def _(act):
            def slot(p, s, has):
                if has(2):
                    j, b = p * 2 + s + 2, s % 2
                    act.wait_ge(h_mm, j + 3)
                    act.wait_ge(ht_mm, j + 1)
                    nc.scalar.activation(H[b][:, :], psH[b][:, :], ACT.Silu).then_inc(h_done, 1)

            slots_of_tiles(act, slot)

        @block.vector
        def _(dve):
            def slot(p, s, has):
                if has(3):
                    j, b = p * 2 + s + 3, (s + 3) % 2
                    dve.wait_ge(xt_mm, j + 3)
                    dve.wait_ge(h_mm, j + 1)
                    nc.vector.tensor_copy(XT[b][:], psX[b][0:CH, 0:2 * P].rearrange("p (k n) -> p k n", k=2)).then_inc(xt_done, 1)
                if has(1):
                    j, b = p * 2 + s + 1, (s + 1) % 2
                    dve.wait_ge(ht_mm, j + 3)
                    dve.wait_ge(y_mm, j + 1)
                    nc.vector.tensor_copy(HT[b][:], psT[b][:, :].rearrange("p (m n) -> p m n", m=NM)).then_inc(ht_done, 1)
                if has(0):
                    j, b = p * 2 + s, s % 2
                    dve.wait_ge(y_mm, j + 3)
                    dve.wait_ge(y_out[b], (p + s // 2) * 16 + 16)
                    nc.vector.tensor_copy(Y[b][:, :], psY[b][:, 0:C]).then_inc(y_done, 1)

            slots_of_tiles(dve, slot)


class FirstExperts:

    def __init__(self, nc, ctx, w):
        two = lambda name, shape: [ctx.enter_context(nc.sbuf_tensor(f"expert_{name}{b}", shape, F32)) for b in range(2)]
        self.w = w
        self.W1, self.b1, self.W2, self.b2 = two("W1", [CH, 2, FF]), two("b1", [P, MF]), two("W2", [P, MF, C]), two("b2", [P, C])

    def load(self, eng, e, b, layer, done):
        w = self.w
        for dst, src, *dims in (((self.W1[b], w["w1"].rearrange("e d m -> e (d m)"), [FF, CH], [CH * FF, 2], [1, FF]), (self.b1[b], w["b1"], [1, P], [P, MF])),
                                ((self.W2[b], w["w2"].rearrange("e m d -> e (m d)"), [C, P], [P * C, MF], [1, C]), (self.b2[b], w["b2"], [0, P], [1, C])))[layer]:
            eng.dma_start(dst[:], image_of(src, e, 0, *dims), allow_slow_non_contiguous=True).then_inc(done, 16)

    def __call__(self, st):
        self.first_in, = st.sems("first_in")
        return self

    def sync(self, sp):
        for b in range(2):
            for layer in range(2):
                self.load(sp, b, b, layer, self.first_in)
        sp.wait_ge(self.first_in, 16 * 8)

    def tensor(self, pe):
        pass

    def scalar(self, act):
        pass

    def vector(self, dve):
        pass


def experts_each(nc, G, weights):
    with Stage(nc, "l3e") as st:
        two = lambda name, shape: [st.sb(f"{name}{b}", shape) for b in range(2)]
        X, XT, HT, Z, Y = two("X", [P, TI, C]), two("XT", [CH, 2, CAP]), two("HT", [P, MF, CAP]), two("Z", [P, TI, C]), two("Y", [P, TI, C])
        W1, b1, W2, b2 = weights.W1, weights.b1, weights.W2, weights.b2
        psX, psY = [st.ps(f"psX{b}") for b in range(2)], [st.ps(f"psY{b}") for b in range(2)]
        psH = [st.ps(f"psH{k}") for k in range(MF // 2)]
        x_in, w_in, y_out = st.sems("x_in0 x_in1"), st.sems("w_in0 w_in1"), st.sems("y_out0 y_out1")
        xt_mm, xt_done, h_mm, h_done, y_mm, z_done, y_done = st.sems("xt_mm xt_done h_mm h_done y_mm z_done y_done")
        H3 = MF // 2
        block = st.block()
        TC = CAP // P

        @block.sync
        def _(sp):
            of_expert = lambda buf, e, *dims: image_of(buf, e, 0, *dims)
            slots = lambda buf: buf.rearrange("(e n) c -> e (n c)", n=CAP)
            tiles = ([C, P], [P * C, TC], [1, C])

            def load_x(pair):
                for b in range(2):
                    sp.dma_start(X[b][:], of_expert(slots(G["xs"]), pair * 2 + b, *tiles)).then_inc(x_in[b], 16)

            def load(pair):
                for b in range(2):
                    sp.wait_ge(xt_mm, pair * 2 + b - 1)
                load_x(pair)
                for b in range(2):
                    e = pair * 2 + b
                    sp.wait_ge(h_done, H3 * e)
                    weights.load(sp, e, b, 0, w_in[b])
                for b in range(2):
                    e = pair * 2 + b
                    sp.wait_ge(z_done, e + 1)
                    weights.load(sp, e, b, 1, w_in[b])

            def store(pair):
                for b in range(2):
                    e = pair * 2 + b
                    sp.wait_ge(y_done, e + 3)
                    sp.dma_start(of_expert(slots(G["ys"]), e, *tiles), Y[b][:]).then_inc(y_out[b], 16)

            for b in range(2):
                sp.sem_inc(y_out[b], 16)
                sp.sem_inc(w_in[b], 64)
            load_x(0)
            with sp.Fori(0, E // 2 - 1) as pair:
                load(pair + 1)
                store(pair)
            store(E // 2 - 1)
            for b in range(2):
                sp.wait_ge(y_out[b], 16 * (E // 2 + 1))

        @block.tensor
        def _(pe):
            for s, k in ((xt_done, 2), (h_done, H3), (z_done, 2), (y_done, 2)):
                pe.sem_inc(s, k)

            def turn(pair):
                for b in range(2):
                    pe.wait_ge(x_in[b], pair * 16 + 16)
                    pe.wait_ge(xt_done, pair * 2 + b + 1)
                    for t in range(TC):
                        for k in range(2):
                            mm = nc.tensor.transpose(psX[b][0:CH, k * CAP + t * P:k * CAP + (t + 1) * P], X[b][:, t, k * CH:(k + 1) * CH], G["ident"][:, :])
                    mm.then_inc(xt_mm, 1)

            def layers(pair, last):
                for b in range(2):
                    e = pair * 2 + b
                    pe.wait_ge(xt_done, e + 3)
                    pe.wait_ge(w_in[b], pair * 64 + 64)
                    for k2 in range(H3):
                        pe.wait_ge(h_done, H3 * e + k2 + 1)
                        for m in (2 * k2, 2 * k2 + 1):
                            for k in range(2):
                                mm = nc.tensor.matmul(psH[k2][:, m % 2 * CAP:(m % 2 + 1) * CAP], W1[b][:, k, m * P:(m + 1) * P], XT[b][:, k, :], start=(k == 0), stop=(k == 1))
                        mm.then_inc(h_mm, 1)
                if not last:
                    turn(pair + 1)
                for b in range(2):
                    e = pair * 2 + b
                    pe.wait_ge(h_done, H3 * (e + 2))
                    pe.wait_ge(z_done, e + 1)
                    for t in range(TC):
                        for m in range(MF):
                            mm = nc.tensor.matmul(psY[b][:, t * C:(t + 1) * C], HT[b][:, m, t * P:(t + 1) * P], W2[b][:, m, :], start=(m == 0), stop=(m == MF - 1))
                    mm.then_inc(y_mm, 1)

            turn(0)
            with pe.Fori(0, E // 2 - 1) as pair:
                layers(pair, False)
            layers(E // 2 - 1, True)

        @block.scalar
        def _(act):
            with act.Fori(0, E // 2) as pair:
                for b in range(2):
                    e = pair * 2 + b
                    act.wait_ge(y_done, e + 1)
                    act.wait_ge(w_in[b], pair * 64 + 64)
                    for k2 in range(H3):
                        act.wait_ge(h_mm, H3 * e + k2 + 1)
                        for m in (2 * k2, 2 * k2 + 1):
                            ge = nc.scalar.activation(HT[b][:, m, :], psH[k2][:, m % 2 * CAP:(m % 2 + 1) * CAP], ACT.Gelu_apprx_tanh, bias=b1[b][:, m:m + 1])
                        ge.then_inc(h_done, 1)
                for b in range(2):
                    e = pair * 2 + b
                    act.wait_ge(z_done, e + 3)
                    act.wait_ge(y_out[b], pair * 16 + 16)
                    nc.scalar.activation(Y[b][:], Z[b][:], ACT.Gelu_apprx_tanh).then_inc(y_done, 1)

        @block.vector
        def _(dve):
            def copy(pair, first):
                for b in range(2):
                    e = pair * 2 + b
                    dve.wait_ge(xt_mm, e + 1)
                    if not first:
                        dve.wait_ge(h_mm, H3 * (e - 1))
                    nc.vector.tensor_copy(XT[b][:], psX[b][0:CH, 0:2 * CAP].rearrange("p (k n) -> p k n", k=2)).then_inc(xt_done, 1)

            def bias(pair):
                for b in range(2):
                    e = pair * 2 + b
                    dve.wait_ge(y_mm, e + 1)
                    dve.wait_ge(y_done, e + 1)
                    nc.vector.tensor_tensor(Z[b][:], psY[b][:, 0:TC * C].rearrange("p (t c) -> p t c", t=TC), free(b2[b][:, 0:1], [0, TC], [1, C]), ALU.add).then_inc(z_done, 1)

            copy(0, True)
            with dve.Fori(0, E // 2 - 1) as pair:
                copy(pair + 1, False)
                bias(pair)
            bias(E // 2 - 1)


class Combined:

    def __init__(self, nc, G, eps):
        self.nc, self.G, self.eps = nc, G, eps

    def __call__(self, st):
        self.Y = [[st.sb(f"Y{b}{k}", [P, C]) for k in range(2)] for b in range(4)]
        self.y_in = [st.sem(f"y_in{b}") for b in range(4)]
        self.added, = st.sems("added")
        self.norm = LnStats(st, self.G, self.eps)
        return self

    def init(self, pool):
        self.norm.init(pool)

    def gather(self, pool, i):
        for b in range(4):
            t = TI * i + b
            if i:
                pool.wait_ge(self.added, 2 * (t - 3))
            for k in range(2):
                pool.indirect_dma_start(out=self.Y[b][k][:, :], out_offset=None, in_=self.G["ys"],
                                        in_offset=bass.IndirectOffsetOnAxis(ap=self.G["slots"][k][:, t:t + 1], axis=0)).then_inc(self.y_in[b], 16)

    def stats(self, pool, i):
        for u in range(2):
            self.norm.gpsimd(self.nc, pool, i + u, u)

    def vector(self, dve, i):
        for k in range(2):
            for b in range(4):
                t = TI * i + b
                if k == 0:
                    dve.wait_ge(self.y_in[b], 16 * i + 32)
                else:
                    dve.wait_ge(self.added, 2 * TI * i + b + 1)
                X = self.G["X"][:, bass.ds(t, 1), :].rearrange("p a c -> p (a c)")
                self.nc.vector.scalar_tensor_tensor(X, self.Y[b][k][:, :], self.G["gates"][k][:, bass.ds(t, 1)], X, ALU.mult, ALU.add).then_inc(self.added, 1)
        for u in range(2):
            self.norm.vector(self.nc, dve, i + u, u, (self.added, 2 * TI * i + 8))

    def ready(self, dve, i):
        for u in range(2):
            dve.wait_ge(self.norm.kept, i + u + 3)


def result(nc, G, slots, gate, out):
    with Stage(nc, "l3c") as st:
        Y = [st.sb(f"Y{t}", [P, C]) for t in range(NT)]
        y_in = [st.sem(f"y_in{t}") for t in range(NT)]
        added, written = st.sems("added written")
        block = st.block()

        @block.sync
        def _(sp):
            for t in range(0, NT, 2):
                sp.wait_ge(added, t + 2)
                sp.dma_start(rows(out, t * P * C, [C, P], [P * C, 2], [1, C]), G["X"][:, t:t + 2, :]).then_inc(written, 16)
            sp.wait_ge(written, 16 * (NT // 2))

        @block.gpsimd
        def _(pool):
            for t in range(NT):
                pool.indirect_dma_start(out=Y[t][:, :], out_offset=None, in_=G["ys"],
                                        in_offset=bass.IndirectOffsetOnAxis(ap=slots[:, t:t + 1], axis=0)).then_inc(y_in[t], 16)

        @block.vector
        def _(dve):
            for t in range(NT):
                dve.wait_ge(y_in[t], 16)
                nc.vector.scalar_tensor_tensor(G["X"][:, t, :], Y[t][:, :], gate[:, t:t + 1], G["X"][:, t, :], ALU.mult, ALU.add).then_inc(added, 1)


def constants():
    import numpy as np

    f32 = lambda a: np.ascontiguousarray(a, dtype=np.float32)
    n = np.arange(W0)
    pos = [(k // WS, k % WS) for k in n]
    ext = [(r, c, w) for w, (_, _, h, wd, _) in enumerate(WINDOWS) if w for r in range(h) for c in range(wd)]
    pads = [(r, c) for r, c in pos if r >= HH - WS or c >= WW - WS]
    one = np.zeros((REL, W0 + EK), np.float32)
    win = np.zeros((12, W0 + EK), np.float32)
    for col, (r, c) in enumerate(pos + [e[:2] for e in ext] + pads):
        one[r, col] = one[WS + c, col] = 1
    for w in (1, 2, 3):
        for k, e in enumerate(ext):
            if e[2] != w:
                win[w - 1, W0 + k] = -1e30
        _, _, h, wd, _ = WINDOWS[w]
        for k, (r, c) in enumerate(pads):
            if r < h and c < wd:
                win[w - 1, T + k] = -1e30
    rowsq = np.zeros((12, T), np.float32)
    for k, e in enumerate(ext):
        rowsq[e[2] - 1, W0 + k] = 1
    head = np.zeros((CH, HB), np.float32)
    head[np.arange(CH), np.arange(CH) // HD] = 1
    unit = np.eye(T).reshape(T, HH, WW)
    freq = np.fft.rfft2(unit, norm="ortho").reshape(T, NF)
    dft = np.concatenate([freq.real, freq.imag], 1).reshape(TI, P, 2 * NF).transpose(1, 0, 2)
    eye = np.eye(NF).reshape(NF, HH, WF)
    inv = np.stack([np.fft.irfft2(eye * z, s=(HH, WW), norm="ortho").reshape(NF, T) for z in (1, 1j)])
    idft = np.zeros((SR, 2, 2, T))
    idft[:, 0] = inv[:, :SR].transpose(1, 0, 2)
    idft[SR - F1:, 1] = inv[:, SR:].transpose(1, 0, 2)
    bf = np.dtype("bfloat16")
    return {"ident": np.eye(P, dtype=np.float32), "reverse": f32(np.eye(KS)[::-1]), "headmask": head,
            "gnones": np.full((P, P), 1 / (T * GC), np.float32), "dft": f32(dft), "idft": f32(idft),
            "zeros": np.zeros((8 * C,), np.float32), "ones": np.ones((P, P), np.float32),
            "tri": np.triu(np.ones((P, P), np.float32)), "desc": np.tile(f32(E - np.arange(E)), (P, 1)),
            "tiles_at": np.tile(f32(np.arange(SLOT_TILES)), (P, 1)),
            "rowid": f32(B * T + np.arange(NT)[None, :] * P + np.arange(P)[:, None]), "blockones": head @ head.T,
            "eyes": f32(np.stack([k * np.eye(CH) for k in (7, 13, 15)], 1)),
            "koh": np.concatenate([one, one, one, win]).astype(bf), "winrows": rowsq.astype(bf)}


class Network:

    def __init__(self, nc, w, consts, ctx):
        self.nc, self.w, self.consts, self.ctx = nc, w, consts, ctx
        self.G = {"consts": consts, "steady": ctx.enter_context(nc.semaphore("steady"))}
        self.sb(ctx, X=(P, NT, C), MEAN=(P, NT), RSTD=(P, NT), ident=(P, P))
        self.dram(xw=(B * T, C), xr=(B * T, C), band=(NH, P * TW))
        self.dram(BF16, qd=(B, 3 * C * T), kd=(B, 3 * C * T))

    def sb(self, ctx, **shapes):
        for name, shape in shapes.items():
            self.G[name] = ctx.enter_context(self.nc.sbuf_tensor(name, list(shape), F32))

    def dram(self, dt=F32, **shapes):
        for name, shape in shapes.items():
            self.G[name] = self.nc.dram_tensor(name, list(shape), dt).ap()

    def part(self, name):
        return {k[len(name):]: v for k, v in self.w.items() if k.startswith(name)}

    def window_attention(self):
        nc, G, w = self.nc, self.G, self.part("L0_conv_")
        with ExitStack() as ctx:
            self.sb(ctx, QF=(CH, 2, B * T), Vall=(WQ, 3 * B, C), vb=(P, C), pb=(P, C), RT=(CH, 2, 2 * WS - 1), hm=(CH, HB))
            self.dram(BF16, kbd=(3, C), rd=(3 * REL * NH, B * T))
            load_x(nc, G, self.w["x"].rearrange("b h w c -> (b h w) c"), self.w["L2_attn_Wconv"], (w["rel_pos_h"], w["rel_pos_w"]), self.consts)
            attention_inputs(nc, G, "l0p", w["qkv_w"], (w["norm1_w"], w["norm1_b"], w["qkv_b"], w["proj_b"]),
                             ((0, WQ), (WQ, WQ), (W0, EXT)))
            l0_rel(nc, G)
            l0_attention(nc, G, w)

    def window_mlp(self):
        l0_mlp(self.nc, self.G, self.part("L0_conv_"))

    def fourier(self):
        l1_afno(self.nc, self.G, self.part("L1_conv_"), self.consts)

    def landmark_attention(self):
        nc, G, w = self.nc, self.G, self.part("L2_attn_")
        with ExitStack() as ctx:
            self.sb(ctx, K1T=(CH, 2, B * T), CV=(CH, 2, B * T), K3=(CH, NG, CH), K2L=(CH, NG, LM), MB=(CH, NG, CH))
            l2_features(nc, G, w, self.consts)
            l2_inverse(nc, G, self.consts)
            l2_output(nc, G, w)

    def routing(self):
        G, alloc = self.G, lambda name, n, dt: self.ctx.enter_context(self.nc.sbuf_tensor(name, [P, n], dt))
        G["gates"] = [alloc(f"gate{k}", NT, F32) for k in range(2)]
        G["slots"] = [alloc(f"slots{k}", NT, U32) for k in range(2)]
        G["tile_expert"] = alloc("tile_expert", SLOT_TILES, I32)

    def two_experts(self):
        nc, G, w = self.nc, self.G, self.part("L2_ffn_")
        slots = SLOT_TILES * P
        G["xs"], G["ys"] = (nc.dram_tensor(name, [slots, C], F32).ap() for name in ("xs2", "ys2"))
        with ExitStack() as ctx:
            self.sb(ctx, W1T=(CH, 2, E * FI), W2T=(P, E * FI // P, C))
            route(nc, G, "l2r", w["router_w"], True, 2, slots, ExpertWeights(nc, G, w["w1"], w["w2"]))
            experts_any(nc, G)

    def full_attention(self):
        with ExitStack() as ctx:
            self.G.pop("Vall", None)
            G = dict(self.G, Vall=ctx.enter_context(self.nc.sbuf_tensor("Vall3", [P, NT, C], F32)))
            attention_inputs(self.nc, G, "l3p", self.w["L3_attn_w_qkv"], None, ((0, P), (P, P)), Combined(self.nc, G, 1e-5))
            attention(self.nc, G, "l3a", self.w["L3_attn_w_proj"], None, L3_REGIONS, ((0, 0, 2, P, 0),), 2, 1e-5)

    def one_expert(self, out):
        nc, G, w = self.nc, self.G, self.part("L3_ffn_")
        G["xs"], G["ys"] = nc.dram_tensor("xs3", [2 * B * T, C], F32).ap(), nc.dram_tensor("ys3", [B * T, C], F32).ap()
        with ExitStack() as ctx:
            weights = FirstExperts(nc, ctx, w)
            route(nc, G, "l3r", w["router_w"], False, 1, B * T, weights)
            experts_each(nc, G, weights)
        result(nc, G, G["slots"][1], G["gates"][0], out)


def build(nc, w, consts, out):
    with ExitStack() as ctx:
        net = Network(nc, w, consts, ctx)
        net.window_attention()
        net.window_mlp()
        net.fourier()
        net.landmark_attention()
        net.routing()
        net.two_experts()
        net.full_attention()
        net.one_expert(out.rearrange("b h w c -> (b h w) c"))


def kernel(**inputs):
    import concourse.bacc as bacc
    import numpy as np
    from concourse.bass_utils import run_bass_kernel_spmd

    nc = bacc.Bacc("TRN2", target_bir_lowering=False, num_devices=1)
    arrays = {}

    def dram_input(name, a):
        arrays[name] = np.ascontiguousarray(a)
        return nc.dram_tensor(name, arrays[name].shape, mybir.dt.from_np(arrays[name].dtype), kind="ExternalInput").ap()

    w = {name: dram_input(f"in_{name}", a) for name, a in inputs.items()}
    consts = {name: dram_input(f"const_{name}", a) for name, a in constants().items()}
    out = nc.dram_tensor("out", [B, HH, WW, C], F32, kind="ExternalOutput").ap()
    build(nc, w, consts, out)
    return run_bass_kernel_spmd(nc, [arrays], core_ids=[0]).results[0]["out"]
```
